# Optimizing a Trainium2 kernel written in Bass

```python
import numpy as np
import jax
import jax.numpy as jnp

def _softmax(x, axis=-1):
    return jax.nn.softmax(x, axis=axis)

def _gelu(x):
    return jax.nn.gelu(x, approximate=True)

def _silu(x):
    return jax.nn.silu(x)

def _sigmoid(x):
    return jax.nn.sigmoid(x)

def _layernorm(x, axis=-1, eps=1e-05):
    m = jnp.mean(x, axis=axis, keepdims=True)
    v = jnp.var(x, axis=axis, keepdims=True)
    return (x - m) / jnp.sqrt(v + eps)

def _scatter_add(tgt, idx, src, axis=0):
    return tgt.at[idx].add(src)

def _segment_sum(src, seg, n):
    return jax.ops.segment_sum(src, seg, n)
kernel_name = 'mk_decoder_postln_d2_seqx_r4_2741c6'

def setup_inputs(seed: int=0):
    np.random.seed(seed)
    _w = jnp.asarray

    def _rec_inputs():
        import jax
        import jax.numpy as jnp
        _rk = jax.random.key(seed)
        x = -0.0002928 + 1 * jax.random.normal(jax.random.fold_in(_rk, 1), (2, 1024, 256), jnp.float32)
        _lenS = 1024 - jax.random.randint(jax.random.fold_in(_rk, 7), (2,), 0, max(1, 1024 // 4) + 1, jnp.int32)
        _lenS2 = 77 - jax.random.randint(jax.random.fold_in(_rk, 8), (2,), 0, max(1, 77 // 4) + 1, jnp.int32)
        _ctx_1024P = jax.random.normal(jax.random.fold_in(_rk, 11), (2, 16, 256), jnp.float32)
        _ctx_1024c = jax.random.dirichlet(jax.random.fold_in(_rk, 511), 0.3 * jnp.ones((16,), jnp.float32), (2, 77))
        _ctx_1024t = jnp.einsum('bsk,bkd->bsd', _ctx_1024c, _ctx_1024P)
        _ctx_1024t = _ctx_1024t * jax.lax.rsqrt(jnp.mean(jnp.square(_ctx_1024t)) + 1e-12) * 0.953939
        ctx_1024 = -1.39393e-06 + 0.999914 * (_ctx_1024t + 0.3 * jax.random.normal(jax.random.fold_in(_rk, 611), (2, 77, 256), jnp.float32))
        return (x, ctx_1024)
    x, ctx_1024 = _rec_inputs()

    def _L0_attn_setup():
        import jax, jax.numpy as jnp
        import numpy as np
        DIM = 256
        HEADS = 16
        HIDDEN = 1024
        B, N = (4, 512)

        def _mlp(x, w1, b1, w2, b2):
            h = jax.nn.gelu(x @ w1 + b1, approximate=False)
            return h @ w2 + b2
        key = jax.random.key(seed)
        ks = jax.random.split(key, 15)
        s_in = 1.0 / np.sqrt(DIM)
        s_hid = 1.0 / np.sqrt(HIDDEN)
        inp = {'x': jax.random.normal(ks[0], (B, N, DIM), dtype=jnp.float32)}
        i = 1
        for name in ('q', 'k', 'v'):
            inp[f'{name}_w1'] = jax.random.normal(ks[i], (DIM, HIDDEN), jnp.float32) * s_in
            i += 1
            inp[f'{name}_b1'] = jax.random.normal(ks[i], (HIDDEN,), jnp.float32) * s_in
            i += 1
            inp[f'{name}_w2'] = jax.random.normal(ks[i], (HIDDEN, DIM), jnp.float32) * s_hid
            i += 1
            inp[f'{name}_b2'] = jax.random.normal(ks[i], (DIM,), jnp.float32) * s_hid
            i += 1
        inp['proj_w'] = jax.random.normal(ks[13], (DIM, DIM), jnp.float32) * s_in
        inp['proj_b'] = jax.random.normal(ks[14], (DIM,), jnp.float32) * s_in
        return inp
    _L0_attn_all = _L0_attn_setup()
    _L0_attn_in = {k: v for k, v in _L0_attn_all.items() if k in ('q_w1', 'q_b1', 'q_w2', 'q_b2', 'k_w1', 'k_b1', 'k_w2', 'k_b2', 'v_w1', 'v_b1', 'v_w2', 'v_b2', 'proj_w', 'proj_b')}
    del _L0_attn_all

    def _L0_xattn_setup():
        import jax, jax.numpy as jnp
        import numpy as np
        D_MODEL = 256
        N_HEADS = 16
        N_KV_HEADS = 4
        HEAD_DIM = 64
        key = jax.random.key(seed)
        ks = jax.random.split(key, 6)
        B, Tq, Tkv = (2, 512, 512)
        query = jax.random.normal(ks[0], (B, Tq, D_MODEL), dtype=jnp.float32)
        context = jax.random.normal(ks[1], (B, Tkv, D_MODEL), dtype=jnp.float32)
        s = 1.0 / np.sqrt(D_MODEL)
        Wq = jax.random.normal(ks[2], (N_HEADS * HEAD_DIM, D_MODEL), dtype=jnp.float32) * s
        Wk = jax.random.normal(ks[3], (N_KV_HEADS * HEAD_DIM, D_MODEL), dtype=jnp.float32) * s
        Wv = jax.random.normal(ks[4], (N_KV_HEADS * HEAD_DIM, D_MODEL), dtype=jnp.float32) * s
        Wo = jax.random.normal(ks[5], (D_MODEL, N_HEADS * HEAD_DIM), dtype=jnp.float32) * s
        return {'query': query, 'context': context, 'Wq': Wq, 'Wk': Wk, 'Wv': Wv, 'Wo': Wo}
    _L0_xattn_all = _L0_xattn_setup()
    _L0_xattn_in = {k: v for k, v in _L0_xattn_all.items() if k in ('Wq', 'Wk', 'Wv', 'Wo')}
    del _L0_xattn_all

    def _L0_ffn_setup():
        import jax, jax.numpy as jnp
        import numpy as np
        B, S, D = (1, 512, 256)
        E, K, F = (8, 2, 352)
        NS = 2
        SCALE = 2.5

        def _swiglu_mlp(x, wg, wu, wd):
            return jax.nn.silu(x @ wg) * (x @ wu) @ wd
        key = jax.random.key(seed)
        ks = jax.random.split(key, 8)
        s = 0.02
        return {'hidden_states': jax.random.normal(ks[0], (B, S, D), jnp.float32), 'gate_w': jax.random.normal(ks[1], (E, D), jnp.float32) * s, 'w_gate': jax.random.normal(ks[2], (E, D, F), jnp.float32) * s, 'w_up': jax.random.normal(ks[3], (E, D, F), jnp.float32) * s, 'w_down': jax.random.normal(ks[4], (E, F, D), jnp.float32) * s, 'sw_gate': jax.random.normal(ks[5], (D, F * NS), jnp.float32) * s, 'sw_up': jax.random.normal(ks[6], (D, F * NS), jnp.float32) * s, 'sw_down': jax.random.normal(ks[7], (F * NS, D), jnp.float32) * s}
    _L0_ffn_all = _L0_ffn_setup()
    _L0_ffn_in = {k: v for k, v in _L0_ffn_all.items() if k in ('gate_w', 'w_gate', 'w_up', 'w_down', 'sw_gate', 'sw_up', 'sw_down')}
    del _L0_ffn_all

    def _L1_attn_setup():
        import jax, jax.numpy as jnp
        import numpy as np
        SLEN, BSZ, IN_DIM = (512, 8, 256)
        H, D = (16, 64)
        LN_EPS = 1e-05

        def elu_p1(x):
            return jax.nn.elu(x) + 1.0

        def sum_norm(x):
            return x / jnp.sum(x, axis=-1, keepdims=True)

        def _forward(x, ln_w, ln_b, w_slow, w_out):
            slen, bsz, in_dim = x.shape
            mu = jnp.mean(x, axis=-1, keepdims=True)
            var = jnp.mean(jnp.square(x - mu), axis=-1, keepdims=True)
            h = (x - mu) * jax.lax.rsqrt(var + LN_EPS) * ln_w + ln_b
            qkvb = (h @ w_slow).reshape(slen, bsz, H, 3 * D + 1)
            q, k, v, beta = jnp.split(qkvb, [D, 2 * D, 3 * D], axis=-1)
            beta = jax.nn.sigmoid(beta)
            q = sum_norm(elu_p1(q))
            k = sum_norm(elu_p1(k))
            W0 = jnp.zeros((bsz, H, D, D), x.dtype)

            def step(W, qkvb_t):
                q_t, k_t, v_t, b_t = qkvb_t
                v_old = jnp.einsum('bhij,bhj->bhi', W, k_t)
                delta = b_t * (v_t - v_old)
                W_new = W + delta[..., :, None] * k_t[..., None, :]
                out_t = jnp.einsum('bhij,bhj->bhi', W_new, q_t)
                return (W_new, out_t)
            _, out = jax.lax.scan(step, W0, (q, k, v, beta))
            out = out.reshape(slen, bsz, H * D) @ w_out
            return x + out
        key = jax.random.key(seed)
        k1, k2, k3, k4, k5 = jax.random.split(key, 5)
        x = jax.random.normal(k1, (SLEN, BSZ, IN_DIM), dtype=jnp.float32)
        ln_w = jnp.ones((IN_DIM,), jnp.float32) + 0.02 * jax.random.normal(k2, (IN_DIM,), jnp.float32)
        ln_b = 0.02 * jax.random.normal(k3, (IN_DIM,), jnp.float32)
        w_slow = jax.random.normal(k4, (IN_DIM, H * (3 * D + 1)), jnp.float32) / np.sqrt(IN_DIM)
        w_out = jax.random.normal(k5, (H * D, IN_DIM), jnp.float32) / np.sqrt(H * D)
        return {'x': x, 'ln_w': ln_w, 'ln_b': ln_b, 'w_slow': w_slow, 'w_out': w_out}
    _L1_attn_all = _L1_attn_setup()
    _L1_attn_in = {k: v for k, v in _L1_attn_all.items() if k in ('ln_w', 'ln_b', 'w_slow', 'w_out')}
    del _L1_attn_all

    def _L1_xattn_setup():
        import jax, jax.numpy as jnp
        import numpy as np
        import math
        NUM_HEAD = 16
        D_MODEL = 256
        BATCH = 2
        SEQ = 512

        def _split_heads(x):
            B, S, D = x.shape
            return x.reshape(B, S, NUM_HEAD, D // NUM_HEAD).transpose(0, 2, 1, 3)
        key = jax.random.key(seed)
        k1, k2, k3, k4 = jax.random.split(key, 4)
        scale = 1.0 / math.sqrt(D_MODEL)
        return {'query': jax.random.normal(k1, (BATCH, SEQ, D_MODEL), dtype=jnp.float32), 'key': jax.random.normal(k2, (BATCH, SEQ, D_MODEL), dtype=jnp.float32), 'value': jax.random.normal(k3, (BATCH, SEQ, D_MODEL), dtype=jnp.float32), 'w_concat': jax.random.normal(k4, (D_MODEL, D_MODEL), dtype=jnp.float32) * scale}
    _L1_xattn_all = _L1_xattn_setup()
    _L1_xattn_in = {k: v for k, v in _L1_xattn_all.items() if k in ('w_concat',)}
    del _L1_xattn_all

    def _L1_ffn_setup():
        import jax, jax.numpy as jnp
        import numpy as np
        D_IN, D_HID = (256, 1024)

        def _ternary(key, shape):
            return jax.random.randint(key, shape, -1, 2).astype(jnp.float32)

        def _tlin(x, w, s):
            return jnp.einsum('bsi,oi->bso', x, w) * s
        key = jax.random.key(seed)
        ks = jax.random.split(key, 12)
        inv = lambda fan: 1.0 / np.sqrt(fan).astype(np.float32)
        return {'x': jax.random.normal(ks[0], (4, 512, D_IN), dtype=jnp.float32), 'w1_w': _ternary(ks[1], (D_HID, D_IN)), 'w1_s': jax.random.uniform(ks[2], (D_HID,), dtype=jnp.float32) * inv(D_IN), 'w2_w': _ternary(ks[3], (D_HID, D_IN)), 'w2_s': jax.random.uniform(ks[4], (D_HID,), dtype=jnp.float32) * inv(D_IN), 'h1_w': _ternary(ks[5], (D_HID, D_HID)), 'h1_s': jax.random.uniform(ks[6], (D_HID,), dtype=jnp.float32) * inv(D_HID), 'h2_w': _ternary(ks[7], (D_HID, D_HID)), 'h2_s': jax.random.uniform(ks[8], (D_HID,), dtype=jnp.float32) * inv(D_HID), 'w3_w': _ternary(ks[9], (D_IN, D_HID)), 'w3_s': jax.random.uniform(ks[10], (D_IN,), dtype=jnp.float32) * inv(D_HID)}
    _L1_ffn_all = _L1_ffn_setup()
    _L1_ffn_in = {k: v for k, v in _L1_ffn_all.items() if k in ('w1_w', 'w1_s', 'w2_w', 'w2_s', 'h1_w', 'h1_s', 'h2_w', 'h2_s', 'w3_w', 'w3_s')}
    del _L1_ffn_all
    return {'x': x, 'ctx_1024': ctx_1024, 'L0_attn_q_w1': _L0_attn_in['q_w1'], 'L0_attn_q_b1': _L0_attn_in['q_b1'], 'L0_attn_q_w2': _L0_attn_in['q_w2'], 'L0_attn_q_b2': _L0_attn_in['q_b2'], 'L0_attn_k_w1': _L0_attn_in['k_w1'], 'L0_attn_k_b1': _L0_attn_in['k_b1'], 'L0_attn_k_w2': _L0_attn_in['k_w2'], 'L0_attn_k_b2': _L0_attn_in['k_b2'], 'L0_attn_v_w1': _L0_attn_in['v_w1'], 'L0_attn_v_b1': _L0_attn_in['v_b1'], 'L0_attn_v_w2': _L0_attn_in['v_w2'], 'L0_attn_v_b2': _L0_attn_in['v_b2'], 'L0_attn_proj_w': _L0_attn_in['proj_w'], 'L0_attn_proj_b': _L0_attn_in['proj_b'], 'L0_xattn_Wq': _L0_xattn_in['Wq'], 'L0_xattn_Wk': _L0_xattn_in['Wk'], 'L0_xattn_Wv': _L0_xattn_in['Wv'], 'L0_xattn_Wo': _L0_xattn_in['Wo'], 'L0_ffn_gate_w': _L0_ffn_in['gate_w'], 'L0_ffn_w_gate': _L0_ffn_in['w_gate'], 'L0_ffn_w_up': _L0_ffn_in['w_up'], 'L0_ffn_w_down': _L0_ffn_in['w_down'], 'L0_ffn_sw_gate': _L0_ffn_in['sw_gate'], 'L0_ffn_sw_up': _L0_ffn_in['sw_up'], 'L0_ffn_sw_down': _L0_ffn_in['sw_down'], 'L1_attn_ln_w': _L1_attn_in['ln_w'], 'L1_attn_ln_b': _L1_attn_in['ln_b'], 'L1_attn_w_slow': _L1_attn_in['w_slow'], 'L1_attn_w_out': _L1_attn_in['w_out'], 'L1_xattn_w_concat': _L1_xattn_in['w_concat'], 'L1_ffn_w1_w': _L1_ffn_in['w1_w'], 'L1_ffn_w1_s': _L1_ffn_in['w1_s'], 'L1_ffn_w2_w': _L1_ffn_in['w2_w'], 'L1_ffn_w2_s': _L1_ffn_in['w2_s'], 'L1_ffn_h1_w': _L1_ffn_in['h1_w'], 'L1_ffn_h1_s': _L1_ffn_in['h1_s'], 'L1_ffn_h2_w': _L1_ffn_in['h2_w'], 'L1_ffn_h2_s': _L1_ffn_in['h2_s'], 'L1_ffn_w3_w': _L1_ffn_in['w3_w'], 'L1_ffn_w3_s': _L1_ffn_in['w3_s']}

def reference(x, ctx_1024, L0_attn_q_w1, L0_attn_q_b1, L0_attn_q_w2, L0_attn_q_b2, L0_attn_k_w1, L0_attn_k_b1, L0_attn_k_w2, L0_attn_k_b2, L0_attn_v_w1, L0_attn_v_b1, L0_attn_v_w2, L0_attn_v_b2, L0_attn_proj_w, L0_attn_proj_b, L0_xattn_Wq, L0_xattn_Wk, L0_xattn_Wv, L0_xattn_Wo, L0_ffn_gate_w, L0_ffn_w_gate, L0_ffn_w_up, L0_ffn_w_down, L0_ffn_sw_gate, L0_ffn_sw_up, L0_ffn_sw_down, L1_attn_ln_w, L1_attn_ln_b, L1_attn_w_slow, L1_attn_w_out, L1_xattn_w_concat, L1_ffn_w1_w, L1_ffn_w1_s, L1_ffn_w2_w, L1_ffn_w2_s, L1_ffn_h1_w, L1_ffn_h1_s, L1_ffn_h2_w, L1_ffn_h2_s, L1_ffn_w3_w, L1_ffn_w3_s):
    import jax
    import jax.numpy as jnp

    def _L0_attn_ref(x, q_w1, q_b1, q_w2, q_b2, k_w1, k_b1, k_w2, k_b2, v_w1, v_b1, v_w2, v_b2, proj_w, proj_b):
        import jax, jax.numpy as jnp
        import numpy as np
        DIM = 256
        HEADS = 16
        HIDDEN = 1024
        B, N = (4, 512)

        def _mlp(x, w1, b1, w2, b2):
            h = jax.nn.gelu(x @ w1 + b1, approximate=False)
            return h @ w2 + b2
        Bx, Nx, C = x.shape
        hd = C // HEADS
        scale = hd ** (-0.5)

        def split_heads(t):
            return t.reshape(Bx, Nx, HEADS, hd).transpose(0, 2, 1, 3)
        q = split_heads(_mlp(x, q_w1, q_b1, q_w2, q_b2))
        k = split_heads(_mlp(x, k_w1, k_b1, k_w2, k_b2))
        v = split_heads(_mlp(x, v_w1, v_b1, v_w2, v_b2))
        attn = jnp.einsum('bhqd,bhkd->bhqk', q, k) * scale
        attn = jax.nn.softmax(attn, axis=-1)
        out = jnp.einsum('bhqk,bhkd->bhqd', attn, v)
        out = out.transpose(0, 2, 1, 3).reshape(Bx, Nx, C)
        return out @ proj_w + proj_b

    def _L0_xattn_ref(query, context, Wq, Wk, Wv, Wo):
        import jax, jax.numpy as jnp
        import numpy as np
        D_MODEL = 256
        N_HEADS = 16
        N_KV_HEADS = 4
        HEAD_DIM = 64
        B, Tq, _ = query.shape
        Tkv = context.shape[1]
        q = (query @ Wq.T).reshape(B, Tq, N_HEADS, HEAD_DIM).transpose(0, 2, 1, 3)
        k = (context @ Wk.T).reshape(B, Tkv, N_KV_HEADS, HEAD_DIM).transpose(0, 2, 1, 3)
        v = (context @ Wv.T).reshape(B, Tkv, N_KV_HEADS, HEAD_DIM).transpose(0, 2, 1, 3)
        groups = N_HEADS // N_KV_HEADS
        k = jnp.repeat(k, groups, axis=1)
        v = jnp.repeat(v, groups, axis=1)
        scale = jnp.sqrt(jnp.float32(HEAD_DIM))
        scores = jnp.einsum('bhqd,bhkd->bhqk', q, k) / scale
        attn = jax.nn.softmax(scores, axis=-1)
        out = jnp.einsum('bhqk,bhkd->bhqd', attn, v)
        out = out.transpose(0, 2, 1, 3).reshape(B, Tq, N_HEADS * HEAD_DIM)
        return out @ Wo.T

    def _L0_ffn_ref(hidden_states, gate_w, w_gate, w_up, w_down, sw_gate, sw_up, sw_down):
        import jax, jax.numpy as jnp
        import numpy as np
        B, S, D = (1, 512, 256)
        E, K, F = (8, 2, 352)
        NS = 2
        SCALE = 2.5

        def _swiglu_mlp(x, wg, wu, wd):
            return jax.nn.silu(x @ wg) * (x @ wu) @ wd
        identity = hidden_states
        x = hidden_states.reshape(-1, hidden_states.shape[-1])
        T = x.shape[0]
        logits = x.astype(jnp.float32) @ gate_w.astype(jnp.float32).T
        scores = jax.nn.softmax(logits, axis=-1)
        topk_w, topk_i = jax.lax.top_k(scores, K)
        topk_w = topk_w / (topk_w.sum(-1, keepdims=True) + 1e-20) * SCALE
        combine = jnp.zeros((T, E), jnp.float32).at[jnp.arange(T)[:, None], topk_i].set(topk_w)
        g = jax.nn.silu(jnp.einsum('td,edf->etf', x, w_gate)) * jnp.einsum('td,edf->etf', x, w_up)
        expert_out = jnp.einsum('etf,efd->etd', g, w_down)
        y = jnp.einsum('te,etd->td', combine, expert_out).astype(x.dtype)
        y = y.reshape(identity.shape)
        return y + _swiglu_mlp(identity, sw_gate, sw_up, sw_down)

    def _L1_attn_ref(x, ln_w, ln_b, w_slow, w_out):
        import jax, jax.numpy as jnp
        import numpy as np
        SLEN, BSZ, IN_DIM = (512, 8, 256)
        H, D = (16, 64)
        LN_EPS = 1e-05

        def elu_p1(x):
            return jax.nn.elu(x) + 1.0

        def sum_norm(x):
            return x / jnp.sum(x, axis=-1, keepdims=True)

        def _forward(x, ln_w, ln_b, w_slow, w_out):
            slen, bsz, in_dim = x.shape
            mu = jnp.mean(x, axis=-1, keepdims=True)
            var = jnp.mean(jnp.square(x - mu), axis=-1, keepdims=True)
            h = (x - mu) * jax.lax.rsqrt(var + LN_EPS) * ln_w + ln_b
            qkvb = (h @ w_slow).reshape(slen, bsz, H, 3 * D + 1)
            q, k, v, beta = jnp.split(qkvb, [D, 2 * D, 3 * D], axis=-1)
            beta = jax.nn.sigmoid(beta)
            q = sum_norm(elu_p1(q))
            k = sum_norm(elu_p1(k))
            W0 = jnp.zeros((bsz, H, D, D), x.dtype)

            def step(W, qkvb_t):
                q_t, k_t, v_t, b_t = qkvb_t
                v_old = jnp.einsum('bhij,bhj->bhi', W, k_t)
                delta = b_t * (v_t - v_old)
                W_new = W + delta[..., :, None] * k_t[..., None, :]
                out_t = jnp.einsum('bhij,bhj->bhi', W_new, q_t)
                return (W_new, out_t)
            _, out = jax.lax.scan(step, W0, (q, k, v, beta))
            out = out.reshape(slen, bsz, H * D) @ w_out
            return x + out
        return _forward(x, ln_w, ln_b, w_slow, w_out)

    def _L1_xattn_ref(query, key, value, w_concat):
        import jax, jax.numpy as jnp
        import numpy as np
        import math
        NUM_HEAD = 16
        D_MODEL = 256
        BATCH = 2
        SEQ = 512

        def _split_heads(x):
            B, S, D = x.shape
            return x.reshape(B, S, NUM_HEAD, D // NUM_HEAD).transpose(0, 2, 1, 3)
        q = _split_heads(query)
        k = _split_heads(key)
        v = _split_heads(value)
        d_k = q.shape[-1]
        scores = jnp.einsum('bhqd,bhkd->bhqk', q, k) / math.sqrt(d_k)
        attn = jax.nn.softmax(scores, axis=-1)
        ctx = jnp.einsum('bhqk,bhkd->bhqd', attn, v)
        B, H, S, dk = ctx.shape
        x = ctx.transpose(0, 2, 1, 3).reshape(B, S, H * dk)
        return x @ w_concat.T

    def _L1_ffn_ref(x, w1_w, w1_s, w2_w, w2_s, h1_w, h1_s, h2_w, h2_s, w3_w, w3_s):
        import jax, jax.numpy as jnp
        import numpy as np
        D_IN, D_HID = (256, 1024)

        def _ternary(key, shape):
            return jax.random.randint(key, shape, -1, 2).astype(jnp.float32)

        def _tlin(x, w, s):
            return jnp.einsum('bsi,oi->bso', x, w) * s
        h = jax.nn.silu(_tlin(x, w1_w, w1_s)) * _tlin(x, w2_w, w2_s)
        h = jax.nn.gelu(_tlin(h, h1_w, h1_s), approximate=False)
        h = jax.nn.gelu(_tlin(h, h2_w, h2_s), approximate=False)
        return _tlin(h, w3_w, w3_s)
    x = _layernorm(x + _L0_attn_ref(x, L0_attn_q_w1, L0_attn_q_b1, L0_attn_q_w2, L0_attn_q_b2, L0_attn_k_w1, L0_attn_k_b1, L0_attn_k_w2, L0_attn_k_b2, L0_attn_v_w1, L0_attn_v_b1, L0_attn_v_w2, L0_attn_v_b2, L0_attn_proj_w, L0_attn_proj_b), axis=-1)
    x = _layernorm(x + _L0_xattn_ref(x, ctx_1024, L0_xattn_Wq, L0_xattn_Wk, L0_xattn_Wv, L0_xattn_Wo), axis=-1)
    x = _layernorm(x + _L0_ffn_ref(x, L0_ffn_gate_w, L0_ffn_w_gate, L0_ffn_w_up, L0_ffn_w_down, L0_ffn_sw_gate, L0_ffn_sw_up, L0_ffn_sw_down), axis=-1)
    x = _layernorm(x + _L1_attn_ref(x, L1_attn_ln_w, L1_attn_ln_b, L1_attn_w_slow, L1_attn_w_out), axis=-1)
    x = _layernorm(x + _L1_xattn_ref(x, ctx_1024, ctx_1024, L1_xattn_w_concat), axis=-1)
    x = _layernorm(x + _L1_ffn_ref(x, L1_ffn_w1_w, L1_ffn_w1_s, L1_ffn_w2_w, L1_ffn_w2_s, L1_ffn_h1_w, L1_ffn_h1_s, L1_ffn_h2_w, L1_ffn_h2_s, L1_ffn_w3_w, L1_ffn_w3_s), axis=-1)
    return x

_drawn_inputs = setup_inputs


def setup_inputs(seed=0):
    import zlib

    import numpy as np

    out = dict(_drawn_inputs(seed))
    spreads = {}
    factors = {'L0_attn_q_w1': 7.573,
     'L0_attn_q_b1': 8.0,
     'L0_attn_q_w2': 6.912,
     'L0_attn_q_b2': 8.0,
     'L0_attn_k_w1': 6.671,
     'L0_attn_k_b1': 8.0,
     'L0_attn_k_w2': 6.915,
     'L0_attn_k_b2': 8.0,
     'L0_attn_v_w1': 2.92,
     'L0_attn_v_b1': 3.254,
     'L0_attn_v_b2': 2.731,
     'L1_attn_ln_w': 8.0,
     'L1_attn_ln_b': 8.0,
     'L1_attn_w_slow': 8.0,
     'L1_attn_w_out': 8.0,
     'L1_ffn_w1_w': 8.0,
     'L1_ffn_w1_s': 8.0,
     'L1_ffn_w2_w': 8.0,
     'L1_ffn_w2_s': 8.0,
     'L1_ffn_h1_w': 8.0,
     'L1_ffn_h1_s': 8.0,
     'L1_ffn_h2_w': 8.0,
     'L1_ffn_h2_s': 8.0,
     'L1_ffn_w3_w': 8.0,
     'L1_ffn_w3_s': 8.0}
    for name, (base, spread) in spreads.items():
        noise = np.random.default_rng([zlib.crc32(name.encode()), seed]).standard_normal(out[name].shape)
        drawn = base * np.exp(spread * noise) if base else spread * noise
        out[name] = jnp.asarray(drawn.astype(out[name].dtype))
    for name, factor in factors.items():
        out[name] = (out[name] * factor).astype(out[name].dtype)
    return out
```

```python
from contextlib import ExitStack

import concourse.bass as bass
from concourse import mybir

F32 = mybir.dt.float32
F32R = mybir.dt.float32r
ALU = mybir.AluOpType
ACT = mybir.ActivationFunctionType
AX = mybir.AxisListType
P = 128
B, N, D = 2, 1024, 256
T = B * N
NT = T // P
KD = D // P
G = 4
GT = NT // G
GW = T // G
NH = 16
HD = D // NH
HID = 1024
KH = HID // P
S = 77
FL = NH * S
FB = -(-FL // P)
E, F = 8, 352
NE = E + 2
EPS = 1e-5
ds = bass.ds


class Ctx:

    def __init__(self, nc, stack):
        self.nc, self.stack = nc, stack

    def sb(self, name, shape, dt=F32):
        return self.stack.enter_context(self.nc.sbuf_tensor(name, shape, dt))

    def ps(self, name, shape, dt=F32):
        return self.stack.enter_context(self.nc.psum_tensor(name, shape, dt))

    def sems(self, *names):
        return [self.stack.enter_context(self.nc.semaphore(n)) for n in names]


def ring(per_loop, i, j, depth):
    return per_loop * i + max(0, j - depth + 1)


def self_attention_qkv(nc, glob, w, scr):
    with ExitStack() as stack:
        c = Ctx(nc, stack)
        xT = c.sb("qkv_xT", [P, KD, T])
        w1 = c.sb("qkv_w1", [P, 3, KD, HID])
        w2 = c.sb("qkv_w2", [P, 3, KH, D])
        b1 = c.sb("qkv_b1", [P, 3, KH])
        b2 = c.sb("qkv_b2", [P, 2, KD])
        b2v = c.sb("qkv_b2v", [P, D])
        hid = c.sb("qkv_hid", [P, 3, KH, GW])
        full = c.sb("qkv_full", [P, GW])
        parts = c.sb("qkv_parts", [P, 2, 2, GW], F32R)
        hb = c.ps("qkv_hb", [P, 4, 512])
        ob = c.ps("qkv_ob", [P, 2, 512])
        loaded, h_ready, h_done, o_ready, o_done, parts_ready, st0, st1 = c.sems(
            "a_loaded", "a_h_ready", "a_h_done", "a_o_ready", "a_o_done", "a_parts_ready", "a_st0", "a_st1")
        stored = [st0, st1]
        V = glob["V"]
        NLOAD = 16 * 12
        with nc.Block() as block:
            @block.sync
            def _(sp):
                sp.dma_start(xT[:], w["xT"].rearrange("(k p) t -> p k t", p=P)).then_inc(loaded, 16)
                for br in range(3):
                    sp.dma_start(w1[:, br], w["w1"][br].rearrange("(k p) n -> p k n", p=P)).then_inc(loaded, 16)
                    sp.dma_start(w2[:, br], w["w2"][br].rearrange("(k p) n -> p k n", p=P)).then_inc(loaded, 16)
                    sp.dma_start(b1[:, br], w["b1"][br]).then_inc(loaded, 16)
                sp.dma_start(b2[:], w["b2qk"]).then_inc(loaded, 16)
                sp.dma_start(b2v[:], w["b2v"].to_broadcast([P, D])).then_inc(loaded, 16)
                sp.dma_start(glob["X"][:], w["x"].rearrange("(t p) d -> p t d", p=P)).then_inc(glob["x_loaded"], 16)
                with sp.Fori(0, B) as b:
                    for half in range(2):
                        for j in range(4):
                            br, mt = j // 2, j % 2
                            sp.wait_ge(parts_ready, 8 * b + 4 * half + j + 1)
                            sp.dma_start(
                                scr["qk"][br, :, ds(b * D + mt * P, P), half * 512:half * 512 + 512]
                                .rearrange("l r n -> r l n"), parts[:, j % 2].bitcast(F32)).then_inc(stored[j % 2], 16)
                for q in stored:
                    sp.wait_ge(q, 16 * 2 * G)
                sp.wait_ge(glob["x_loaded"], 16)

            @block.tensor
            def _(pe):
                pe.wait_ge(loaded, NLOAD)
                with pe.Fori(0, G) as t:
                    def up(br):
                        for m in range(KH):
                            j = br * KH + m
                            pe.wait_ge(h_done, ring(3 * KH, t, j, 4))
                            for k in range(KD):
                                mm = pe.matmul(hb[:, j % 4], w1[:, br, k, m * P:m * P + P],
                                               xT[:, k, ds(t * GW, GW)], start=k == 0, stop=k == KD - 1)
                            mm.then_inc(h_ready, 1)

                    def down(br):
                        pe.wait_ge(h_done, 3 * KH * t + (br + 1) * KH)
                        for u in range(2 if br < 2 else GT):
                            j = 2 * br + u
                            pe.wait_ge(o_done, ring(8, t, j, 2))
                            for k in range(KH):
                                if br < 2:
                                    mm = pe.matmul(ob[:, j % 2], w2[:, br, k, u * P:u * P + P],
                                                   hid[:, br, k], start=k == 0, stop=k == KH - 1)
                                else:
                                    mm = pe.matmul(ob[:, j % 2, 0:D], hid[:, br, k, u * P:u * P + P],
                                                   w2[:, br, k], start=k == 0, stop=k == KH - 1)
                            mm.then_inc(o_ready, 1)

                    up(0)
                    up(1)
                    down(0)
                    up(2)
                    down(1)
                    down(2)

            @block.scalar
            def _(act):
                act.wait_ge(loaded, NLOAD)
                with act.Fori(0, G) as t:
                    for j in range(3 * KH):
                        br, m = j // KH, j % KH
                        act.wait_ge(h_ready, 3 * KH * t + j + 1)
                        act.activation(hid[:, br, m], hb[:, j % 4], ACT.Gelu,
                                       bias=b1[:, br, m:m + 1]).then_inc(h_done, 1)

            @block.vector
            def _(dve):
                dve.memset(V[:, :, :, HD:HD + 1], 1.0)
                dve.wait_ge(loaded, NLOAD)
                with dve.Fori(0, G) as t:
                    for j in range(8):
                        if j < 4:
                            br, mt = j // 2, j % 2
                            dve.drain()
                            dve.wait_ge(o_ready, 8 * t + j + 1)
                            dve.tensor_scalar(full[:], ob[:, j % 2], b2[:, br, mt:mt + 1], None,
                                              ALU.add).then_inc(o_done, 1)
                            dve.drain()
                            dve.wait_ge(stored[j % 2], 16 * (2 * t + j // 2))
                            dve.tensor_copy(parts[:, j % 2, 0], full[:])
                            dve.drain()
                            dve.tensor_tensor(parts[:, j % 2, 1], full[:], parts[:, j % 2, 0].bitcast(F32),
                                              ALU.subtract).then_inc(parts_ready, 1)
                        else:
                            dve.wait_ge(o_ready, 8 * t + j + 1)
                            v = V[:, ds(t * GT + j - 4, 1), :, 0:HD].rearrange("p a h d -> p (a h) d")
                            dve.tensor_tensor(v, ob[:, j % 2, 0:D].rearrange("p (h d) -> p h d", h=NH),
                                              b2v[:].rearrange("p (h d) -> p h d", h=NH),
                                              ALU.add).then_inc(o_done, 1)

            @block.gpsimd
            def _(pool):
                pool.memset(glob["ident"][:], 0.0)
                pool.drain()
                pool.affine_select(out=glob["ident"][:], in_=glob["ident"][:], compare_op=ALU.not_equal,
                                   fill=1.0, base=0, pattern=[[-1, P]], channel_multiplier=1)
                pool.memset(glob["mhalf"][:], -0.5)
                pool.memset(glob["eps"][:], EPS)


def self_attention_heads(nc, glob, scr):
    NQ = N // P
    KR = 4 * HD + 2
    NLD = 16 * 9
    with ExitStack() as stack:
        c = Ctx(nc, stack)
        qs = c.sb("at_qs", [KR, 2, N], F32R)
        ks = c.sb("at_ks", [KR, 2, N], F32R)
        zero = c.sb("at_zero", [2, N], F32R)
        vs = c.sb("at_vs", [P, 2, NQ, HD + 1])
        probs = c.sb("at_probs", [P, 2, NQ, 512])
        mx = c.sb("at_mx", [P, NQ, 2])
        nm = c.sb("at_nm", [P, NQ])
        nmT = c.sb("at_nmT", [NQ, P])
        nmp = c.sb("at_nmp", [NQ, 2, P], F32R)
        outT = c.sb("at_outT", [P, 512])
        rc = c.sb("at_rc", [P, 4])
        s1 = c.ps("at_s1", [P, 2, 512])
        s2 = c.ps("at_s2", [P, 2, 512])
        pv = c.ps("at_pv", [P, 2, 512])
        tm = c.ps("at_tm", [P, 512])
        to = c.ps("at_to", [P, 512])
        (ld0, ld1, mrow0, mrow1, s1_ready, s1_done, s2_ready, p_ready, v_ready, pv_ready, out_ready, to_ready,
         to_done, nm_ready, tm_ready, nmp_ready, const_ready) = c.sems(
            "b_ld0", "b_ld1", "b_mrow0", "b_mrow1", "b_s1_ready", "b_s1_done", "b_s2_ready", "b_p_ready",
            "b_v_ready", "b_pv_ready", "b_out_ready", "b_to_ready", "b_to_done", "b_nm_ready", "b_tm_ready",
            "b_nmp_ready", "b_const_ready")
        ld, mrow = [ld0, ld1], [mrow0, mrow1]
        V, ATT, ident = glob["V"], glob["ATT"], glob["ident"]
        NB = B * NH

        def heads(eng, one):
            one(0, 0, True, False)
            one(1, 1, True, True)
            with eng.Fori(1, NB // 2 - 1) as i:
                one(2 * i, 0, True, True)
                one(2 * i + 1, 1, True, True)
            one(NB - 2, 0, True, True)
            one(NB - 1, 1, False, True)

        with nc.Block() as block:
            @block.sync
            def _(sp):
                sp.wait_ge(const_ready, 1)

                def load(n, p):
                    for part in range(2):
                        for k in (part, part + 2):
                            sp.dma_start(qs[k * HD:(k + 1) * HD, p].bitcast(F32),
                                         scr["qk"][0, part, ds(n * HD, HD), :]).then_inc(ld[p], 16)
                        for k in (2 * part, 2 * part + 1):
                            sp.dma_start(ks[k * HD:(k + 1) * HD, p].bitcast(F32),
                                         scr["qk"][1, part, ds(n * HD, HD), :]).then_inc(ld[p], 16)
                    sp.dma_start(qs[4 * HD:KR, p].bitcast(F32), zero[:].bitcast(F32)).then_inc(ld[p], 16)

                def maxima(n, p):
                    sp.wait_ge(nmp_ready, n + 1)
                    for part in range(2):
                        sp.dma_start(qs[4 * HD + part:4 * HD + part + 1, p].bitcast(F32)
                                     .rearrange("a (q r) -> a q r", r=P), nmp[:, part, :].bitcast(F32)).then_inc(mrow[p], 16)

                load(0, 0)
                load(1, 1)
                maxima(0, 0)

                with sp.Fori(0, NB // 2 - 1) as i:
                    for p in range(2):
                        n = 2 * i + p
                        maxima(n + 1, 1 - p)
                        sp.wait_ge(s2_ready, 16 * (n + 1))
                        load(n + 2, p)
                maxima(NB - 1, 1)

            @block.tensor
            def _(pe):
                pe.wait_ge(const_ready, 1)

                def score_rows(n, p, u):
                    qt, kh = u // 2, u % 2
                    if u == 0:
                        pe.wait_ge(ld[p], NLD * (n // 2 + 1))
                    if isinstance(n, int) and n == 0:
                        if u >= 2:
                            pe.wait_ge(s1_done, u - 1)
                    else:
                        pe.wait_ge(s1_done, 16 * n + u - 1)
                    pe.matmul(s1[:, u % 2], qs[:, p, qt * P:qt * P + P], ks[:, p, kh * 512:kh * 512 + 512],
                              start=True, stop=True).then_inc(s1_ready, 1)

                def turn_maxima(n):
                    pe.wait_ge(nm_ready, n + 1)
                    pe.transpose(tm[0:NQ, 0:P], nm[:], ident[:]).then_inc(tm_ready, 1)

                def turn_out(n, qh):
                    pe.wait_ge(out_ready, 2 * n + qh + 1)
                    pe.wait_ge(to_done, 2 * n + qh)
                    for st in range(4):
                        t = pe.transpose(to[:, st * P:st * P + P], outT[:, st * P:st * P + P], ident[:])
                    t.then_inc(to_ready, 1)

                def values(n, p, s):
                    qh, kt = s // NQ, s % NQ
                    pe.wait_ge(p_ready, 16 * n + s + 1)
                    if s == 0:
                        pe.wait_ge(v_ready, n + 1)
                    if kt == 0:
                        pe.wait_ge(out_ready, 2 * n)
                    mm = pe.matmul(pv[0:HD + 1, qh], vs[:, p, kt], probs[:, qh, kt], start=kt == 0,
                                   stop=kt == NQ - 1)
                    if kt == NQ - 1:
                        mm.then_inc(pv_ready, 1)

                def one(n, p, nxt, prev):
                    for s in range(16):
                        qh, kt = s // NQ, s % NQ
                        if s == 0:
                            pe.wait_ge(mrow[p], 32 * (n // 2 + 1))
                        pe.wait_ge(p_ready, ring(16, n, s, 2))
                        pe.matmul(s2[:, s % 2], ks[:, p, kt * P:kt * P + P], qs[:, p, qh * 512:qh * 512 + 512],
                                  start=True, stop=True).then_inc(s2_ready, 1)
                        if nxt and 4 <= s < 12:
                            score_rows(n + 1, 1 - p, 2 * (s - 4))
                            score_rows(n + 1, 1 - p, 2 * (s - 4) + 1)
                        if s >= 2:
                            values(n, p, s - 2)
                        if s == 3 and prev:
                            turn_out(n - 1, 1)
                        if s == 12:
                            turn_out(n, 0)
                        if s == 13 and nxt:
                            turn_maxima(n + 1)
                    values(n, p, 14)
                    values(n, p, 15)

                for u in range(16):
                    score_rows(0, 0, u)
                turn_maxima(0)
                heads(pe, one)
                turn_out(NB - 1, 1)

            @block.scalar
            def _(act):
                with act.Fori(0, NB) as n:
                    act.wait_ge(pv_ready, 2 * n)
                    for s in range(16):
                        act.wait_ge(s2_ready, 16 * n + s + 1)
                        act.activation(probs[:, s // NQ, s % NQ], s2[:, s % 2], ACT.Exp,
                                       scale=float(HD) ** -0.5).then_inc(p_ready, 1)

            @block.vector
            def _(dve):
                dve.memset(zero[:].bitcast(mybir.dt.uint32), 0)
                dve.memset(ks[4 * HD:KR].bitcast(F32), 1.0)
                dve.memset(outT[:], 0.0)
                dve.drain()
                dve.memset(rc[:], 0.0).then_inc(const_ready, 1)

                def row_max(n, u):
                    dve.wait_ge(s1_ready, 16 * n + u + 1)
                    dve.reduce_max(mx[:, u // 2, u % 2:u % 2 + 1], s1[:, u % 2], AX.X).then_inc(s1_done, 1)

                def head_max(n):
                    dve.drain()
                    dve.tensor_reduce(nm[:], mx[:], AX.X, ALU.max, negate=True).then_inc(nm_ready, 1)

                def split_max(n, p):
                    dve.drain()
                    dve.wait_ge(tm_ready, n + 1)
                    dve.wait_ge(mrow[1 - p], 32 * ((n + p) // 2))
                    dve.tensor_copy(nmT[:], tm[0:NQ, 0:P])
                    dve.drain()
                    dve.tensor_copy(nmp[:, 0], nmT[:])
                    dve.drain()
                    dve.tensor_tensor(nmp[:, 1], nmT[:], nmp[:, 0].bitcast(F32), ALU.subtract)\
                       .then_inc(nmp_ready, 1)

                def copy_out(n, qh):
                    dve.drain()
                    dve.wait_ge(pv_ready, 2 * n + qh + 1)
                    dve.tensor_copy(outT[0:HD + 1], pv[0:HD + 1, qh]).then_inc(out_ready, 1)

                def normalise(n, qh):
                    dve.wait_ge(to_ready, 2 * n + qh + 1)
                    o = to[:].rearrange("p (s d) -> p s d", d=P)
                    dve.reciprocal(rc[:].rearrange("p (s d) -> p s d", d=1), o[:, :, HD:HD + 1])
                    dve.drain()
                    dve.tensor_tensor(ATT[:, ds((n // NH) * NQ + qh * 4, 4), ds((n % NH) * HD, HD)],
                                      o[:, :, 0:HD], rc[:].rearrange("p (s d) -> p s d", d=1)
                                      .to_broadcast([P, 4, HD]), ALU.mult).then_inc(to_done, 1)

                def one(n, p, nxt, prev):
                    if prev:
                        copy_out(n - 1, 1)
                        normalise(n - 1, 1)
                    if nxt:
                        for u in range(12):
                            row_max(n + 1, u)
                    copy_out(n, 0)
                    if nxt:
                        for u in range(12, 16):
                            row_max(n + 1, u)
                        head_max(n + 1)
                    normalise(n, 0)
                    if nxt:
                        split_max(n + 1, 1 - p)

                for u in range(16):
                    row_max(0, u)
                head_max(0)
                split_max(0, 0)
                heads(dve, one)
                copy_out(NB - 1, 1)
                normalise(NB - 1, 1)

            @block.gpsimd
            def _(pool):
                def take(n, p):
                    pool.tensor_copy(vs[:, p].rearrange("p k d -> p k d"),
                                     V[:, ds((n // NH) * NQ, NQ), ds(n % NH, 1), :]
                                     .rearrange("p k a d -> p k (a d)")).then_inc(v_ready, 1)
                take(0, 0)
                take(1, 1)
                with pool.Fori(1, NB // 2) as i:
                    for p in range(2):
                        pool.wait_ge(pv_ready, 4 * i + 2 * p - 2)
                        take(2 * i + p, p)


def turn_group(pe, s, g, xs, tb, ident, used=0, per=2):
    pe.wait_ge(s["xs_ready"], g + 1)
    for k in range(KD):
        pe.wait_ge(s["tb_done"], ring(per, g, k, 2))
        for st in range(GT):
            t = pe.transpose(tb[:, k, st * P:st * P + P], xs[:, st, k * P:k * P + P], ident[:])
        t.then_inc(s["tb_ready"], 1)


def stage_group(pool, s, g, xs, src, per=2):
    pool.wait_ge(s["tb_ready"], per * g)
    pool.tensor_copy(xs[:], src[:, ds(g * GT, GT), :]).then_inc(s["xs_ready"], 1)


def rstd_group(pool, s, n, mv, rstd, glob, k):
    eps, mhalf = glob["eps"], glob["mhalf"]
    pool.wait_ge(s["mv_ready"], n)
    pool.tensor_tensor(rstd[:], mv[:, :, 1], eps[:].to_broadcast([P, k]), ALU.add)
    pool.drain()
    pool.tensor_tensor(rstd[:], rstd[:], mhalf[:].to_broadcast([P, k]), ALU.pow).then_inc(s["rstd_ready"], 1)


def stats(dve, s, r, st6, mv, k):
    dve.drain()
    for i in range(k):
        dve.bn_stats(st6[:, i], r(i))
    dve.drain()
    for i in range(k):
        a = dve.bn_aggr(mv[:, i], st6[:, i])
    a.then_inc(s["mv_ready"], 1)


def attention_out(nc, glob, w):
    with ExitStack() as stack:
        c = Ctx(nc, stack)
        xs = c.sb("c_xs", [P, GT, D])
        xT = c.sb("c_xT", [P, KD, GW])
        pw = c.sb("c_pw", [P, KD, D])
        pb = c.sb("c_pb", [P, D])
        r = c.sb("c_r", [P, GT, D])
        st6 = c.sb("c_st6", [P, GT, 6])
        mv = c.sb("c_mv", [P, GT, 2])
        rstd = c.sb("c_rstd", [P, GT])
        tb = c.ps("c_tb", [P, 2, 512])
        acc = c.ps("c_acc", [P, 4, 512])
        names = ["loaded", "xs_ready", "tb_ready", "tb_done", "acc_ready", "acc_done", "mv_ready", "rstd_ready"]
        s = dict(zip(names, c.sems(*["c_" + n for n in names])))
        X, ident = glob["X"], glob["ident"]
        with nc.Block() as block:
            @block.sync
            def _(sp):
                sp.dma_start(pw[:], w["proj_w"].rearrange("(k p) n -> p k n", p=P)).then_inc(s["loaded"], 16)
                sp.dma_start(pb[:], w["proj_b"].to_broadcast([P, D])).then_inc(s["loaded"], 16)

            @block.gpsimd
            def _(pool):
                with pool.Fori(0, G) as g:
                    stage_group(pool, s, g, xs, glob["ATT"])
                    rstd_group(pool, s, g + 1, mv, rstd, glob, GT)

            @block.tensor
            def _(pe):
                pe.wait_ge(s["loaded"], 32)
                with pe.Fori(0, G) as g:
                    turn_group(pe, s, g, xs, tb, ident)
                    pe.wait_ge(s["tb_done"], 2 * g + 2)
                    for st in range(GT):
                        pe.wait_ge(s["acc_done"], GT * g)
                        for k in range(KD):
                            mm = pe.matmul(acc[:, st, 0:D], xT[:, k, st * P:st * P + P], pw[:, k],
                                           start=k == 0, stop=k == KD - 1)
                        mm.then_inc(s["acc_ready"], 1)

            @block.scalar
            def _(act):
                with act.Fori(0, G) as g:
                    for k in range(KD):
                        act.wait_ge(s["tb_ready"], KD * g + k + 1)
                        act.copy(xT[:, k], tb[:, k]).then_inc(s["tb_done"], 1)

            @block.vector
            def _(dve):
                dve.wait_ge(s["loaded"], 32)
                with dve.Fori(0, G) as g:
                    dve.drain()
                    for st in range(GT):
                        dve.wait_ge(s["acc_ready"], GT * g + st + 1)
                        dve.tensor_tensor(r[:, st], acc[:, st, 0:D], pb[:], ALU.add).then_inc(s["acc_done"], 1)
                    dve.drain()
                    dve.tensor_tensor(r[:], r[:], X[:, ds(g * GT, GT), :], ALU.add)
                    stats(dve, s, lambda i: r[:, i], st6, mv, GT)
                    dve.wait_ge(s["rstd_ready"], g + 1)
                    for st in range(GT):
                        dve.tensor_scalar(X[:, ds(g * GT + st, 1), :].rearrange("p a d -> p (a d)"), r[:, st],
                                          mv[:, st, 0:1], rstd[:, st:st + 1], ALU.subtract, ALU.mult)


def cross_attention(nc, glob, w, scr, first):
    tag = "e" if first else "h"
    scale = 64.0 ** -0.5 if first else float(HD) ** -0.5
    with ExitStack() as stack:
        c = Ctx(nc, stack)
        keys = c.sb(tag + "_keys", [P, B, KD, FL])
        vals = c.sb(tag + "_vals", [P, B, FB, D])
        X, ident = glob["X"], glob["ident"]
        BS = B * S
        LAST = FL - (FB - 1) * P

        with ExitStack() as inner:
            d = Ctx(nc, inner)
            cT = d.sb(tag + "_cT", [P, KD, BS])
            loaded, kv_ready, kv_done, m_ready, m_done, o_ready, o_done, stored, back, zeroed = d.sems(
                *[tag + "p_" + n for n in ("loaded", "kv_ready", "kv_done", "m_ready", "m_done", "o_ready",
                                           "o_done", "stored", "back", "zeroed")])
            if first:
                wk = d.sb("e_wk", [P, KD, D])
                wv = d.sb("e_wv", [P, KD, D])
                wq = d.sb("e_wq", [P, KH, D])
                wo = d.sb("e_wo", [P, KH, D])
                kvT = d.sb("e_kvT", [P, 2, KD, BS])
                vstage = d.sb("e_vstage", [S, B, NH, D])
                kvb = d.ps("e_kvb", [P, 2, 512])
                mb = d.ps("e_mb", [P, 2, 512])
                vb = d.ps("e_vb", [P, 4, 512])
                def head(rt, half):
                    return 8 * (rt // 4) + rt % 4 + 4 * half
                with nc.Block() as block:
                    @block.sync
                    def _(sp):
                        sp.dma_start(cT[:], w["ctxT"].rearrange("(k p) n -> p k n", p=P)).then_inc(loaded, 16)
                        for dst, name in ((wk, "WkT"), (wv, "WvT"), (wq, "WqR"), (wo, "WoR")):
                            sp.dma_start(dst[:], w[name].rearrange("(k p) n -> p k n", p=P)).then_inc(loaded, 16)
                        sp.wait_ge(o_done, 2 * KH)
                        sp.dma_start(scr["vals"].rearrange("b (h s) d -> s b h d", s=S), vstage[:])\
                          .then_inc(stored, 16)
                        sp.wait_ge(stored, 16)
                        for b in range(B):
                            sp.dma_start(vals[:, b, 0:FB - 1], scr["vals"][b, 0:(FB - 1) * P]
                                         .rearrange("(k p) d -> p k d", p=P)).then_inc(back, 16)
                            sp.dma_start(vals[0:LAST, b, FB - 1], scr["vals"][b, (FB - 1) * P:FL])\
                              .then_inc(back, 16)
                        sp.wait_ge(back, 64)

                    @block.tensor
                    def _(pe):
                        pe.wait_ge(loaded, 80)
                        for kv, wt in enumerate((wk, wv)):
                            for mt in range(KD):
                                for k in range(KD):
                                    mm = pe.matmul(kvb[:, kv, mt * BS:(mt + 1) * BS], wt[:, k, mt * P:mt * P + P],
                                                   cT[:, k], start=k == 0, stop=k == KD - 1)
                            mm.then_inc(kv_ready, 1)
                        pe.wait_ge(kv_done, 2)
                        for rt in range(KH):
                            for half in range(2):
                                rows = slice(64 * half, 64 * half + 64)
                                tile = head(rt, half) // 8
                                j = 2 * rt + half
                                if j >= 2:
                                    pe.wait_ge(m_done, j - 1)
                                for k in range(KD):
                                    mm = pe.matmul(mb[:, half, k * BS:(k + 1) * BS], wq[rows, rt, k * P:k * P + P],
                                                   kvT[rows, 0, tile], start=True, stop=True)
                                mm.then_inc(m_ready, 1)
                                if j >= 4:
                                    pe.wait_ge(o_done, j - 3)
                                for b in range(B):
                                    mm = pe.matmul(vb[0:S, 2 * (rt % 2) + half, b * D:(b + 1) * D],
                                                   kvT[rows, 1, tile, b * S:(b + 1) * S], wo[rows, rt],
                                                   start=True, stop=True)
                                mm.then_inc(o_ready, 1)

                    @block.vector
                    def _(dve):
                        for kv in range(2):
                            dve.wait_ge(kv_ready, kv + 1)
                            dve.tensor_copy(kvT[:, kv], kvb[:, kv, 0:KD * BS].rearrange("p (k n) -> p k n", k=KD))\
                               .then_inc(kv_done, 1)
                        for j in range(2 * KH):
                            h = head(j // 2, j % 2)
                            dve.wait_ge(m_ready, j + 1)
                            for k in range(KD):
                                cp = dve.tensor_copy(keys[:, :, k, h * S:(h + 1) * S],
                                                     mb[:, j % 2, k * BS:(k + 1) * BS]
                                                     .rearrange("p (b s) -> p b s", b=B))
                            cp.then_inc(m_done, 1)

                    @block.scalar
                    def _(act):
                        for j in range(2 * KH):
                            h = head(j // 2, j % 2)
                            act.wait_ge(o_ready, j + 1)
                            act.copy(vstage[:, :, h], vb[0:S, 2 * (j // 2 % 2) + j % 2]
                                     .rearrange("p (b d) -> p b d", b=B)).then_inc(o_done, 1)
            else:
                wc = d.sb("h_wc", [P, KD, D])
                vb = d.ps("h_vb", [P, 2, 512])
                with nc.Block() as block:
                    @block.sync
                    def _(sp):
                        sp.dma_start(wc[:], w["WcT"].rearrange("(k p) n -> p k n", p=P)).then_inc(loaded, 16)
                        sp.wait_ge(zeroed, 1)
                        for h in range(NH):
                            r0 = (h % 8) * HD
                            sp.dma_start(keys[r0:r0 + HD, :, h // 8, h * S:(h + 1) * S],
                                         w["ctxT"][h * HD:(h + 1) * HD].rearrange("r (b s) -> r b s", b=B))\
                              .then_inc(loaded, 16)

                    @block.vector
                    def _(dve):
                        dve.memset(keys[:], 0.0).then_inc(zeroed, 1)
                        for j in range(B * FB):
                            b, blk = j // FB, j % FB
                            rows = P if blk < FB - 1 else LAST
                            dve.wait_ge(o_ready, j + 1)
                            dve.tensor_copy(vals[0:rows, b, blk], vb[0:rows, j % 2, 0:D]).then_inc(o_done, 1)

                    @block.tensor
                    def _(pe):
                        pe.wait_ge(loaded, 16 * (NH + 1))
                        for j in range(B * FB):
                            b, blk = j // FB, j % FB
                            rows = P if blk < FB - 1 else LAST
                            if j >= 2:
                                pe.wait_ge(o_done, j - 1)
                            for k in range(KD):
                                mm = pe.matmul(vb[0:rows, j % 2, 0:D], keys[:, b, k, blk * P:blk * P + rows],
                                               wc[:, k], start=k == 0, stop=k == KD - 1)
                            mm.then_inc(o_ready, 1)

        xs = c.sb(tag + "_xs", [P, GT, D])
        xT = c.sb(tag + "_xT", [P, KD, GW])
        pr = c.sb(tag + "_pr", [P, 2, FL])
        pT = c.sb(tag + "_pT", [P, FB, P])
        r = c.sb(tag + "_r", [P, GT, D])
        mx = c.sb(tag + "_mx", [P, 2, NH])
        sm = c.sb(tag + "_sm", [P, 2, NH])
        st6 = c.sb(tag + "_st6", [P, GT, 6])
        mv = c.sb(tag + "_mv", [P, GT, 2])
        rstd = c.sb(tag + "_rstd", [P, GT])
        sc = c.ps(tag + "_sc", [P, 3 * 512])
        tb = c.ps(tag + "_tb", [P, 2, 512])
        acc = c.ps(tag + "_acc", [P, 2, 512])
        names = ["xs_ready", "tb_ready", "tb_done", "s_ready", "d_ready", "e_ready", "p_ready",
                 "acc_ready", "acc_done", "mv_ready", "rstd_ready"]
        s = dict(zip(names, c.sems(*[tag + "_" + n for n in names])))
        NB3 = -(-FB // 4)
        PER = KD + GT * NB3
        if first:
            products = [[(a, min(a + 512, FL), k) for k in range(KD)] for a in range(0, FL, 512)]
        else:
            mid = FL // 2
            products = [[(0, 512, 0)], [(512, mid, 0)], [(mid, 1024, 1)], [(1024, FL, 1)]]
        with nc.Block() as block:
            @block.gpsimd
            def _(pool):
                with pool.Fori(0, G) as g:
                    stage_group(pool, s, g, xs, X, PER)
                    rstd_group(pool, s, g + 1, mv, rstd, glob, GT)

            @block.tensor
            def _(pe):
                with pe.Fori(0, G) as g:
                    b = g // 2

                    def scores(st):
                        pe.wait_ge(s["d_ready"], GT * g + st)
                        for group in products:
                            for i, (a, z, k) in enumerate(group):
                                mm = pe.matmul(sc[:, a:z], xT[:, k, st * P:st * P + P],
                                               keys[:, ds(b, 1), k, a:z].rearrange("p a n -> p (a n)"),
                                               start=i == 0, stop=i == len(group) - 1)
                        mm.then_inc(s["s_ready"], 1)

                    turn_group(pe, s, g, xs, tb, ident, per=PER)
                    pe.wait_ge(s["tb_done"], PER * g + KD)
                    scores(0)
                    for st in range(GT):
                        if st < GT - 1:
                            scores(st + 1)
                        pe.wait_ge(s["p_ready"], GT * g + st + 1)
                        for q in range(NB3):
                            j = KD + NB3 * st + q
                            pe.wait_ge(s["tb_done"], ring(PER, g, j, 2))
                            for blk in range(4 * q, min(4 * q + 4, FB)):
                                rows = P if blk < FB - 1 else LAST
                                t = pe.transpose(tb[0:rows, j % 2, (blk % 4) * P:(blk % 4) * P + P],
                                                 pr[:, st % 2, blk * P:blk * P + rows], ident[:])
                            t.then_inc(s["tb_ready"], 1)
                        pe.wait_ge(s["tb_done"], PER * g + KD + NB3 * (st + 1))
                        pe.wait_ge(s["acc_done"], ring(GT, g, st, 2))
                        for blk in range(FB):
                            rows = P if blk < FB - 1 else LAST
                            mm = pe.matmul(acc[:, st % 2, 0:D], pT[0:rows, blk],
                                           vals[0:rows, ds(b, 1), blk].rearrange("p a n -> p (a n)"),
                                           start=blk == 0, stop=blk == FB - 1)
                        mm.then_inc(s["acc_ready"], 1)

            @block.scalar
            def _(act):
                with act.Fori(0, G) as g:
                    for k in range(KD):
                        act.wait_ge(s["tb_ready"], PER * g + k + 1)
                        act.copy(xT[:, k], tb[:, k]).then_inc(s["tb_done"], 1)

                    def exps(st):
                        act.wait_ge(s["d_ready"], GT * g + st + 1)
                        act.activation(pr[:, st % 2], pr[:, st % 2], ACT.Exp, scale=scale)\
                           .then_inc(s["e_ready"], 1)

                    exps(0)
                    for st in range(GT):
                        if st < GT - 1:
                            exps(st + 1)
                        for q in range(NB3):
                            j = KD + NB3 * st + q
                            act.wait_ge(s["tb_ready"], PER * g + j + 1)
                            if q < NB3 - 1:
                                act.copy(pT[:, 4 * q:4 * q + 4], tb[:, j % 2].rearrange("p (a n) -> p a n", n=P))\
                                   .then_inc(s["tb_done"], 1)
                            else:
                                full = (FB - 1) % 4
                                act.copy(pT[:, 4 * q:FB - 1], tb[:, j % 2, 0:full * P]
                                         .rearrange("p (a n) -> p a n", n=P))
                                act.copy(pT[0:LAST, FB - 1], tb[0:LAST, j % 2, full * P:full * P + P])\
                                   .then_inc(s["tb_done"], 1)

            @block.vector
            def _(dve):
                with dve.Fori(0, G) as g:
                    def shift(st):
                        q = st % 2
                        dve.drain()
                        dve.wait_ge(s["s_ready"], GT * g + st + 1)
                        dve.tensor_reduce(mx[:, q], sc[:, 0:FL].rearrange("p (h s) -> p h s", s=S), AX.X, ALU.max)
                        dve.drain()
                        dve.tensor_tensor(pr[:, q].rearrange("p (h s) -> p h s", s=S),
                                          sc[:, 0:FL].rearrange("p (h s) -> p h s", s=S),
                                          mx[:, q].rearrange("p (h a) -> p h a", a=1).to_broadcast([P, NH, S]),
                                          ALU.subtract).then_inc(s["d_ready"], 1)

                    def norm(st):
                        q = st % 2
                        dve.wait_ge(s["e_ready"], GT * g + st + 1)
                        e = pr[:, q].rearrange("p (h s) -> p h s", s=S)
                        dve.tensor_reduce(sm[:, q], e, AX.X, ALU.add)
                        dve.drain()
                        dve.reciprocal(sm[:, q], sm[:, q])
                        dve.drain()
                        dve.tensor_tensor(e, e, sm[:, q].rearrange("p (h a) -> p h a", a=1)
                                          .to_broadcast([P, NH, S]), ALU.mult).then_inc(s["p_ready"], 1)

                    def residual(st):
                        dve.wait_ge(s["acc_ready"], GT * g + st + 1)
                        dve.tensor_tensor(r[:, st], acc[:, st % 2, 0:D],
                                          X[:, ds(g * GT + st, 1), :].rearrange("p a d -> p (a d)"),
                                          ALU.add).then_inc(s["acc_done"], 1)

                    shift(0)
                    for st in range(GT):
                        if st < GT - 1:
                            shift(st + 1)
                        norm(st)
                        if st:
                            residual(st - 1)
                    residual(GT - 1)
                    stats(dve, s, lambda i: r[:, i], st6, mv, GT)
                    dve.wait_ge(s["rstd_ready"], g + 1)
                    for st in range(GT):
                        dve.tensor_scalar(X[:, ds(g * GT + st, 1), :].rearrange("p a d -> p (a d)"), r[:, st],
                                          mv[:, st, 0:1], rstd[:, st:st + 1], ALU.subtract, ALU.mult)


def mixture_of_experts(nc, glob, w):
    FT = -(-F // P)
    FP = [min(P, F - P * i) for i in range(FT)]
    with ExitStack() as stack:
        c = Ctx(nc, stack)
        xs = c.sb("f_xs", [P, GT, D])
        XT = c.sb("f_XT", [P, KD, T])
        gw = c.sb("f_gw", [P, KD, E])
        wgu = c.sb("f_wgu", [P, 2, 2, KD, F])
        wd = c.sb("f_wd", [P, 2, FT, D])
        rank = c.sb("f_rank", [P, GT, E])
        lg = c.sb("f_lg", [P, GT, E])
        pe_ = c.sb("f_scores", [P, GT, E])
        hot1 = c.sb("f_hot1", [P, GT, E])
        hot2 = c.sb("f_hot2", [P, GT, E])
        tmp = c.sb("f_tmp", [P, GT, E])
        m0 = c.sb("f_m0", [P, GT, 1])
        m1 = c.sb("f_m1", [P, GT, 1])
        m2 = c.sb("f_m2", [P, GT, 1])
        den = c.sb("f_den", [P, GT, 1])
        lgT = c.sb("f_lgT", [P, GW])
        comb = c.sb("f_comb", [P, NE, NT])
        ce = c.sb("f_ce", [P, 2, NT])
        sg = c.sb("f_sg", [P, 2, 512])
        hid = c.sb("f_hid", [P, 2, FT, 512])
        st6 = c.sb("f_st6", [P, GT, 6])
        mv = c.sb("f_mv", [P, GT, 2])
        rstd = c.sb("f_rstd", [P, GT])
        tb = c.ps("f_tb", [P, 2, 512])
        gu = c.ps("f_gu", [P, 2, 2, 512])
        acc = c.ps("f_acc", [P, 2, 512])
        names = ["loaded", "xs_ready", "tb_ready", "tb_done", "l_ready", "l_done", "x_ready", "sub_ready",
                 "exp_ready", "gu_ready", "sg_ready", "h_done", "acc_ready", "acc_done", "ce_ready", "mv_ready",
                 "rstd_ready", "wl0", "wl1", "rank_ready"]
        s = dict(zip(names, c.sems(*["f_" + n for n in names])))
        wl = [s["wl0"], s["wl1"]]
        X, ident = glob["X"], glob["ident"]
        HPE = G * FT

        with nc.Block() as block:
            @block.sync
            def _(sp):
                def load(e, p):
                    sp.dma_start(wgu[:, p], w["w_gu"][ds(e, 1)].rearrange("a u (k p) f -> p (a u) k f", p=P))\
                      .then_inc(wl[p], 16)
                    sp.dma_start(wd[:, p, 0:FT - 1], w["w_dn"][ds(e, 1), 0:(FT - 1) * P]
                                 .rearrange("a (k p) d -> p (a k) d", p=P)).then_inc(wl[p], 16)
                    sp.dma_start(wd[0:FP[-1], p, FT - 1], w["w_dn"][ds(e, 1), (FT - 1) * P:F]
                                 .rearrange("a p d -> p (a d)")).then_inc(wl[p], 16)
                sp.dma_start(gw[:], w["gate_wT"].rearrange("(k p) e -> p k e", p=P)).then_inc(s["loaded"], 16)
                load(0, 0)
                load(1, 1)
                with sp.Fori(1, NE // 2) as i:
                    for p in range(2):
                        sp.wait_ge(s["acc_ready"], NT * (2 * i + p - 1))
                        load(2 * i + p, p)

            @block.gpsimd
            def _(pool):
                for j in range(E):
                    pool.memset(rank[:, :, j:j + 1], float(E - j))
                pool.drain()
                pool.memset(comb[:, E:NE], 1.0).then_inc(s["rank_ready"], 1)
                with pool.Fori(0, G) as g:
                    stage_group(pool, s, g, xs, X)
                pool.wait_ge(s["x_ready"], G)
                with pool.Fori(0, NE // 2) as i:
                    for p in range(2):
                        e = 2 * i + p
                        pool.wait_ge(s["acc_done"], NT * e)
                        pool.tensor_copy(ce[:, p:p + 1], comb[:, ds(e, 1)]).then_inc(s["ce_ready"], 1)
                with pool.Fori(0, G) as g:
                    rstd_group(pool, s, g + 1, mv, rstd, glob, GT)

            @block.tensor
            def _(pe):
                pe.wait_ge(s["loaded"], 16)
                with pe.Fori(0, G) as g:
                    turn_group(pe, s, g, xs, tb, ident)
                    pe.wait_ge(s["tb_done"], 2 * g + 2)
                    pe.wait_ge(s["l_done"], g)
                    for k in range(KD):
                        mm = pe.matmul(acc[0:E, 0], gw[:, k], XT[:, k, ds(g * GW, GW)], start=k == 0,
                                       stop=k == KD - 1)
                    mm.then_inc(s["l_ready"], 1)
                    pe.wait_ge(s["sub_ready"], 2 * g + 1)
                    for st in range(GT):
                        t = pe.transpose(acc[:, 1, st * P:st * P + P], lgT[:, st * P:st * P + P], ident[:])
                    t.then_inc(s["l_ready"], 1)

                with pe.Fori(0, NE // 2) as i:
                    for p in range(2):
                        e = 2 * i + p

                        def up(g):
                            for hm in range(FT):
                                j = FT * g + hm
                                pe.wait_ge(s["h_done"], ring(HPE, e, j, 2))
                                if j == 0:
                                    pe.wait_ge(wl[p], 48 * (i + 1))
                                for u in range(2):
                                    for k in range(KD):
                                        mm = pe.matmul(gu[0:FP[hm], j % 2, u],
                                                       wgu[:, p, u, k, hm * P:hm * P + FP[hm]],
                                                       XT[:, k, g * GW:g * GW + GW], start=k == 0,
                                                       stop=k == KD - 1)
                                mm.then_inc(s["gu_ready"], 1)

                        def down(g):
                            pe.wait_ge(s["h_done"], HPE * e + FT * (g + 1))
                            for st in range(GT):
                                pe.wait_ge(s["acc_done"], ring(NT, e, GT * g + st, 2))
                                for hm in range(FT):
                                    mm = pe.matmul(acc[:, st % 2, 0:D], hid[0:FP[hm], g % 2, hm, st * P:st * P + P],
                                                   wd[0:FP[hm], p, hm], start=hm == 0, stop=hm == FT - 1)
                                mm.then_inc(s["acc_ready"], 1)

                        up(0)
                        for g in range(1, G):
                            up(g)
                            down(g - 1)
                        down(G - 1)

            @block.scalar
            def _(act):
                with act.Fori(0, G) as g:
                    for k in range(KD):
                        act.wait_ge(s["tb_ready"], KD * g + k + 1)
                        act.copy(XT[:, k, ds(g * GW, GW)], tb[:, k]).then_inc(s["tb_done"], 1)
                    act.wait_ge(s["sub_ready"], 2 * g + 2)
                    act.activation(pe_[:], lg[:], ACT.Exp).then_inc(s["exp_ready"], 1)
                with act.Fori(0, NE) as e:
                    for j in range(HPE):
                        act.wait_ge(s["gu_ready"], HPE * e + j + 1)
                        act.wait_ge(s["h_done"], ring(HPE, e, j, 2))
                        n = FP[j % FT]
                        act.activation(sg[0:n, j % 2], gu[0:n, j % 2, 0], ACT.Silu).then_inc(s["sg_ready"], 1)

            @block.vector
            def _(dve):
                dve.memset(lgT[:], 0.0)
                dve.drain()
                dve.wait_ge(s["rank_ready"], 1)

                def wide(a):
                    return a[:].to_broadcast([P, GT, E])

                def first_of(hot, scores, top):
                    dve.tensor_tensor(tmp[:], scores[:], wide(top), ALU.is_equal)
                    dve.drain()
                    dve.tensor_tensor(tmp[:], tmp[:], rank[:], ALU.mult)
                    dve.drain()
                    dve.tensor_reduce(m0[:], tmp[:], AX.X, ALU.max)
                    dve.drain()
                    dve.tensor_tensor(hot[:], tmp[:], wide(m0), ALU.is_equal)
                    dve.drain()

                with dve.Fori(0, G) as g:
                    dve.drain()
                    dve.wait_ge(s["l_ready"], 2 * g + 1)
                    dve.tensor_copy(lgT[0:E], acc[0:E, 0]).then_inc(s["sub_ready"], 1)
                    dve.wait_ge(s["l_ready"], 2 * g + 2)
                    dve.tensor_copy(tmp[:], acc[:, 1].rearrange("p (s e) -> p s e", e=P)[:, :, 0:E])\
                       .then_inc(s["l_done"], 1)
                    dve.drain()
                    dve.tensor_reduce(m0[:], tmp[:], AX.X, ALU.max)
                    dve.drain()
                    dve.tensor_tensor(lg[:], tmp[:], wide(m0), ALU.subtract).then_inc(s["sub_ready"], 1)
                    dve.wait_ge(s["exp_ready"], g + 1)
                    dve.tensor_reduce(den[:], pe_[:], AX.X, ALU.add)
                    dve.drain()
                    dve.reciprocal(den[:], den[:])
                    dve.drain()
                    dve.tensor_tensor(pe_[:], pe_[:], wide(den), ALU.mult)
                    dve.drain()
                    dve.tensor_reduce(m1[:], pe_[:], AX.X, ALU.max)
                    dve.drain()
                    first_of(hot1, pe_, m1)
                    dve.scalar_tensor_tensor(out=pe_[:], in0=hot1[:], scalar=-2.0, in1=pe_[:], op0=ALU.mult,
                                             op1=ALU.add)
                    dve.drain()
                    dve.tensor_reduce(m2[:], pe_[:], AX.X, ALU.max)
                    dve.drain()
                    first_of(hot2, pe_, m2)
                    dve.tensor_tensor(den[:], m1[:], m2[:], ALU.add)
                    dve.drain()
                    dve.tensor_scalar(den[:], den[:], 1e-20, None, ALU.add)
                    dve.drain()
                    dve.reciprocal(den[:], den[:])
                    dve.drain()
                    dve.scalar_tensor_tensor(out=m1[:], in0=m1[:], scalar=2.5, in1=den[:], op0=ALU.mult,
                                             op1=ALU.mult)
                    dve.scalar_tensor_tensor(out=m2[:], in0=m2[:], scalar=2.5, in1=den[:], op0=ALU.mult,
                                             op1=ALU.mult)
                    dve.drain()
                    dve.tensor_tensor(hot1[:], hot1[:], wide(m1), ALU.mult)
                    dve.tensor_tensor(hot2[:], hot2[:], wide(m2), ALU.mult)
                    dve.drain()
                    dve.tensor_tensor(comb[:, 0:E, ds(g * GT, GT)].rearrange("p e s -> p s e"), hot1[:], hot2[:],
                                      ALU.add).then_inc(s["x_ready"], 1)

                with dve.Fori(0, NE // 2) as i:
                    for p in range(2):
                        e = 2 * i + p

                        def hidden(g):
                            for hm in range(FT):
                                j = FT * g + hm
                                n = FP[hm]
                                dve.wait_ge(s["sg_ready"], HPE * e + j + 1)
                                dve.tensor_tensor(hid[0:n, g % 2, hm], sg[0:n, j % 2], gu[0:n, j % 2, 1],
                                                  ALU.mult).then_inc(s["h_done"], 1)

                        def add_up(g):
                            if g == 0:
                                dve.wait_ge(s["ce_ready"], e + 1)
                            for st in range(GT):
                                t = g * GT + st
                                dve.wait_ge(s["acc_ready"], NT * e + t + 1)
                                dve.scalar_tensor_tensor(out=X[:, t], in0=acc[:, st % 2, 0:D],
                                                         scalar=ce[:, p, t:t + 1], in1=X[:, t], op0=ALU.mult,
                                                         op1=ALU.add).then_inc(s["acc_done"], 1)

                        hidden(0)
                        for g in range(1, G):
                            hidden(g)
                            add_up(g - 1)
                        add_up(G - 1)

                with dve.Fori(0, G) as g:
                    stats(dve, s, lambda i: X[:, ds(g * GT + i, 1), :].rearrange("p a d -> p (a d)"), st6, mv, GT)
                    dve.wait_ge(s["rstd_ready"], g + 1)
                    for st in range(GT):
                        x = X[:, ds(g * GT + st, 1), :].rearrange("p a d -> p (a d)")
                        dve.tensor_scalar(x, x, mv[:, st, 0:1], rstd[:, st:st + 1], ALU.subtract, ALU.mult)


def delta_rule(nc, glob, w):
    NP = NT // 2
    KW = HID // NH
    CH = 7
    with ExitStack() as stack:
        c = Ctx(nc, stack)
        ws = c.sb("g_ws", [P, KD, 3 * HID + NH])
        wo = c.sb("g_wo", [P, KH, D])
        lnw = c.sb("g_lnw", [P, D])
        lnb = c.sb("g_lnb", [P, D])
        hs = c.sb("g_hs", [P, 2, D])
        hT = c.sb("g_hT", [P, 2, KD, P])
        st6 = c.sb("g_st6", [P, 2, 6])
        mv = c.sb("g_mv", [P, 2, 2])
        rstd = c.sb("g_rstd", [P, 2])
        ut = c.sb("g_ut", [P, 2, 512])
        qk = c.sb("g_qk", [P, 2, 2, HID])
        vb = c.sb("g_vb", [P, 2, HID])
        bt = c.sb("g_bt", [P, 2, NH])
        prod = c.sb("g_prod", [P, 4, HID])
        sums = c.sb("g_sums", [P, 4, NH])
        dots = c.sb("g_dots", [P, 4, NH])
        fac = c.sb("g_fac", [P, 4, NH])
        co = c.sb("g_co", [P, 3, NH])
        out = c.sb("g_out", [P, 2, HID])
        oT = c.sb("g_oT", [P, 2, KH, P])
        r = c.sb("g_r", [P, 2, D])
        hb = c.ps("g_hb", [P, 512])
        ch = c.ps("g_ch", [P, 3, 512])
        tb = c.ps("g_tb", [P, 2, 512])
        acc = c.ps("g_acc", [P, 2, 512])
        names = ["loaded", "mv_ready", "rstd_ready", "hs_ready", "hb_ready", "hT_ready", "ch_ready", "act_done",
                 "t_ready", "stt_done", "qk_ready", "prod_ready", "co_ready", "part_ready", "o_ready", "tb_ready",
                 "tb_done", "acc_ready", "acc_done"]
        s = dict(zip(names, c.sems(*["g_" + n for n in names])))
        X, ident = glob["X"], glob["ident"]

        def heads(a):
            return a.rearrange("p (h d) -> p h d", h=NH)

        with nc.Block() as block:
            @block.sync
            def _(sp):
                for k in range(KD):
                    sp.dma_start(ws[:, k], w["w_slow"][k * P:(k + 1) * P]).then_inc(s["loaded"], 16)
                sp.dma_start(wo[:], w["w_out"].rearrange("(k p) n -> p k n", p=P)).then_inc(s["loaded"], 16)
                sp.dma_start(lnw[:], w["ln_w"].to_broadcast([P, D])).then_inc(s["loaded"], 16)
                sp.dma_start(lnb[:], w["ln_b"].to_broadcast([P, D])).then_inc(s["loaded"], 16)

            @block.gpsimd
            def _(pool):
                def dot_products(p):
                    pool.wait_ge(s["qk_ready"], p + 1)
                    q0, k0, q1, k1 = qk[:, 0, 0], qk[:, 0, 1], qk[:, 1, 0], qk[:, 1, 1]
                    for i, (a, b) in enumerate(((k0, q0), (k0, k1), (k0, q1), (k1, q1))):
                        pool.tensor_tensor(prod[:, i], a, b, ALU.mult).then_inc(s["prod_ready"], 1)

                def outputs(p):
                    pool.wait_ge(s["co_ready"], p + 1)
                    pool.wait_ge(s["act_done"], 2 * CH * p + 2 * CH)
                    pool.wait_ge(s["tb_ready"], 4 * p)
                    pool.tensor_tensor(heads(out[:, 0]), heads(vb[:, 0]), co[:, 0].rearrange(
                        "p (h a) -> p h a", a=1).to_broadcast([P, NH, KW]), ALU.mult).then_inc(s["part_ready"], 1)
                    pool.tensor_tensor(heads(prod[:, 0]), heads(vb[:, 1]), co[:, 2].rearrange(
                        "p (h a) -> p h a", a=1).to_broadcast([P, NH, KW]), ALU.mult).then_inc(s["part_ready"], 1)

                with pool.Fori(0, NP) as p:
                    rstd_group(pool, s, 2 * p + 1, mv, rstd, glob, 2)
                    dot_products(p)
                    outputs(p)
                    rstd_group(pool, s, 2 * p + 2, mv, rstd, glob, 2)

            @block.tensor
            def _(pe):
                def project(p):
                    pe.wait_ge(s["hs_ready"], p + 1)
                    pe.wait_ge(s["hT_ready"], p)
                    for tm in range(2):
                        for k in range(KD):
                            a = (tm * KD + k) * P
                            t = pe.transpose(hb[:, a:a + P], hs[:, tm, k * P:k * P + P], ident[:])
                    t.then_inc(s["hb_ready"], 1)
                    pe.wait_ge(s["hT_ready"], p + 1)
                    for j in range(2 * CH):
                        tm, q = j // CH, j % CH
                        width = 512 if q < 6 else NH
                        if j < 3:
                            pe.wait_ge(s["act_done"], 2 * CH * p)
                            pe.wait_ge(s["stt_done"], 8 * p)
                        elif (j - 3) % CH < 4:
                            pe.wait_ge(s["stt_done"], 8 * p + 4 * ((j - 3) // CH) + (j - 3) % CH + 1)
                        else:
                            pe.wait_ge(s["act_done"], 2 * CH * p + j - 3 + 1)
                        for k in range(KD):
                            mm = pe.matmul(ch[:, j % 3, 0:width], hT[:, tm, k], ws[:, k, q * 512:q * 512 + width],
                                           start=k == 0, stop=k == KD - 1)
                        mm.then_inc(s["ch_ready"], 1)

                def project_out(p):
                    pe.wait_ge(s["o_ready"], p + 1)
                    for q in range(4):
                        pe.wait_ge(s["tb_done"], ring(4, p, q, 2))
                        for blk in range(4):
                            b8 = (q % 2) * 4 + blk
                            t = pe.transpose(tb[:, q % 2, blk * P:blk * P + P],
                                             out[:, q // 2, b8 * P:b8 * P + P], ident[:])
                        t.then_inc(s["tb_ready"], 1)
                    for tm in range(2):
                        pe.wait_ge(s["tb_done"], 4 * p + 2 * tm + 2)
                        pe.wait_ge(s["acc_done"], 2 * p)
                        for k in range(KH):
                            mm = pe.matmul(acc[:, tm, 0:D], oT[:, tm, k], wo[:, k], start=k == 0, stop=k == KH - 1)
                        mm.then_inc(s["acc_ready"], 1)

                pe.wait_ge(s["loaded"], 16 * (KD + 3))
                with pe.Fori(0, NP) as p:
                    project(p)
                    project_out(p)

            @block.scalar
            def _(act):
                with act.Fori(0, NP) as p:
                    act.wait_ge(s["hb_ready"], p + 1)
                    act.copy(hT[:], hb[:].rearrange("p (t k n) -> p t k n", t=2, k=KD)).then_inc(s["hT_ready"], 1)
                    n = 0
                    for j in range(2 * CH):
                        tm, q = j // CH, j % CH
                        act.wait_ge(s["ch_ready"], 2 * CH * p + j + 1)
                        if q < 4:
                            act.wait_ge(s["stt_done"], ring(8, p, n, 2))
                            act.activation(ut[:, n % 2], ch[:, j % 3], ACT.Relu, scale=-1.0)\
                               .then_inc(s["act_done"], 1)
                            act.drain()
                            act.activation(ut[:, n % 2], ut[:, n % 2], ACT.Exp, scale=-1.0)\
                               .then_inc(s["t_ready"], 1)
                            n += 1
                        elif q < 6:
                            if j == 4:
                                act.wait_ge(s["o_ready"], p)
                            act.copy(vb[:, tm, (q - 4) * 512:(q - 3) * 512], ch[:, j % 3])\
                               .then_inc(s["act_done"], 1)
                        else:
                            if tm == 0:
                                act.wait_ge(s["co_ready"], p)
                            act.activation(bt[:, tm], ch[:, j % 3, 0:NH], ACT.Tanh, scale=0.5)\
                               .then_inc(s["act_done"], 1)
                    for q in range(4):
                        act.wait_ge(s["tb_ready"], 4 * p + q + 1)
                        act.copy(oT[:, q // 2, (q % 2) * 4:(q % 2) * 4 + 4],
                                 tb[:, q % 2].rearrange("p (b n) -> p b n", n=P)).then_inc(s["tb_done"], 1)

            @block.vector
            def _(dve):
                dve.wait_ge(s["loaded"], 16 * (KD + 3))

                def tile(p, tm):
                    return X[:, ds(p + NP * tm, 1), :].rearrange("p a d -> p (a d)")

                def normed(p):
                    stats(dve, s, lambda i: tile(p, i), st6, mv, 2)
                    dve.wait_ge(s["rstd_ready"], 2 * p + 1)
                    dve.wait_ge(s["hb_ready"], p)
                    for tm in range(2):
                        dve.tensor_scalar(hs[:, tm], tile(p, tm), mv[:, tm, 0:1], rstd[:, tm:tm + 1],
                                          ALU.subtract, ALU.mult)
                    dve.drain()
                    for tm in range(2):
                        dve.tensor_tensor(hs[:, tm], hs[:, tm], lnw[:], ALU.mult)
                    dve.drain()
                    for tm in range(2):
                        a = dve.tensor_tensor(hs[:, tm], hs[:, tm], lnb[:], ALU.add)
                    a.then_inc(s["hs_ready"], 1)

                def positive(p):
                    n = 0
                    for j in range(2 * CH):
                        tm, q = j // CH, j % CH
                        if q < 4:
                            dve.wait_ge(s["t_ready"], 8 * p + n + 1)
                            dve.scalar_tensor_tensor(out=qk[:, tm, q // 2, (q % 2) * 512:(q % 2) * 512 + 512],
                                                     in0=ch[:, j % 3], scalar=0.0, in1=ut[:, n % 2], op0=ALU.max,
                                                     op1=ALU.add).then_inc(s["stt_done"], 1)
                            n += 1
                    dve.drain()
                    dve.tensor_reduce(sums[:].rearrange("p a h -> p (a h)"),
                                      qk[:].rearrange("p t a (h d) -> p (t a h) d", h=NH), AX.X, ALU.add)\
                       .then_inc(s["qk_ready"], 1)

                def coefficients(p):
                    dve.drain()
                    dve.reciprocal(sums[:], sums[:])
                    dve.drain()
                    q0, k0, q1, k1 = (sums[:, i] for i in range(4))
                    for i, (a, b) in enumerate(((k0, q0), (k0, k1), (k0, q1), (k1, q1))):
                        dve.tensor_tensor(fac[:, i], a, b, ALU.mult)
                    for i in range(4):
                        dve.wait_ge(s["prod_ready"], 4 * p + i + 1)
                        dve.tensor_reduce(dots[:, i], heads(prod[:, i]), AX.X, ALU.add)
                    dve.drain()
                    dve.wait_ge(s["act_done"], 2 * CH * p + 2 * CH)
                    dve.tensor_tensor(dots[:], dots[:], fac[:], ALU.mult)
                    dve.tensor_scalar(bt[:], bt[:], 0.5, 0.5, ALU.mult, ALU.add)
                    dve.drain()
                    b0, b1 = bt[:, 0], bt[:, 1]
                    dve.tensor_tensor(co[:, 0], b0, dots[:, 0], ALU.mult)
                    dve.tensor_tensor(fac[:, 0], b0, dots[:, 1], ALU.mult)
                    dve.tensor_tensor(fac[:, 1], b0, dots[:, 2], ALU.mult)
                    dve.tensor_tensor(co[:, 2], b1, dots[:, 3], ALU.mult)
                    dve.drain()
                    dve.tensor_tensor(fac[:, 0], fac[:, 0], co[:, 2], ALU.mult)
                    dve.drain()
                    dve.tensor_tensor(co[:, 1], fac[:, 1], fac[:, 0], ALU.subtract).then_inc(s["co_ready"], 1)
                    dve.drain()
                    dve.wait_ge(s["tb_ready"], 4 * p)
                    dve.tensor_tensor(heads(out[:, 1]), heads(vb[:, 0]), co[:, 1].rearrange(
                        "p (h a) -> p h a", a=1).to_broadcast([P, NH, KW]), ALU.mult)
                    dve.drain()
                    dve.wait_ge(s["part_ready"], 2 * p + 2)
                    dve.tensor_tensor(out[:, 1], out[:, 1], prod[:, 0], ALU.add).then_inc(s["o_ready"], 1)

                def residual(p):
                    dve.drain()
                    for tm in range(2):
                        dve.wait_ge(s["acc_ready"], 2 * p + tm + 1)
                        dve.scalar_tensor_tensor(out=r[:, tm], in0=tile(p, tm), scalar=2.0, in1=acc[:, tm, 0:D],
                                                 op0=ALU.mult, op1=ALU.add).then_inc(s["acc_done"], 1)
                    stats(dve, s, lambda i: r[:, i], st6, mv, 2)
                    dve.wait_ge(s["rstd_ready"], 2 * p + 2)
                    for tm in range(2):
                        dve.tensor_scalar(tile(p, tm), r[:, tm], mv[:, tm, 0:1], rstd[:, tm:tm + 1],
                                          ALU.subtract, ALU.mult)

                with dve.Fori(0, NP) as p:
                    normed(p)
                    positive(p)
                    coefficients(p)
                    residual(p)


def gated_mlp(nc, glob, w, y):
    with ExitStack() as stack:
        c = Ctx(nc, stack)
        xs = c.sb("i_xs", [P, GT, D])
        xT = c.sb("i_xT", [P, KD, GW])
        wab = c.sb("i_wab", [P, 2, KD, HID])
        wh = c.sb("i_wh", [P, 2, KH, HID])
        w3 = c.sb("i_w3", [P, KH, D])
        sc = c.sb("i_sc", [P, 4, KH])
        s3 = c.sb("i_s3", [P, D])
        sg = c.sb("i_sg", [P, 2, 512])
        h = c.sb("i_h", [P, 2, KH, GW])
        r = c.sb("i_r", [P, GT, D])
        st6 = c.sb("i_st6", [P, GT, 6])
        mv = c.sb("i_mv", [P, GT, 2])
        rstd = c.sb("i_rstd", [P, GT])
        tb = c.ps("i_tb", [P, 2, 512])
        hb = c.ps("i_hb", [P, 4, 512])
        acc = c.ps("i_acc", [P, 2, 512])
        names = ["loaded", "xs_ready", "tb_ready", "tb_done", "ab_ready", "sg_ready", "ab_done", "h_ready",
                 "h_done", "acc_ready", "acc_done", "mv_ready", "rstd_ready", "y_ready", "stored"]
        s = dict(zip(names, c.sems(*["i_" + n for n in names])))
        X, ident = glob["X"], glob["ident"]
        NL = 16 * 7
        with nc.Block() as block:
            @block.sync
            def _(sp):
                for i, name in enumerate(("w1T", "w2T")):
                    sp.dma_start(wab[:, i], w[name].rearrange("(k p) n -> p k n", p=P)).then_inc(s["loaded"], 16)
                for i, name in enumerate(("h1T", "h2T")):
                    sp.dma_start(wh[:, i], w[name].rearrange("(k p) n -> p k n", p=P)).then_inc(s["loaded"], 16)
                sp.dma_start(w3[:], w["w3T"].rearrange("(k p) n -> p k n", p=P)).then_inc(s["loaded"], 16)
                sp.dma_start(sc[:], w["scales"]).then_inc(s["loaded"], 16)
                sp.dma_start(s3[:], w["w3_s"].to_broadcast([P, D])).then_inc(s["loaded"], 16)
                with sp.Fori(0, G) as g:
                    sp.wait_ge(s["y_ready"], g + 1)
                    sp.dma_start(y.rearrange("(t p) d -> p t d", p=P)[:, ds(g * GT, GT), :],
                                 X[:, ds(g * GT, GT), :]).then_inc(s["stored"], 16)
                sp.wait_ge(s["stored"], 16 * G)

            @block.gpsimd
            def _(pool):
                with pool.Fori(0, G) as g:
                    stage_group(pool, s, g, xs, X)
                    rstd_group(pool, s, g + 1, mv, rstd, glob, GT)

            @block.tensor
            def _(pe):
                pe.wait_ge(s["loaded"], NL)
                with pe.Fori(0, G) as g:
                    turn_group(pe, s, g, xs, tb, ident)
                    pe.wait_ge(s["tb_done"], 2 * g + 2)
                    for m in range(KH):
                        pe.wait_ge(s["ab_done"], ring(KH, g, m, 2))
                        for i in range(2):
                            for k in range(KD):
                                mm = pe.matmul(hb[:, 2 * (m % 2) + i], wab[:, i, k, m * P:m * P + P], xT[:, k],
                                               start=k == 0, stop=k == KD - 1)
                        mm.then_inc(s["ab_ready"], 1)
                    for layer in range(2):
                        if layer == 0:
                            pe.wait_ge(s["ab_done"], KH * (g + 1))
                        else:
                            pe.wait_ge(s["h_done"], 2 * KH * g + KH)
                        for m in range(KH):
                            pe.wait_ge(s["h_done"], ring(2 * KH, g, KH * layer + m, 4))
                            for k in range(KH):
                                mm = pe.matmul(hb[:, m % 4], wh[:, layer, k, m * P:m * P + P], h[:, layer, k],
                                               start=k == 0, stop=k == KH - 1)
                            mm.then_inc(s["h_ready"], 1)
                    pe.wait_ge(s["h_done"], 2 * KH * (g + 1))
                    for st in range(GT):
                        pe.wait_ge(s["acc_done"], ring(GT, g, st, 2))
                        for k in range(KH):
                            mm = pe.matmul(acc[:, st % 2, 0:D], h[:, 0, k, st * P:st * P + P], w3[:, k],
                                           start=k == 0, stop=k == KH - 1)
                        mm.then_inc(s["acc_ready"], 1)

            @block.scalar
            def _(act):
                act.wait_ge(s["loaded"], NL)
                with act.Fori(0, G) as g:
                    for k in range(KD):
                        act.wait_ge(s["tb_ready"], KD * g + k + 1)
                        act.copy(xT[:, k], tb[:, k]).then_inc(s["tb_done"], 1)
                    for m in range(KH):
                        act.wait_ge(s["ab_ready"], KH * g + m + 1)
                        act.wait_ge(s["ab_done"], ring(KH, g, m, 2))
                        act.activation(sg[:, m % 2], hb[:, 2 * (m % 2)], ACT.Silu, scale=sc[:, 0, m:m + 1])\
                           .then_inc(s["sg_ready"], 1)
                    for layer in range(2):
                        for m in range(KH):
                            act.wait_ge(s["h_ready"], 2 * KH * g + KH * layer + m + 1)
                            act.activation(h[:, 1 - layer, m], hb[:, m % 4], ACT.Gelu,
                                           scale=sc[:, 2 + layer, m:m + 1]).then_inc(s["h_done"], 1)

            @block.vector
            def _(dve):
                dve.wait_ge(s["loaded"], NL)
                with dve.Fori(0, G) as g:
                    for m in range(KH):
                        dve.wait_ge(s["sg_ready"], KH * g + m + 1)
                        dve.scalar_tensor_tensor(out=h[:, 0, m], in0=hb[:, 2 * (m % 2) + 1],
                                                 scalar=sc[:, 1, m:m + 1], in1=sg[:, m % 2], op0=ALU.mult,
                                                 op1=ALU.mult).then_inc(s["ab_done"], 1)
                    dve.drain()
                    for st in range(GT):
                        dve.wait_ge(s["acc_ready"], GT * g + st + 1)
                        dve.tensor_tensor(r[:, st], acc[:, st % 2, 0:D], s3[:], ALU.mult)\
                           .then_inc(s["acc_done"], 1)
                    dve.drain()
                    dve.tensor_tensor(r[:], r[:], X[:, ds(g * GT, GT), :], ALU.add)
                    stats(dve, s, lambda i: r[:, i], st6, mv, GT)
                    dve.wait_ge(s["rstd_ready"], g + 1)
                    for st in range(GT):
                        a = dve.tensor_scalar(X[:, ds(g * GT + st, 1), :].rearrange("p a d -> p (a d)"), r[:, st],
                                              mv[:, st, 0:1], rstd[:, st:st + 1], ALU.subtract, ALU.mult)
                    a.then_inc(s["y_ready"], 1)


def decoder(nc, a, y, scr):
    with ExitStack() as stack:
        c = Ctx(nc, stack)
        glob = {"X": c.sb("X", [P, NT, D]), "ident": c.sb("ident", [P, P]), "mhalf": c.sb("mhalf", [P, 1]),
                "eps": c.sb("eps", [P, 1])}
        glob["x_loaded"], = c.sems("x_loaded")
        with ExitStack() as att:
            ca = Ctx(nc, att)
            glob["ATT"] = ca.sb("ATT", [P, NT, D])
            glob["V"] = ca.sb("V", [P, NT, NH, HD + 1])
            self_attention_qkv(nc, glob, a, scr)
            self_attention_heads(nc, glob, scr)
            attention_out(nc, glob, a)
        cross_attention(nc, glob, a, scr, True)
        mixture_of_experts(nc, glob, a)
        delta_rule(nc, glob, a)
        cross_attention(nc, glob, a, scr, False)
        gated_mlp(nc, glob, a, y)


def layouts(i, np):
    def t(a):
        return np.ascontiguousarray(a.T)

    def cols(v, k):
        return np.ascontiguousarray(v.reshape(k, P).T)

    o = {}
    x = i["x"].reshape(T, D)
    o["x"] = x
    o["xT"] = t(x)
    o["ctxT"] = np.ascontiguousarray(i["ctx_1024"].reshape(B * S, D).T)
    o["w1"] = np.stack([i[f"L0_attn_{q}_w1"] for q in "qkv"])
    o["w2"] = np.stack([i[f"L0_attn_{q}_w2"] for q in "qkv"])
    o["b1"] = np.stack([cols(i[f"L0_attn_{q}_b1"], KH) for q in "qkv"])
    o["b2qk"] = np.stack([cols(i[f"L0_attn_{q}_b2"], KD) for q in "qk"], axis=1)
    o["b2v"] = i["L0_attn_v_b2"].reshape(1, D)
    o["proj_w"] = i["L0_attn_proj_w"]
    o["proj_b"] = i["L0_attn_proj_b"].reshape(1, D)
    o["WkT"], o["WvT"] = t(i["L0_xattn_Wk"]), t(i["L0_xattn_Wv"])
    order = [8 * (rt // 4) + rt % 4 + 4 * half for rt in range(KH) for half in range(2)]
    o["WqR"] = np.ascontiguousarray(i["L0_xattn_Wq"].reshape(NH, 64, D)[order].reshape(HID, D))
    o["WoR"] = np.ascontiguousarray(i["L0_xattn_Wo"].T.reshape(NH, 64, D)[order].reshape(HID, D))
    o["gate_wT"] = t(i["L0_ffn_gate_w"])
    shared = [np.ascontiguousarray(i[f"L0_ffn_sw_{n}"].reshape(D, 2, F).transpose(1, 0, 2)) for n in ("gate", "up")]
    o["w_gu"] = np.ascontiguousarray(np.stack([np.concatenate([i["L0_ffn_w_gate"], shared[0]]),
                                               np.concatenate([i["L0_ffn_w_up"], shared[1]])], axis=1))
    o["w_dn"] = np.concatenate([i["L0_ffn_w_down"], i["L0_ffn_sw_down"].reshape(2, F, D)])
    o["ln_w"], o["ln_b"] = i["L1_attn_ln_w"].reshape(1, D), i["L1_attn_ln_b"].reshape(1, D)
    ws = i["L1_attn_w_slow"].reshape(D, NH, 3 * 64 + 1)
    o["w_slow"] = np.concatenate([np.ascontiguousarray(ws[:, :, 64 * j:64 * j + 64]).reshape(D, HID)
                                  for j in range(3)] + [np.ascontiguousarray(ws[:, :, 192])], axis=1)
    o["w_out"] = i["L1_attn_w_out"]
    o["WcT"] = t(i["L1_xattn_w_concat"])
    for n in ("w1", "w2", "h1", "h2", "w3"):
        o[n + "T"] = t(i[f"L1_ffn_{n}_w"])
    o["scales"] = np.stack([cols(i[f"L1_ffn_{n}_s"], KH) for n in ("w1", "w2", "h1", "h2")], axis=1)
    o["w3_s"] = i["L1_ffn_w3_s"].reshape(1, D)
    return o


def kernel(**inputs):
    import numpy as _np
    import concourse.bacc as _bacc
    from concourse import mybir as _mybir
    from concourse.bass_utils import run_bass_kernel_spmd as _run

    nc = _bacc.Bacc("TRN2", target_bir_lowering=False, num_devices=1)
    laid = layouts({k: _np.asarray(v) for k, v in inputs.items()}, _np)
    arrays, args = {}, {}
    for name, a in laid.items():
        a = _np.ascontiguousarray(a)
        arrays[f"in_{name}_dram"] = a
        args[name] = nc.dram_tensor(f"in_{name}_dram", a.shape, _mybir.dt.from_np(a.dtype),
                                    kind="ExternalInput").ap()
    y = nc.dram_tensor("out_0_dram", (T, D), _mybir.dt.float32, kind="ExternalOutput").ap()
    scr = {"qk": nc.dram_tensor("scr_qk", (2, 2, B * D, N), _mybir.dt.float32, kind="Internal").ap(),
           "vals": nc.dram_tensor("scr_vals", (B, FL, D), _mybir.dt.float32, kind="Internal").ap()}
    decoder(nc, args, y, scr)
    r = _run(nc, [arrays], core_ids=[0])
    return r.results[0]["out_0_dram"].reshape(B, N, D)
```

```python
from contextlib import ExitStack

import concourse.bass as bass
from concourse import mybir

F32 = mybir.dt.float32
F32R = mybir.dt.float32r
U32 = mybir.dt.uint32
ALU = mybir.AluOpType
ACT = mybir.ActivationFunctionType
AX = mybir.AxisListType
P = 128
B, N, D = 2, 1024, 256
T = B * N
NT = T // P
KD = D // P
G = 4
GT = NT // G
GW = T // G
NH = 16
HD = D // NH
HID = 1024
KH = HID // P
S = 77
FL = NH * S
FB = -(-FL // P)
E, F = 8, 352
NE = E + 2
EPS = 1e-5
ds = bass.ds
NAB, NWH, NW3 = 2 * KD * HID, 2 * KH * HID, KH * D
NW = NAB + NWH + NW3
WCH = NW // NT
FULL_BITS = (1 << 12) - 1


class Ctx:

    def __init__(self, nc, stack):
        self.nc, self.stack = nc, stack

    def sb(self, name, shape, dt=F32):
        return self.stack.enter_context(self.nc.sbuf_tensor(name, shape, dt))

    def ps(self, name, shape, dt=F32):
        return self.stack.enter_context(self.nc.psum_tensor(name, shape, dt))

    def sems(self, *names):
        return [self.stack.enter_context(self.nc.semaphore(n)) for n in names]


def ring(per_loop, i, j, depth):
    return per_loop * i + max(0, j - depth + 1)


def self_attention_qkv(nc, glob, w, scr):
    with ExitStack() as stack:
        c = Ctx(nc, stack)
        xT = c.sb("qkv_xT", [P, KD, T])
        w1 = c.sb("qkv_w1", [P, 3, KD, HID])
        w2 = c.sb("qkv_w2", [P, 3, KH, D])
        b1 = c.sb("qkv_b1", [P, 3, KH])
        b2 = c.sb("qkv_b2", [P, 2, KD])
        b2v = c.sb("qkv_b2v", [P, D])
        hid = c.sb("qkv_hid", [P, 3, KH, GW])
        full = c.sb("qkv_full", [P, GW])
        parts = c.sb("qkv_parts", [P, 2, 2, GW], F32R)
        hb = c.ps("qkv_hb", [P, 4, 512])
        ob = c.ps("qkv_ob", [P, 2, 512])
        loaded, h_ready, h_done, o_ready, o_done, parts_ready, st0, st1 = c.sems(
            "a_loaded", "a_h_ready", "a_h_done", "a_o_ready", "a_o_done", "a_parts_ready", "a_st0", "a_st1")
        stored = [st0, st1]
        V = glob["V"]
        NLOAD = 16 * 12
        with nc.Block() as block:
            @block.sync
            def _(sp):
                sp.dma_start(xT[:], w["xT"].rearrange("(k p) t -> p k t", p=P)).then_inc(loaded, 16)
                for br in range(3):
                    sp.dma_start(w1[:, br], w["w1"][br].rearrange("(k p) n -> p k n", p=P)).then_inc(loaded, 16)
                    sp.dma_start(w2[:, br], w["w2"][br].rearrange("(k p) n -> p k n", p=P)).then_inc(loaded, 16)
                    sp.dma_start(b1[:, br], w["b1"][br]).then_inc(loaded, 16)
                sp.dma_start(b2[:], w["b2qk"]).then_inc(loaded, 16)
                sp.dma_start(b2v[:], w["b2v"].to_broadcast([P, D])).then_inc(loaded, 16)
                sp.dma_start(glob["X"][:], w["x"].rearrange("(t p) d -> p t d", p=P)).then_inc(glob["x_loaded"], 16)
                with sp.Fori(0, B) as b:
                    for half in range(2):
                        for j in range(4):
                            br, mt = j // 2, j % 2
                            sp.wait_ge(parts_ready, 8 * b + 4 * half + j + 1)
                            sp.dma_start(
                                scr["qk"][br, :, ds(b * D + mt * P, P), half * 512:half * 512 + 512]
                                .rearrange("l r n -> r l n"), parts[:, j % 2].bitcast(F32)).then_inc(stored[j % 2], 16)
                for q in stored:
                    sp.wait_ge(q, 16 * 2 * G)
                sp.wait_ge(glob["x_loaded"], 16)

            @block.tensor
            def _(pe):
                pe.wait_ge(loaded, NLOAD)
                with pe.Fori(0, G) as t:
                    def up(br):
                        for m in range(KH):
                            j = br * KH + m
                            pe.wait_ge(h_done, ring(3 * KH, t, j, 4))
                            for k in range(KD):
                                mm = pe.matmul(hb[:, j % 4], w1[:, br, k, m * P:m * P + P],
                                               xT[:, k, ds(t * GW, GW)], start=k == 0, stop=k == KD - 1)
                            mm.then_inc(h_ready, 1)

                    def down(br):
                        pe.wait_ge(h_done, 3 * KH * t + (br + 1) * KH)
                        for u in range(2 if br < 2 else GT):
                            j = 2 * br + u
                            pe.wait_ge(o_done, ring(8, t, j, 2))
                            for k in range(KH):
                                if br < 2:
                                    mm = pe.matmul(ob[:, j % 2], w2[:, br, k, u * P:u * P + P],
                                                   hid[:, br, k], start=k == 0, stop=k == KH - 1)
                                else:
                                    mm = pe.matmul(ob[:, j % 2, 0:D], hid[:, br, k, u * P:u * P + P],
                                                   w2[:, br, k], start=k == 0, stop=k == KH - 1)
                            mm.then_inc(o_ready, 1)

                    up(0)
                    up(1)
                    down(0)
                    up(2)
                    down(1)
                    down(2)

            @block.scalar
            def _(act):
                act.wait_ge(loaded, NLOAD)
                with act.Fori(0, G) as t:
                    for j in range(3 * KH):
                        br, m = j // KH, j % KH
                        act.wait_ge(h_ready, 3 * KH * t + j + 1)
                        act.activation(hid[:, br, m], hb[:, j % 4], ACT.Gelu,
                                       bias=b1[:, br, m:m + 1]).then_inc(h_done, 1)

            @block.vector
            def _(dve):
                dve.memset(V[:, :, :, HD:HD + 1], 1.0)
                dve.wait_ge(loaded, NLOAD)
                with dve.Fori(0, G) as t:
                    for j in range(8):
                        if j < 4:
                            br, mt = j // 2, j % 2
                            dve.drain()
                            dve.wait_ge(o_ready, 8 * t + j + 1)
                            dve.tensor_scalar(full[:], ob[:, j % 2], b2[:, br, mt:mt + 1], None,
                                              ALU.add).then_inc(o_done, 1)
                            dve.drain()
                            dve.wait_ge(stored[j % 2], 16 * (2 * t + j // 2))
                            dve.tensor_copy(parts[:, j % 2, 0], full[:])
                            dve.drain()
                            dve.tensor_tensor(parts[:, j % 2, 1], full[:], parts[:, j % 2, 0].bitcast(F32),
                                              ALU.subtract).then_inc(parts_ready, 1)
                        else:
                            dve.wait_ge(o_ready, 8 * t + j + 1)
                            v = V[:, ds(t // 2 * NH, NH), ds(t % 2 * GT + j - 4, 1), 0:HD].rearrange("p h a d -> p (h a) d")
                            dve.tensor_tensor(v, ob[:, j % 2, 0:D].rearrange("p (h d) -> p h d", h=NH),
                                              b2v[:].rearrange("p (h d) -> p h d", h=NH),
                                              ALU.add).then_inc(o_done, 1)

            @block.gpsimd
            def _(pool):
                pool.memset(glob["ident"][:], 0.0)
                pool.drain()
                pool.affine_select(out=glob["ident"][:], in_=glob["ident"][:], compare_op=ALU.not_equal,
                                   fill=1.0, base=0, pattern=[[-1, P]], channel_multiplier=1)
                pool.memset(glob["mhalf"][:], -0.5)
                pool.memset(glob["eps"][:], EPS)


def self_attention_heads(nc, glob, scr):
    NQ = N // P
    VR = 66
    VC = HD + 1
    SB = 3
    LAG = 4
    LEAD = 8
    KR = 4 * HD + 2
    NLD = 16 * 9
    with ExitStack() as stack:
        c = Ctx(nc, stack)
        qs = c.sb("at_qs", [KR, SB, N], F32R)
        ks = c.sb("at_ks", [KR, SB, N], F32R)
        zero = c.sb("at_zero", [2, N], F32R)
        vs = c.sb("at_vs", [P, SB, NQ - 1, VR], F32R)
        vs7 = c.sb("at_vs7", [P, SB, VR])
        pfull = c.sb("at_pfull", [P, NQ - 1, 512])
        pfull7 = c.sb("at_pfull7", [P, 2, 512])
        phi = c.sb("at_phi", [P, 2, NQ - 1, 512], F32R)
        plo = c.sb("at_plo", [P, 2, NQ - 1, 512], F32R)
        olo = c.sb("at_olo", [P, NQ, VC])
        osum = c.sb("at_osum", [P, NQ, VC])
        mx = c.sb("at_mx", [P, SB, NQ, 2])
        nm = c.sb("at_nm", [P, NQ])
        nmp = c.sb("at_nmp", [NQ, 2, P], F32R)
        outT = c.sb("at_outT", [2 * VC, 2, 512])
        rc = c.sb("at_rc", [P, NQ, 1])
        s1 = c.ps("at_s1", [P, SB, 512])
        s2 = c.ps("at_s2", [P, 2, 512])
        pv = c.ps("at_pv", [P, 2, 512])
        turned = c.ps("at_turned", [P, 512])
        ld = c.sems(*[f"b_ld{i}" for i in range(SB)])
        mrow = c.sems(*[f"b_mrow{i}" for i in range(SB)])
        (s1_ready, s1_done, s2_ready, p_ready, v_ready, pv_ready, out_ready, to_ready,
         to_done, nm_ready, tm_ready, nmp_ready, const_ready, lo_pool, lo_dve) = c.sems(
            "b_s1_ready", "b_s1_done", "b_s2_ready", "b_p_ready",
            "b_v_ready", "b_pv_ready", "b_out_ready", "b_to_ready", "b_to_done", "b_nm_ready", "b_tm_ready",
            "b_nmp_ready", "b_const_ready", "b_lo_pool", "b_lo_dve")
        V, ATT, ident = glob["V"], glob["ATT"], glob["ident"]
        NB = B * NH

        to = turned[:, 0:NQ * 2 * VC].rearrange("p (k c) -> p k c", c=2 * VC)
        tm = turned[0:NQ, NQ * 2 * VC:NQ * 2 * VC + P]

        def heads(eng, one):
            one((0, 0, 0))
            with eng.Fori(0, (NB - 3) // SB) as i:
                for k in range(1, SB + 1):
                    one((SB * i + k, k % SB, i + k // SB))
            for n in range(1 + (NB - 3) // SB * SB, NB):
                one((n, n % SB, n // SB))

        def after(h, d):
            n, q, r = h
            if isinstance(n, int) and n + d >= NB:
                return None
            return n + d, (q + d) % SB, r + (q + d) // SB

        def first(h):
            return isinstance(h[0], int) and h[0] == 0

        def row_at(h, s):
            a = after(h, 1 + (s + LEAD) // 16)
            return (a, (s + LEAD) % 16) if a else None

        with nc.Block() as block:
            @block.sync
            def _(sp):
                sp.wait_ge(const_ready, 1)

                def load(n, p):
                    for part in range(2):
                        for k in (part, part + 2):
                            sp.dma_start(qs[k * HD:(k + 1) * HD, p].bitcast(F32),
                                         scr["qk"][0, part, ds(n * HD, HD), :]).then_inc(ld[p], 16)
                        for k in (2 * part, 2 * part + 1):
                            sp.dma_start(ks[k * HD:(k + 1) * HD, p].bitcast(F32),
                                         scr["qk"][1, part, ds(n * HD, HD), :]).then_inc(ld[p], 16)
                    sp.dma_start(qs[4 * HD:KR, p].bitcast(F32), zero[:].bitcast(F32)).then_inc(ld[p], 16)

                def maxima(n, p):
                    sp.wait_ge(nmp_ready, n + 1)
                    for part in range(2):
                        sp.dma_start(qs[4 * HD + part:4 * HD + part + 1, p].bitcast(F32)
                                     .rearrange("a (q r) -> a q r", r=P), nmp[:, part, :].bitcast(F32)).then_inc(mrow[p], 16)

                def one(n, q):
                    maxima(n + 1, (q + 1) % SB)
                    sp.wait_ge(s2_ready, 16 * (n + 1))
                    load(n + SB, q)

                for n in range(SB):
                    load(n, n)
                maxima(0, 0)
                with sp.Fori(0, (NB - SB) // SB) as i:
                    for q in range(SB):
                        one(SB * i + q, q)
                for n in range((NB - SB) // SB * SB, NB - SB):
                    one(n, n % SB)
                for n in range(NB - SB, NB - 1):
                    maxima(n + 1, (n + 1) % SB)

            @block.tensor
            def _(pe):
                pe.wait_ge(const_ready, 1)

                def score_rows(h, u):
                    n, q, r = h
                    qt, kh, bank = u // 2, u % 2, (q + u) % SB
                    if u == 0:
                        pe.wait_ge(ld[q], NLD * (r + 1))
                    if not first(h):
                        pe.wait_ge(s1_done, 16 * n + u - SB + 1)
                    elif u >= SB:
                        pe.wait_ge(s1_done, u - SB + 1)
                    pe.matmul(s1[:, bank], qs[:, q, qt * P:qt * P + P], ks[:, q, kh * 512:kh * 512 + 512],
                              start=True, stop=True).then_inc(s1_ready, 1)

                def score_cols(h, s):
                    n, q, r = h
                    qh, kt = s // NQ, s % NQ
                    if s == 0:
                        pe.wait_ge(mrow[q], 32 * (r + 1))
                    if not first(h):
                        pe.wait_ge(p_ready, 16 * n + s - 1)
                    elif s >= 2:
                        pe.wait_ge(p_ready, s - 1)
                    pe.matmul(s2[:, s % 2], ks[:, q, kt * P:kt * P + P], qs[:, q, qh * 512:qh * 512 + 512],
                              start=True, stop=True).then_inc(s2_ready, 1)

                def turn_maxima(h):
                    pe.wait_ge(nm_ready, h[0] + 1)
                    if not isinstance(h[0], int) or h[0] > 1:
                        pe.wait_ge(to_done, h[0] - 1)
                    pe.transpose(tm, nm[:], ident[:]).then_inc(tm_ready, 1)

                def may_turn_out(n):
                    pe.wait_ge(out_ready, 2 * n + 2)
                    pe.wait_ge(nmp_ready, NB if isinstance(n, int) and n == NB - 1 else n + 2)

                def turn_out():
                    for k in range(NQ):
                        t = pe.transpose(to[:, k], outT[:, k // 4, k % 4 * P:k % 4 * P + P],
                                         ident[0:2 * VC, 0:2 * VC])
                    t.then_inc(to_ready, 1)

                def values(h, s):
                    n, q, r = h
                    qh, kt = s // NQ, s % NQ
                    pe.wait_ge(p_ready, 16 * n + s + 1)
                    if s == 0:
                        pe.wait_ge(v_ready, n + 1)
                    if kt == 0 and not (first(h) and qh == 0):
                        pe.wait_ge(out_ready, 2 * n + qh - 1)
                    if kt == NQ - 1:
                        pe.matmul(pv[0:VR, qh], vs7[:, q], pfull7[:, qh], start=False, stop=True)\
                          .then_inc(pv_ready, 1)
                    else:
                        pe.matmul(pv[0:VR, qh], vs[:, q, kt], phi[:, qh, kt], start=kt == 0, stop=False)
                        if kt == 0:
                            pe.wait_ge(lo_dve, 2 * n + qh + 1)
                        else:
                            pe.wait_ge(lo_pool, 6 + 12 * n + 6 * qh + kt)
                        pe.matmul(pv[0:VR, qh], vs[:, q, kt], plo[:, qh, kt], start=False, stop=False)

                def one(h):
                    following = after(h, 1)
                    for s in range(LAG, 16 + LAG):
                        if s < 16:
                            score_cols(h, s)
                        elif following:
                            score_cols(following, s - 16)
                        row = row_at(h, s)
                        if row:
                            score_rows(*row)
                        if s == 18 - LEAD and following:
                            turn_maxima(following)
                        if s == 7 and not first(h):
                            may_turn_out(h[0] - 1)
                        values(h, s - LAG)
                        if s == 7 and not first(h):
                            turn_out()

                for u in range(16):
                    score_rows((0, 0, 0), u)
                turn_maxima((0, 0, 0))
                for u in range(LAG + LEAD):
                    score_rows((1, 1, 0), u)
                for u in range(LAG):
                    score_cols((0, 0, 0), u)
                heads(pe, one)
                may_turn_out(NB - 1)
                turn_out()

            @block.scalar
            def _(act):
                act.preload_act_table(ACT.Exp)
                with act.Fori(0, NB) as n:
                    for s in range(16):
                        qh, kt = s // NQ, s % NQ
                        full = pfull7[:, qh] if kt == NQ - 1 else pfull[:, kt]
                        if kt == 0:
                            act.wait_ge(pv_ready, 2 * n + qh)
                            act.wait_ge(lo_dve, 2 * n + qh)
                        elif kt < NQ - 1:
                            act.wait_ge(lo_pool, 12 * n + 6 * qh + kt)
                        act.wait_ge(s2_ready, 16 * n + s + 1)
                        a = act.activation(full, s2[:, s % 2], ACT.Exp, scale=float(HD) ** -0.5)
                        if kt < NQ - 1:
                            a = act.activation(phi[:, qh, kt], s2[:, s % 2], ACT.Exp, scale=float(HD) ** -0.5)
                        a.then_inc(p_ready, 1)

            @block.vector
            def _(dve):
                dve.memset(zero[:].bitcast(mybir.dt.uint32), 0)
                dve.memset(ks[4 * HD:KR].bitcast(F32), 1.0)
                dve.memset(vs[:].bitcast(F32), 0.0)
                dve.drain()
                dve.memset(vs7[:], 0.0).then_inc(const_ready, 1)

                def row_max(h, u):
                    n, q, r = h
                    dve.wait_ge(s1_ready, 16 * n + u + 1)
                    dve.reduce_max(mx[:, q, u // 2, u % 2:u % 2 + 1], s1[:, (q + u) % SB], AX.X)\
                       .then_inc(s1_done, 1)

                def head_max(h):
                    dve.drain()
                    dve.tensor_reduce(nm[:], mx[:, h[1]], AX.X, ALU.max, negate=True).then_inc(nm_ready, 1)

                def split_max(h):
                    n, q, r = h
                    dve.wait_ge(tm_ready, n + 1)
                    if not first(h):
                        dve.wait_ge(mrow[(q - 1) % SB], 32 * (r + (1 if q else 0)))
                    dve.tensor_copy(nmp[:, 0], tm)
                    dve.drain()
                    dve.tensor_tensor(nmp[:, 1], tm, nmp[:, 0].bitcast(F32), ALU.subtract)\
                       .then_inc(nmp_ready, 1)

                def copy_out(n, qh):
                    if not isinstance(n, int) or n:
                        dve.wait_ge(to_ready, n)
                    dve.wait_ge(pv_ready, 2 * n + qh + 2)
                    dve.tensor_copy(outT[:, qh], pv[0:2 * VC, qh]).then_inc(out_ready, 1)

                def normalise(n):
                    dve.wait_ge(to_ready, n + 1)
                    dve.tensor_copy(olo[:], to[:, :, VC:2 * VC])
                    dve.drain()
                    dve.tensor_tensor(osum[:], to[:, :, 0:VC], olo[:], ALU.add).then_inc(to_done, 1)
                    dve.drain()
                    dve.reciprocal(rc[:], osum[:, :, HD:VC])
                    dve.drain()
                    dve.tensor_tensor(ATT[:, ds(n, 1)].rearrange("p a k d -> p (a k) d"),
                                      osum[:, :, 0:HD], rc[:].to_broadcast([P, NQ, HD]), ALU.mult)

                def low_part(h, qh):
                    dve.wait_ge(p_ready, 16 * h[0] + NQ * qh + 1)
                    dve.tensor_tensor(plo[:, qh, 0], pfull[:, 0], phi[:, qh, 0].bitcast(F32), ALU.subtract)\
                       .then_inc(lo_dve, 1)

                def take_v(h):
                    n, q, r = h
                    if not (isinstance(n, int) and n < SB):
                        dve.wait_ge(pv_ready, 2 * (n - SB) + 3)
                    v = V[:, ds(n, 1)].rearrange("p a k d -> p (a k) d")
                    dve.tensor_copy(vs[:, q, :, 0:VC], v[:, 0:NQ - 1])
                    dve.tensor_copy(vs7[:, q, 0:VC], v[:, NQ - 1])
                    dve.drain()
                    dve.tensor_tensor(vs[:, q, :, VC:2 * VC], v[:, 0:NQ - 1],
                                      vs[:, q, :, 0:VC].bitcast(F32), ALU.subtract).then_inc(v_ready, 1)

                def one(h):
                    following = after(h, 1)
                    for s in range(LAG, 16 + LAG):
                        if s == 5 and not first(h):
                            copy_out(h[0] - 1, 1)
                        if s == 9 and not first(h):
                            normalise(h[0] - 1)
                        if s == 10:
                            low_part(h, 1)
                        if s == 13:
                            copy_out(h[0], 0)
                        if following:
                            if s == 16 - LEAD:
                                head_max(following)
                            if s == 19 - LEAD:
                                split_max(following)
                            if s == 15:
                                take_v(following)
                            if s == 18:
                                low_part(following, 0)
                        row = row_at(h, s)
                        if row:
                            row_max(*row)

                for u in range(16):
                    row_max((0, 0, 0), u)
                head_max((0, 0, 0))
                take_v((0, 0, 0))
                split_max((0, 0, 0))
                for u in range(LAG + LEAD):
                    row_max((1, 1, 0), u)
                low_part((0, 0, 0), 0)
                heads(dve, one)
                copy_out(NB - 1, 1)
                normalise(NB - 1)

            @block.gpsimd
            def _(pool):
                pool.sem_inc(lo_pool, 6)
                pool.sem_inc(pv_ready, 1)
                with pool.Fori(0, NB) as n:
                    for qh in range(2):
                        for kt in range(1, NQ - 1):
                            pool.wait_ge(p_ready, 16 * n + NQ * qh + kt + 1)
                            pool.tensor_tensor(plo[:, qh, kt], pfull[:, kt], phi[:, qh, kt].bitcast(F32),
                                               ALU.subtract).then_inc(lo_pool, 1)


def turn_group(pe, s, g, xs, tb, ident, used=0, per=2):
    pe.wait_ge(s["xs_ready"], g + 1)
    for k in range(KD):
        pe.wait_ge(s["tb_done"], ring(per, g, k, 2))
        for st in range(GT):
            t = pe.transpose(tb[:, k, st * P:st * P + P], xs[:, st, k * P:k * P + P], ident[:])
        t.then_inc(s["tb_ready"], 1)


def stage_group(pool, s, g, xs, src, per=2):
    pool.wait_ge(s["tb_ready"], per * g)
    pool.tensor_copy(xs[:], src[:, ds(g * GT, GT), :]).then_inc(s["xs_ready"], 1)


def rstd_group(pool, s, n, mv, rstd, glob, k):
    eps, mhalf = glob["eps"], glob["mhalf"]
    pool.wait_ge(s["mv_ready"], n)
    pool.tensor_tensor(rstd[:], mv[:, :, 1], eps[:].to_broadcast([P, k]), ALU.add)
    pool.drain()
    pool.tensor_tensor(rstd[:], rstd[:], mhalf[:].to_broadcast([P, k]), ALU.pow).then_inc(s["rstd_ready"], 1)


def stats(dve, s, r, st6, mv, k):
    dve.drain()
    for i in range(k):
        dve.bn_stats(st6[:, i], r(i))
    dve.drain()
    for i in range(k):
        a = dve.bn_aggr(mv[:, i], st6[:, i])
    a.then_inc(s["mv_ready"], 1)


def attention_out(nc, glob, w):
    with ExitStack() as stack:
        c = Ctx(nc, stack)
        xs = c.sb("c_xs", [P, GT, D])
        xT = c.sb("c_xT", [P, KD, GW])
        pw = c.sb("c_pw", [P, KD, D])
        pb = c.sb("c_pb", [P, D])
        r = c.sb("c_r", [P, GT, D])
        st6 = c.sb("c_st6", [P, GT, 6])
        mv = c.sb("c_mv", [P, GT, 2])
        rstd = c.sb("c_rstd", [P, GT])
        tb = c.ps("c_tb", [P, 2, 512])
        acc = c.ps("c_acc", [P, 4, 512])
        names = ["loaded", "xs_ready", "tb_ready", "tb_done", "acc_ready", "acc_done", "mv_ready", "rstd_ready"]
        s = dict(zip(names, c.sems(*["c_" + n for n in names])))
        X, ident = glob["X"], glob["ident"]
        with nc.Block() as block:
            @block.sync
            def _(sp):
                sp.dma_start(pw[:], w["proj_w"].rearrange("(k p) n -> p k n", p=P)).then_inc(s["loaded"], 16)
                sp.dma_start(pb[:], w["proj_b"].to_broadcast([P, D])).then_inc(s["loaded"], 16)

            @block.gpsimd
            def _(pool):
                with pool.Fori(0, G) as g:
                    pool.wait_ge(s["tb_ready"], KD * g)
                    for st in range(GT):
                        a = pool.tensor_copy(xs[:, st].rearrange("p (h d) -> p h d", d=HD),
                                             glob["ATT"][:, ds(g // 2 * NH, NH), ds(g % 2 * GT + st, 1)]
                                             .rearrange("p h a d -> p (h a) d"))
                    a.then_inc(s["xs_ready"], 1)
                    rstd_group(pool, s, g + 1, mv, rstd, glob, GT)

            @block.tensor
            def _(pe):
                pe.wait_ge(s["loaded"], 32)
                with pe.Fori(0, G) as g:
                    turn_group(pe, s, g, xs, tb, ident)
                    pe.wait_ge(s["tb_done"], 2 * g + 2)
                    for st in range(GT):
                        pe.wait_ge(s["acc_done"], GT * g)
                        for k in range(KD):
                            mm = pe.matmul(acc[:, st, 0:D], xT[:, k, st * P:st * P + P], pw[:, k],
                                           start=k == 0, stop=k == KD - 1)
                        mm.then_inc(s["acc_ready"], 1)

            @block.scalar
            def _(act):
                with act.Fori(0, G) as g:
                    for k in range(KD):
                        act.wait_ge(s["tb_ready"], KD * g + k + 1)
                        act.copy(xT[:, k], tb[:, k]).then_inc(s["tb_done"], 1)

            @block.vector
            def _(dve):
                dve.wait_ge(s["loaded"], 32)
                with dve.Fori(0, G) as g:
                    dve.drain()
                    for st in range(GT):
                        dve.wait_ge(s["acc_ready"], GT * g + st + 1)
                        dve.tensor_tensor(r[:, st], acc[:, st, 0:D], pb[:], ALU.add).then_inc(s["acc_done"], 1)
                    dve.drain()
                    dve.tensor_tensor(r[:], r[:], X[:, ds(g * GT, GT), :], ALU.add)
                    stats(dve, s, lambda i: r[:, i], st6, mv, GT)
                    dve.wait_ge(s["rstd_ready"], g + 1)
                    for st in range(GT):
                        dve.tensor_scalar(X[:, ds(g * GT + st, 1), :].rearrange("p a d -> p (a d)"), r[:, st],
                                          mv[:, st, 0:1], rstd[:, st:st + 1], ALU.subtract, ALU.mult)


def mlp_weights(tile):
    return (tile[:, 0:NAB].rearrange("p (i k n) -> p i k n", i=2, k=KD),
            tile[:, NAB:NAB + NWH].rearrange("p (i k n) -> p i k n", i=2, k=KH),
            tile[:, NAB + NWH:NW].rearrange("p (k n) -> p k n", k=KH))


def load_mlp_weights(pool, glob, w):
    wab, wh, w3 = mlp_weights(glob["mlp_w"])
    for dst, name in ((wab[:, 0], "w1T"), (wab[:, 1], "w2T"), (wh[:, 0], "h1T"), (wh[:, 1], "h2T"), (w3, "w3T")):
        pool.dma_start(dst, w[name].rearrange("(k p) n -> p k n", p=P)).then_inc(glob["mlp_loaded"], 16)


def cross_attention(nc, glob, w, scr, first):
    tag = "e" if first else "h"
    scale = 64.0 ** -0.5 if first else float(HD) ** -0.5
    with ExitStack() as stack:
        c = Ctx(nc, stack)
        keys = c.sb(tag + "_keys", [P, B, KD, FL])
        vals = c.sb(tag + "_vals", [P, B, FB, D])
        X, ident = glob["X"], glob["ident"]
        BS = B * S
        LAST = FL - (FB - 1) * P

        with ExitStack() as inner:
            d = Ctx(nc, inner)
            cT = d.sb(tag + "_cT", [P, KD, BS])
            loaded, kv_ready, kv_done, m_ready, m_done, o_ready, o_done, stored, back, zeroed = d.sems(
                *[tag + "p_" + n for n in ("loaded", "kv_ready", "kv_done", "m_ready", "m_done", "o_ready",
                                           "o_done", "stored", "back", "zeroed")])
            if first:
                wk = d.sb("e_wk", [P, KD, D])
                wv = d.sb("e_wv", [P, KD, D])
                wq = d.sb("e_wq", [P, KH, D])
                wo = d.sb("e_wo", [P, KH, D])
                kvT = d.sb("e_kvT", [P, 2, KD, BS])
                vstage = d.sb("e_vstage", [S, B, NH, D])
                kvb = d.ps("e_kvb", [P, 2, 512])
                mb = d.ps("e_mb", [P, 2, 512])
                vb = d.ps("e_vb", [P, 4, 512])
                def head(rt, half):
                    return 8 * (rt // 4) + rt % 4 + 4 * half
                with nc.Block() as block:
                    @block.sync
                    def _(sp):
                        sp.dma_start(cT[:], w["ctxT"].rearrange("(k p) n -> p k n", p=P)).then_inc(loaded, 16)
                        for dst, name in ((wk, "WkT"), (wv, "WvT"), (wq, "WqR"), (wo, "WoR")):
                            sp.dma_start(dst[:], w[name].rearrange("(k p) n -> p k n", p=P)).then_inc(loaded, 16)
                        sp.wait_ge(o_done, 2 * KH)
                        sp.dma_start(scr["vals"].rearrange("b (h s) d -> s b h d", s=S), vstage[:])\
                          .then_inc(stored, 16)
                        sp.wait_ge(stored, 16)
                        for b in range(B):
                            sp.dma_start(vals[:, b, 0:FB - 1], scr["vals"][b, 0:(FB - 1) * P]
                                         .rearrange("(k p) d -> p k d", p=P)).then_inc(back, 16)
                            sp.dma_start(vals[0:LAST, b, FB - 1], scr["vals"][b, (FB - 1) * P:FL])\
                              .then_inc(back, 16)
                        sp.wait_ge(back, 64)

                    @block.tensor
                    def _(pe):
                        pe.wait_ge(loaded, 80)
                        for kv, wt in enumerate((wk, wv)):
                            for mt in range(KD):
                                for k in range(KD):
                                    mm = pe.matmul(kvb[:, kv, mt * BS:(mt + 1) * BS], wt[:, k, mt * P:mt * P + P],
                                                   cT[:, k], start=k == 0, stop=k == KD - 1)
                            mm.then_inc(kv_ready, 1)
                        pe.wait_ge(kv_done, 2)
                        for rt in range(KH):
                            for half in range(2):
                                rows = slice(64 * half, 64 * half + 64)
                                tile = head(rt, half) // 8
                                j = 2 * rt + half
                                if j >= 2:
                                    pe.wait_ge(m_done, j - 1)
                                for k in range(KD):
                                    mm = pe.matmul(mb[:, half, k * BS:(k + 1) * BS], wq[rows, rt, k * P:k * P + P],
                                                   kvT[rows, 0, tile], start=True, stop=True)
                                mm.then_inc(m_ready, 1)
                                if j >= 4:
                                    pe.wait_ge(o_done, j - 3)
                                for b in range(B):
                                    mm = pe.matmul(vb[0:S, 2 * (rt % 2) + half, b * D:(b + 1) * D],
                                                   kvT[rows, 1, tile, b * S:(b + 1) * S], wo[rows, rt],
                                                   start=True, stop=True)
                                mm.then_inc(o_ready, 1)

                    @block.vector
                    def _(dve):
                        for kv in range(2):
                            dve.wait_ge(kv_ready, kv + 1)
                            dve.tensor_copy(kvT[:, kv], kvb[:, kv, 0:KD * BS].rearrange("p (k n) -> p k n", k=KD))\
                               .then_inc(kv_done, 1)
                        for j in range(2 * KH):
                            h = head(j // 2, j % 2)
                            dve.wait_ge(m_ready, j + 1)
                            for k in range(KD):
                                cp = dve.tensor_copy(keys[:, :, k, h * S:(h + 1) * S],
                                                     mb[:, j % 2, k * BS:(k + 1) * BS]
                                                     .rearrange("p (b s) -> p b s", b=B))
                            cp.then_inc(m_done, 1)

                    @block.scalar
                    def _(act):
                        for j in range(2 * KH):
                            h = head(j // 2, j % 2)
                            act.wait_ge(o_ready, j + 1)
                            act.copy(vstage[:, :, h], vb[0:S, 2 * (j // 2 % 2) + j % 2]
                                     .rearrange("p (b d) -> p b d", b=B)).then_inc(o_done, 1)
            else:
                wc = d.sb("h_wc", [P, KD, D])
                vb = d.ps("h_vb", [P, 2, 512])
                with nc.Block() as block:
                    @block.sync
                    def _(sp):
                        sp.dma_start(wc[:], w["WcT"].rearrange("(k p) n -> p k n", p=P)).then_inc(loaded, 16)
                        sp.wait_ge(zeroed, 1)
                        for h in range(NH):
                            r0 = (h % 8) * HD
                            sp.dma_start(keys[r0:r0 + HD, :, h // 8, h * S:(h + 1) * S],
                                         w["ctxT"][h * HD:(h + 1) * HD].rearrange("r (b s) -> r b s", b=B))\
                              .then_inc(loaded, 16)

                    @block.gpsimd
                    def _(pool):
                        load_mlp_weights(pool, glob, w)

                    @block.vector
                    def _(dve):
                        dve.memset(keys[:], 0.0).then_inc(zeroed, 1)
                        dve.memset(glob["mlp_raw"][:, 0:WCH].bitcast(U32), 0)
                        for j in range(B * FB):
                            b, blk = j // FB, j % FB
                            rows = P if blk < FB - 1 else LAST
                            dve.wait_ge(o_ready, j + 1)
                            dve.tensor_copy(vals[0:rows, b, blk], vb[0:rows, j % 2, 0:D]).then_inc(o_done, 1)

                    @block.tensor
                    def _(pe):
                        pe.wait_ge(loaded, 16 * (NH + 1))
                        for j in range(B * FB):
                            b, blk = j // FB, j % FB
                            rows = P if blk < FB - 1 else LAST
                            if j >= 2:
                                pe.wait_ge(o_done, j - 1)
                            for k in range(KD):
                                mm = pe.matmul(vb[0:rows, j % 2, 0:D], keys[:, b, k, blk * P:blk * P + rows],
                                               wc[:, k], start=k == 0, stop=k == KD - 1)
                            mm.then_inc(o_ready, 1)

        xs = c.sb(tag + "_xs", [P, GT, D])
        xT = c.sb(tag + "_xT", [P, KD, GW])
        pr = c.sb(tag + "_pr", [P, 2, FL])
        pT = c.sb(tag + "_pT", [P, FB, P])
        r = c.sb(tag + "_r", [P, GT, D])
        mx = c.sb(tag + "_mx", [P, 2, NH])
        sm = c.sb(tag + "_sm", [P, 2, NH])
        st6 = c.sb(tag + "_st6", [P, GT, 6])
        mv = c.sb(tag + "_mv", [P, GT, 2])
        rstd = c.sb(tag + "_rstd", [P, GT])
        sc = c.ps(tag + "_sc", [P, 3 * 512])
        tb = c.ps(tag + "_tb", [P, 2, 512])
        acc = c.ps(tag + "_acc", [P, 2, 512])
        names = ["xs_ready", "tb_ready", "tb_done", "s_ready", "d_ready", "e_ready", "p_ready",
                 "acc_ready", "acc_done", "mv_ready", "rstd_ready", "share_done"]
        s = dict(zip(names, c.sems(*[tag + "_" + n for n in names])))
        if not first:
            share = c.sb("h_share", [P, 2, WCH])
            share_ready = c.sems("h_share_ready0", "h_share_ready1")
            bits = glob["mlp_raw"][:, 0:WCH].bitcast(U32)
        NB3 = -(-FB // 4)
        PER = KD + GT * NB3
        if first:
            products = [[(a, min(a + 512, FL), k) for k in range(KD)] for a in range(0, FL, 512)]
        else:
            mid = FL // 2
            products = [[(0, 512, 0)], [(512, mid, 0)], [(mid, 1024, 1)], [(1024, FL, 1)]]
        with nc.Block() as block:
            @block.sync
            def _(sp):
                if not first:
                    with sp.Fori(0, NT // 2) as i:
                        for q in range(2):
                            sp.wait_ge(s["share_done"], 2 * i + q)
                            sp.dma_start(share[:, q], w["mlp_shares"][ds(2 * i + q, 1)]
                                         .rearrange("a p n -> p (a n)")).then_inc(share_ready[q], 16)

            @block.gpsimd
            def _(pool):
                with pool.Fori(0, G) as g:
                    stage_group(pool, s, g, xs, X, PER)
                    rstd_group(pool, s, g + 1, mv, rstd, glob, GT)

            @block.tensor
            def _(pe):
                with pe.Fori(0, G) as g:
                    b = g // 2

                    def scores(st):
                        pe.wait_ge(s["d_ready"], GT * g + st)
                        for group in products:
                            for i, (a, z, k) in enumerate(group):
                                mm = pe.matmul(sc[:, a:z], xT[:, k, st * P:st * P + P],
                                               keys[:, ds(b, 1), k, a:z].rearrange("p a n -> p (a n)"),
                                               start=i == 0, stop=i == len(group) - 1)
                        mm.then_inc(s["s_ready"], 1)

                    turn_group(pe, s, g, xs, tb, ident, per=PER)
                    pe.wait_ge(s["tb_done"], PER * g + KD)
                    scores(0)
                    for st in range(GT):
                        if st < GT - 1:
                            scores(st + 1)
                        pe.wait_ge(s["p_ready"], GT * g + st + 1)
                        for q in range(NB3):
                            j = KD + NB3 * st + q
                            pe.wait_ge(s["tb_done"], ring(PER, g, j, 2))
                            for blk in range(4 * q, min(4 * q + 4, FB)):
                                rows = P if blk < FB - 1 else LAST
                                t = pe.transpose(tb[0:rows, j % 2, (blk % 4) * P:(blk % 4) * P + P],
                                                 pr[:, st % 2, blk * P:blk * P + rows], ident[:])
                            t.then_inc(s["tb_ready"], 1)
                        pe.wait_ge(s["tb_done"], PER * g + KD + NB3 * (st + 1))
                        pe.wait_ge(s["acc_done"], ring(GT, g, st, 2))
                        for blk in range(FB):
                            rows = P if blk < FB - 1 else LAST
                            mm = pe.matmul(acc[:, st % 2, 0:D], pT[0:rows, blk],
                                           vals[0:rows, ds(b, 1), blk].rearrange("p a n -> p (a n)"),
                                           start=blk == 0, stop=blk == FB - 1)
                        mm.then_inc(s["acc_ready"], 1)

            @block.scalar
            def _(act):
                with act.Fori(0, G) as g:
                    for k in range(KD):
                        act.wait_ge(s["tb_ready"], PER * g + k + 1)
                        act.copy(xT[:, k], tb[:, k]).then_inc(s["tb_done"], 1)

                    def exps(st):
                        act.wait_ge(s["d_ready"], GT * g + st + 1)
                        act.activation(pr[:, st % 2], pr[:, st % 2], ACT.Exp, scale=scale)\
                           .then_inc(s["e_ready"], 1)

                    exps(0)
                    for st in range(GT):
                        if st < GT - 1:
                            exps(st + 1)
                        for q in range(NB3):
                            j = KD + NB3 * st + q
                            act.wait_ge(s["tb_ready"], PER * g + j + 1)
                            if q < NB3 - 1:
                                act.copy(pT[:, 4 * q:4 * q + 4], tb[:, j % 2].rearrange("p (a n) -> p a n", n=P))\
                                   .then_inc(s["tb_done"], 1)
                            else:
                                full = (FB - 1) % 4
                                act.copy(pT[:, 4 * q:FB - 1], tb[:, j % 2, 0:full * P]
                                         .rearrange("p (a n) -> p a n", n=P))
                                act.copy(pT[0:LAST, FB - 1], tb[0:LAST, j % 2, full * P:full * P + P])\
                                   .then_inc(s["tb_done"], 1)

            @block.vector
            def _(dve):
                with dve.Fori(0, G) as g:
                    def shift(st):
                        q = st % 2
                        dve.drain()
                        dve.wait_ge(s["s_ready"], GT * g + st + 1)
                        dve.tensor_reduce(mx[:, q], sc[:, 0:FL].rearrange("p (h s) -> p h s", s=S), AX.X, ALU.max)
                        dve.drain()
                        dve.tensor_tensor(pr[:, q].rearrange("p (h s) -> p h s", s=S),
                                          sc[:, 0:FL].rearrange("p (h s) -> p h s", s=S),
                                          mx[:, q].rearrange("p (h a) -> p h a", a=1).to_broadcast([P, NH, S]),
                                          ALU.subtract).then_inc(s["d_ready"], 1)

                    def norm(st):
                        q = st % 2
                        dve.wait_ge(s["e_ready"], GT * g + st + 1)
                        e = pr[:, q].rearrange("p (h s) -> p h s", s=S)
                        dve.tensor_reduce(sm[:, q], e, AX.X, ALU.add)
                        dve.drain()
                        dve.reciprocal(sm[:, q], sm[:, q])
                        dve.drain()
                        dve.tensor_tensor(e, e, sm[:, q].rearrange("p (h a) -> p h a", a=1)
                                          .to_broadcast([P, NH, S]), ALU.mult).then_inc(s["p_ready"], 1)

                    def residual(st):
                        dve.wait_ge(s["acc_ready"], GT * g + st + 1)
                        dve.tensor_tensor(r[:, st], acc[:, st % 2, 0:D],
                                          X[:, ds(g * GT + st, 1), :].rearrange("p a d -> p (a d)"),
                                          ALU.add).then_inc(s["acc_done"], 1)

                    shift(0)
                    for st in range(GT):
                        if st < GT - 1:
                            shift(st + 1)
                        norm(st)
                        if st:
                            residual(st - 1)
                        if not first:
                            dve.wait_ge(share_ready[st % 2], 16 * (g * GT // 2 + st // 2 + 1))
                            dve.tensor_tensor(bits, bits, share[:, st % 2].bitcast(U32), ALU.bitwise_or)\
                               .then_inc(s["share_done"], 1)
                    residual(GT - 1)
                    stats(dve, s, lambda i: r[:, i], st6, mv, GT)
                    dve.wait_ge(s["rstd_ready"], g + 1)
                    for st in range(GT):
                        dve.tensor_scalar(X[:, ds(g * GT + st, 1), :].rearrange("p a d -> p (a d)"), r[:, st],
                                          mv[:, st, 0:1], rstd[:, st:st + 1], ALU.subtract, ALU.mult)


def mixture_of_experts(nc, glob, w):
    FT = -(-F // P)
    FP = [min(P, F - P * i) for i in range(FT)]
    with ExitStack() as stack:
        c = Ctx(nc, stack)
        xs = c.sb("f_xs", [P, GT, D])
        XT = c.sb("f_XT", [P, KD, T])
        gw = c.sb("f_gw", [P, KD, E])
        wgu = c.sb("f_wgu", [P, 2, 2, KD, F])
        wd = c.sb("f_wd", [P, 2, FT, D])
        rank = c.sb("f_rank", [P, GT, E])
        lg = c.sb("f_lg", [P, GT, E])
        pe_ = c.sb("f_scores", [P, GT, E])
        hot1 = c.sb("f_hot1", [P, GT, E])
        hot2 = c.sb("f_hot2", [P, GT, E])
        tmp = c.sb("f_tmp", [P, GT, E])
        m0 = c.sb("f_m0", [P, GT, 1])
        m1 = c.sb("f_m1", [P, GT, 1])
        m2 = c.sb("f_m2", [P, GT, 1])
        den = c.sb("f_den", [P, GT, 1])
        lgT = c.sb("f_lgT", [P, GW])
        comb = c.sb("f_comb", [P, NE, NT])
        ce = c.sb("f_ce", [P, 2, NT])
        sg = c.sb("f_sg", [P, 2, 512])
        hid = c.sb("f_hid", [P, 2, FT, 512])
        st6 = c.sb("f_st6", [P, GT, 6])
        mv = c.sb("f_mv", [P, GT, 2])
        rstd = c.sb("f_rstd", [P, GT])
        tb = c.ps("f_tb", [P, 2, 512])
        gu = c.ps("f_gu", [P, 2, 2, 512])
        acc = c.ps("f_acc", [P, 2, 512])
        names = ["loaded", "xs_ready", "tb_ready", "tb_done", "l_ready", "l_done", "x_ready", "sub_ready",
                 "exp_ready", "gu_ready", "sg_ready", "h_done", "acc_ready", "acc_done", "ce_ready", "mv_ready",
                 "rstd_ready", "wl0", "wl1", "rank_ready"]
        s = dict(zip(names, c.sems(*["f_" + n for n in names])))
        wl = [s["wl0"], s["wl1"]]
        X, ident = glob["X"], glob["ident"]
        HPE = G * FT

        with nc.Block() as block:
            @block.sync
            def _(sp):
                def load(e, p):
                    sp.dma_start(wgu[:, p], w["w_gu"][ds(e, 1)].rearrange("a u (k p) f -> p (a u) k f", p=P))\
                      .then_inc(wl[p], 16)
                    sp.dma_start(wd[:, p, 0:FT - 1], w["w_dn"][ds(e, 1), 0:(FT - 1) * P]
                                 .rearrange("a (k p) d -> p (a k) d", p=P)).then_inc(wl[p], 16)
                    sp.dma_start(wd[0:FP[-1], p, FT - 1], w["w_dn"][ds(e, 1), (FT - 1) * P:F]
                                 .rearrange("a p d -> p (a d)")).then_inc(wl[p], 16)
                sp.dma_start(gw[:], w["gate_wT"].rearrange("(k p) e -> p k e", p=P)).then_inc(s["loaded"], 16)
                load(0, 0)
                load(1, 1)
                with sp.Fori(1, NE // 2) as i:
                    for p in range(2):
                        sp.wait_ge(s["acc_ready"], NT * (2 * i + p - 1))
                        load(2 * i + p, p)

            @block.gpsimd
            def _(pool):
                for j in range(E):
                    pool.memset(rank[:, :, j:j + 1], float(E - j))
                pool.drain()
                pool.memset(comb[:, E:NE], 1.0).then_inc(s["rank_ready"], 1)
                with pool.Fori(0, G) as g:
                    stage_group(pool, s, g, xs, X)
                pool.wait_ge(s["x_ready"], G)
                with pool.Fori(0, NE // 2) as i:
                    for p in range(2):
                        e = 2 * i + p
                        pool.wait_ge(s["acc_done"], NT * e)
                        pool.tensor_copy(ce[:, p:p + 1], comb[:, ds(e, 1)]).then_inc(s["ce_ready"], 1)
                with pool.Fori(0, G) as g:
                    rstd_group(pool, s, g + 1, mv, rstd, glob, GT)

            @block.tensor
            def _(pe):
                pe.wait_ge(s["loaded"], 16)
                with pe.Fori(0, G) as g:
                    turn_group(pe, s, g, xs, tb, ident)
                    pe.wait_ge(s["tb_done"], 2 * g + 2)
                    pe.wait_ge(s["l_done"], g)
                    for k in range(KD):
                        mm = pe.matmul(acc[0:E, 0], gw[:, k], XT[:, k, ds(g * GW, GW)], start=k == 0,
                                       stop=k == KD - 1)
                    mm.then_inc(s["l_ready"], 1)
                    pe.wait_ge(s["sub_ready"], 2 * g + 1)
                    for st in range(GT):
                        t = pe.transpose(acc[:, 1, st * P:st * P + P], lgT[:, st * P:st * P + P], ident[:])
                    t.then_inc(s["l_ready"], 1)

                with pe.Fori(0, NE // 2) as i:
                    for p in range(2):
                        e = 2 * i + p

                        def up(g):
                            for hm in range(FT):
                                j = FT * g + hm
                                pe.wait_ge(s["h_done"], ring(HPE, e, j, 2))
                                if j == 0:
                                    pe.wait_ge(wl[p], 48 * (i + 1))
                                for u in range(2):
                                    for k in range(KD):
                                        mm = pe.matmul(gu[0:FP[hm], j % 2, u],
                                                       wgu[:, p, u, k, hm * P:hm * P + FP[hm]],
                                                       XT[:, k, g * GW:g * GW + GW], start=k == 0,
                                                       stop=k == KD - 1)
                                mm.then_inc(s["gu_ready"], 1)

                        def down(g):
                            pe.wait_ge(s["h_done"], HPE * e + FT * (g + 1))
                            for st in range(GT):
                                pe.wait_ge(s["acc_done"], ring(NT, e, GT * g + st, 2))
                                for hm in range(FT):
                                    mm = pe.matmul(acc[:, st % 2, 0:D], hid[0:FP[hm], g % 2, hm, st * P:st * P + P],
                                                   wd[0:FP[hm], p, hm], start=hm == 0, stop=hm == FT - 1)
                                mm.then_inc(s["acc_ready"], 1)

                        up(0)
                        for g in range(1, G):
                            up(g)
                            down(g - 1)
                        down(G - 1)

            @block.scalar
            def _(act):
                with act.Fori(0, G) as g:
                    for k in range(KD):
                        act.wait_ge(s["tb_ready"], KD * g + k + 1)
                        act.copy(XT[:, k, ds(g * GW, GW)], tb[:, k]).then_inc(s["tb_done"], 1)
                    act.wait_ge(s["sub_ready"], 2 * g + 2)
                    act.activation(pe_[:], lg[:], ACT.Exp).then_inc(s["exp_ready"], 1)
                with act.Fori(0, NE) as e:
                    for j in range(HPE):
                        act.wait_ge(s["gu_ready"], HPE * e + j + 1)
                        act.wait_ge(s["h_done"], ring(HPE, e, j, 2))
                        n = FP[j % FT]
                        act.activation(sg[0:n, j % 2], gu[0:n, j % 2, 0], ACT.Silu).then_inc(s["sg_ready"], 1)

            @block.vector
            def _(dve):
                dve.memset(lgT[:], 0.0)
                dve.drain()
                dve.wait_ge(s["rank_ready"], 1)

                def wide(a):
                    return a[:].to_broadcast([P, GT, E])

                def first_of(hot, scores, top):
                    dve.tensor_tensor(tmp[:], scores[:], wide(top), ALU.is_equal)
                    dve.drain()
                    dve.tensor_tensor(tmp[:], tmp[:], rank[:], ALU.mult)
                    dve.drain()
                    dve.tensor_reduce(m0[:], tmp[:], AX.X, ALU.max)
                    dve.drain()
                    dve.tensor_tensor(hot[:], tmp[:], wide(m0), ALU.is_equal)
                    dve.drain()

                with dve.Fori(0, G) as g:
                    dve.drain()
                    dve.wait_ge(s["l_ready"], 2 * g + 1)
                    dve.tensor_copy(lgT[0:E], acc[0:E, 0]).then_inc(s["sub_ready"], 1)
                    dve.wait_ge(s["l_ready"], 2 * g + 2)
                    dve.tensor_copy(tmp[:], acc[:, 1].rearrange("p (s e) -> p s e", e=P)[:, :, 0:E])\
                       .then_inc(s["l_done"], 1)
                    dve.drain()
                    dve.tensor_reduce(m0[:], tmp[:], AX.X, ALU.max)
                    dve.drain()
                    dve.tensor_tensor(lg[:], tmp[:], wide(m0), ALU.subtract).then_inc(s["sub_ready"], 1)
                    dve.wait_ge(s["exp_ready"], g + 1)
                    dve.tensor_reduce(den[:], pe_[:], AX.X, ALU.add)
                    dve.drain()
                    dve.reciprocal(den[:], den[:])
                    dve.drain()
                    dve.tensor_tensor(pe_[:], pe_[:], wide(den), ALU.mult)
                    dve.drain()
                    dve.tensor_reduce(m1[:], pe_[:], AX.X, ALU.max)
                    dve.drain()
                    first_of(hot1, pe_, m1)
                    dve.scalar_tensor_tensor(out=pe_[:], in0=hot1[:], scalar=-2.0, in1=pe_[:], op0=ALU.mult,
                                             op1=ALU.add)
                    dve.drain()
                    dve.tensor_reduce(m2[:], pe_[:], AX.X, ALU.max)
                    dve.drain()
                    first_of(hot2, pe_, m2)
                    dve.tensor_tensor(den[:], m1[:], m2[:], ALU.add)
                    dve.drain()
                    dve.tensor_scalar(den[:], den[:], 1e-20, None, ALU.add)
                    dve.drain()
                    dve.reciprocal(den[:], den[:])
                    dve.drain()
                    dve.scalar_tensor_tensor(out=m1[:], in0=m1[:], scalar=2.5, in1=den[:], op0=ALU.mult,
                                             op1=ALU.mult)
                    dve.scalar_tensor_tensor(out=m2[:], in0=m2[:], scalar=2.5, in1=den[:], op0=ALU.mult,
                                             op1=ALU.mult)
                    dve.drain()
                    dve.tensor_tensor(hot1[:], hot1[:], wide(m1), ALU.mult)
                    dve.tensor_tensor(hot2[:], hot2[:], wide(m2), ALU.mult)
                    dve.drain()
                    dve.tensor_tensor(comb[:, 0:E, ds(g * GT, GT)].rearrange("p e s -> p s e"), hot1[:], hot2[:],
                                      ALU.add).then_inc(s["x_ready"], 1)

                with dve.Fori(0, NE // 2) as i:
                    for p in range(2):
                        e = 2 * i + p

                        def hidden(g):
                            for hm in range(FT):
                                j = FT * g + hm
                                n = FP[hm]
                                dve.wait_ge(s["sg_ready"], HPE * e + j + 1)
                                dve.tensor_tensor(hid[0:n, g % 2, hm], sg[0:n, j % 2], gu[0:n, j % 2, 1],
                                                  ALU.mult).then_inc(s["h_done"], 1)

                        def add_up(g):
                            if g == 0:
                                dve.wait_ge(s["ce_ready"], e + 1)
                            for st in range(GT):
                                t = g * GT + st
                                dve.wait_ge(s["acc_ready"], NT * e + t + 1)
                                dve.scalar_tensor_tensor(out=X[:, t], in0=acc[:, st % 2, 0:D],
                                                         scalar=ce[:, p, t:t + 1], in1=X[:, t], op0=ALU.mult,
                                                         op1=ALU.add).then_inc(s["acc_done"], 1)

                        hidden(0)
                        for g in range(1, G):
                            hidden(g)
                            add_up(g - 1)
                        add_up(G - 1)

                with dve.Fori(0, G) as g:
                    stats(dve, s, lambda i: X[:, ds(g * GT + i, 1), :].rearrange("p a d -> p (a d)"), st6, mv, GT)
                    dve.wait_ge(s["rstd_ready"], g + 1)
                    for st in range(GT):
                        x = X[:, ds(g * GT + st, 1), :].rearrange("p a d -> p (a d)")
                        dve.tensor_scalar(x, x, mv[:, st, 0:1], rstd[:, st:st + 1], ALU.subtract, ALU.mult)


def delta_rule(nc, glob, w):
    NP = NT // 2
    KW = HID // NH
    CH = 7
    with ExitStack() as stack:
        c = Ctx(nc, stack)
        ws = c.sb("g_ws", [P, KD, 3 * HID + NH])
        wo = c.sb("g_wo", [P, KH, D])
        lnw = c.sb("g_lnw", [P, D])
        lnb = c.sb("g_lnb", [P, D])
        hs = c.sb("g_hs", [P, 2, D])
        hT = c.sb("g_hT", [P, 2, KD, P])
        st6 = c.sb("g_st6", [P, 2, 6])
        mv = c.sb("g_mv", [P, 2, 2])
        rstd = c.sb("g_rstd", [P, 2])
        ut = c.sb("g_ut", [P, 2, 512])
        qk = c.sb("g_qk", [P, 2, 2, HID])
        vb = c.sb("g_vb", [P, 2, HID])
        bt = c.sb("g_bt", [P, 2, NH])
        prod = c.sb("g_prod", [P, 4, HID])
        sums = c.sb("g_sums", [P, 4, NH])
        dots = c.sb("g_dots", [P, 4, NH])
        fac = c.sb("g_fac", [P, 4, NH])
        co = c.sb("g_co", [P, 3, NH])
        out = c.sb("g_out", [P, 2, HID])
        oT = c.sb("g_oT", [P, 2, KH, P])
        r = c.sb("g_r", [P, 2, D])
        hb = c.ps("g_hb", [P, 512])
        ch = c.ps("g_ch", [P, 3, 512])
        tb = c.ps("g_tb", [P, 2, 512])
        acc = c.ps("g_acc", [P, 2, 512])
        names = ["loaded", "mv_ready", "rstd_ready", "hs_ready", "hb_ready", "hT_ready", "ch_ready", "act_done",
                 "t_ready", "stt_done", "qk_ready", "prod_ready", "co_ready", "part_ready", "o_ready", "tb_ready",
                 "tb_done", "acc_ready", "acc_done"]
        s = dict(zip(names, c.sems(*["g_" + n for n in names])))
        X, ident = glob["X"], glob["ident"]

        def heads(a):
            return a.rearrange("p (h d) -> p h d", h=NH)

        with nc.Block() as block:
            @block.sync
            def _(sp):
                for k in range(KD):
                    sp.dma_start(ws[:, k], w["w_slow"][k * P:(k + 1) * P]).then_inc(s["loaded"], 16)
                sp.dma_start(wo[:], w["w_out"].rearrange("(k p) n -> p k n", p=P)).then_inc(s["loaded"], 16)
                sp.dma_start(lnw[:], w["ln_w"].to_broadcast([P, D])).then_inc(s["loaded"], 16)
                sp.dma_start(lnb[:], w["ln_b"].to_broadcast([P, D])).then_inc(s["loaded"], 16)

            @block.gpsimd
            def _(pool):
                def dot_products(p):
                    pool.wait_ge(s["qk_ready"], p + 1)
                    q0, k0, q1, k1 = qk[:, 0, 0], qk[:, 0, 1], qk[:, 1, 0], qk[:, 1, 1]
                    for i, (a, b) in enumerate(((k0, q0), (k0, k1), (k0, q1), (k1, q1))):
                        pool.tensor_tensor(prod[:, i], a, b, ALU.mult).then_inc(s["prod_ready"], 1)

                def outputs(p):
                    pool.wait_ge(s["co_ready"], p + 1)
                    pool.wait_ge(s["act_done"], 2 * CH * p + 2 * CH)
                    pool.wait_ge(s["tb_ready"], 4 * p)
                    pool.tensor_tensor(heads(out[:, 0]), heads(vb[:, 0]), co[:, 0].rearrange(
                        "p (h a) -> p h a", a=1).to_broadcast([P, NH, KW]), ALU.mult).then_inc(s["part_ready"], 1)
                    pool.tensor_tensor(heads(prod[:, 0]), heads(vb[:, 1]), co[:, 2].rearrange(
                        "p (h a) -> p h a", a=1).to_broadcast([P, NH, KW]), ALU.mult).then_inc(s["part_ready"], 1)

                with pool.Fori(0, NP) as p:
                    rstd_group(pool, s, 2 * p + 1, mv, rstd, glob, 2)
                    dot_products(p)
                    outputs(p)
                    rstd_group(pool, s, 2 * p + 2, mv, rstd, glob, 2)

            @block.tensor
            def _(pe):
                def project(p):
                    pe.wait_ge(s["hs_ready"], p + 1)
                    pe.wait_ge(s["hT_ready"], p)
                    for tm in range(2):
                        for k in range(KD):
                            a = (tm * KD + k) * P
                            t = pe.transpose(hb[:, a:a + P], hs[:, tm, k * P:k * P + P], ident[:])
                    t.then_inc(s["hb_ready"], 1)
                    pe.wait_ge(s["hT_ready"], p + 1)
                    for j in range(2 * CH):
                        tm, q = j // CH, j % CH
                        width = 512 if q < 6 else NH
                        if j < 3:
                            pe.wait_ge(s["act_done"], 2 * CH * p)
                            pe.wait_ge(s["stt_done"], 8 * p)
                        elif (j - 3) % CH < 4:
                            pe.wait_ge(s["stt_done"], 8 * p + 4 * ((j - 3) // CH) + (j - 3) % CH + 1)
                        else:
                            pe.wait_ge(s["act_done"], 2 * CH * p + j - 3 + 1)
                        for k in range(KD):
                            mm = pe.matmul(ch[:, j % 3, 0:width], hT[:, tm, k], ws[:, k, q * 512:q * 512 + width],
                                           start=k == 0, stop=k == KD - 1)
                        mm.then_inc(s["ch_ready"], 1)

                def project_out(p):
                    pe.wait_ge(s["o_ready"], p + 1)
                    for q in range(4):
                        pe.wait_ge(s["tb_done"], ring(4, p, q, 2))
                        for blk in range(4):
                            b8 = (q % 2) * 4 + blk
                            t = pe.transpose(tb[:, q % 2, blk * P:blk * P + P],
                                             out[:, q // 2, b8 * P:b8 * P + P], ident[:])
                        t.then_inc(s["tb_ready"], 1)
                    for tm in range(2):
                        pe.wait_ge(s["tb_done"], 4 * p + 2 * tm + 2)
                        pe.wait_ge(s["acc_done"], 2 * p)
                        for k in range(KH):
                            mm = pe.matmul(acc[:, tm, 0:D], oT[:, tm, k], wo[:, k], start=k == 0, stop=k == KH - 1)
                        mm.then_inc(s["acc_ready"], 1)

                pe.wait_ge(s["loaded"], 16 * (KD + 3))
                with pe.Fori(0, NP) as p:
                    project(p)
                    project_out(p)

            @block.scalar
            def _(act):
                with act.Fori(0, NP) as p:
                    act.wait_ge(s["hb_ready"], p + 1)
                    act.copy(hT[:], hb[:].rearrange("p (t k n) -> p t k n", t=2, k=KD)).then_inc(s["hT_ready"], 1)
                    n = 0
                    for j in range(2 * CH):
                        tm, q = j // CH, j % CH
                        act.wait_ge(s["ch_ready"], 2 * CH * p + j + 1)
                        if q < 4:
                            act.wait_ge(s["stt_done"], ring(8, p, n, 2))
                            act.activation(ut[:, n % 2], ch[:, j % 3], ACT.Relu, scale=-1.0)\
                               .then_inc(s["act_done"], 1)
                            act.drain()
                            act.activation(ut[:, n % 2], ut[:, n % 2], ACT.Exp, scale=-1.0)\
                               .then_inc(s["t_ready"], 1)
                            n += 1
                        elif q < 6:
                            if j == 4:
                                act.wait_ge(s["o_ready"], p)
                            act.copy(vb[:, tm, (q - 4) * 512:(q - 3) * 512], ch[:, j % 3])\
                               .then_inc(s["act_done"], 1)
                        else:
                            if tm == 0:
                                act.wait_ge(s["co_ready"], p)
                            act.activation(bt[:, tm], ch[:, j % 3, 0:NH], ACT.Tanh, scale=0.5)\
                               .then_inc(s["act_done"], 1)
                    for q in range(4):
                        act.wait_ge(s["tb_ready"], 4 * p + q + 1)
                        act.copy(oT[:, q // 2, (q % 2) * 4:(q % 2) * 4 + 4],
                                 tb[:, q % 2].rearrange("p (b n) -> p b n", n=P)).then_inc(s["tb_done"], 1)

            @block.vector
            def _(dve):
                dve.wait_ge(s["loaded"], 16 * (KD + 3))

                def tile(p, tm):
                    return X[:, ds(p + NP * tm, 1), :].rearrange("p a d -> p (a d)")

                def normed(p):
                    stats(dve, s, lambda i: tile(p, i), st6, mv, 2)
                    dve.wait_ge(s["rstd_ready"], 2 * p + 1)
                    dve.wait_ge(s["hb_ready"], p)
                    for tm in range(2):
                        dve.tensor_scalar(hs[:, tm], tile(p, tm), mv[:, tm, 0:1], rstd[:, tm:tm + 1],
                                          ALU.subtract, ALU.mult)
                    dve.drain()
                    for tm in range(2):
                        dve.tensor_tensor(hs[:, tm], hs[:, tm], lnw[:], ALU.mult)
                    dve.drain()
                    for tm in range(2):
                        a = dve.tensor_tensor(hs[:, tm], hs[:, tm], lnb[:], ALU.add)
                    a.then_inc(s["hs_ready"], 1)

                def positive(p):
                    n = 0
                    for j in range(2 * CH):
                        tm, q = j // CH, j % CH
                        if q < 4:
                            dve.wait_ge(s["t_ready"], 8 * p + n + 1)
                            dve.scalar_tensor_tensor(out=qk[:, tm, q // 2, (q % 2) * 512:(q % 2) * 512 + 512],
                                                     in0=ch[:, j % 3], scalar=0.0, in1=ut[:, n % 2], op0=ALU.max,
                                                     op1=ALU.add).then_inc(s["stt_done"], 1)
                            n += 1
                    dve.drain()
                    dve.tensor_reduce(sums[:].rearrange("p a h -> p (a h)"),
                                      qk[:].rearrange("p t a (h d) -> p (t a h) d", h=NH), AX.X, ALU.add)\
                       .then_inc(s["qk_ready"], 1)

                def coefficients(p):
                    dve.drain()
                    dve.reciprocal(sums[:], sums[:])
                    dve.drain()
                    q0, k0, q1, k1 = (sums[:, i] for i in range(4))
                    for i, (a, b) in enumerate(((k0, q0), (k0, k1), (k0, q1), (k1, q1))):
                        dve.tensor_tensor(fac[:, i], a, b, ALU.mult)
                    for i in range(4):
                        dve.wait_ge(s["prod_ready"], 4 * p + i + 1)
                        dve.tensor_reduce(dots[:, i], heads(prod[:, i]), AX.X, ALU.add)
                    dve.drain()
                    dve.wait_ge(s["act_done"], 2 * CH * p + 2 * CH)
                    dve.tensor_tensor(dots[:], dots[:], fac[:], ALU.mult)
                    dve.tensor_scalar(bt[:], bt[:], 0.5, 0.5, ALU.mult, ALU.add)
                    dve.drain()
                    b0, b1 = bt[:, 0], bt[:, 1]
                    dve.tensor_tensor(co[:, 0], b0, dots[:, 0], ALU.mult)
                    dve.tensor_tensor(fac[:, 0], b0, dots[:, 1], ALU.mult)
                    dve.tensor_tensor(fac[:, 1], b0, dots[:, 2], ALU.mult)
                    dve.tensor_tensor(co[:, 2], b1, dots[:, 3], ALU.mult)
                    dve.drain()
                    dve.tensor_tensor(fac[:, 0], fac[:, 0], co[:, 2], ALU.mult)
                    dve.drain()
                    dve.tensor_tensor(co[:, 1], fac[:, 1], fac[:, 0], ALU.subtract).then_inc(s["co_ready"], 1)
                    dve.drain()
                    dve.wait_ge(s["tb_ready"], 4 * p)
                    dve.tensor_tensor(heads(out[:, 1]), heads(vb[:, 0]), co[:, 1].rearrange(
                        "p (h a) -> p h a", a=1).to_broadcast([P, NH, KW]), ALU.mult)
                    dve.drain()
                    dve.wait_ge(s["part_ready"], 2 * p + 2)
                    dve.tensor_tensor(out[:, 1], out[:, 1], prod[:, 0], ALU.add).then_inc(s["o_ready"], 1)

                def residual(p):
                    dve.drain()
                    for tm in range(2):
                        dve.wait_ge(s["acc_ready"], 2 * p + tm + 1)
                        dve.scalar_tensor_tensor(out=r[:, tm], in0=tile(p, tm), scalar=2.0, in1=acc[:, tm, 0:D],
                                                 op0=ALU.mult, op1=ALU.add).then_inc(s["acc_done"], 1)
                    stats(dve, s, lambda i: r[:, i], st6, mv, 2)
                    dve.wait_ge(s["rstd_ready"], 2 * p + 2)
                    for tm in range(2):
                        dve.tensor_scalar(tile(p, tm), r[:, tm], mv[:, tm, 0:1], rstd[:, tm:tm + 1],
                                          ALU.subtract, ALU.mult)

                with dve.Fori(0, NP) as p:
                    normed(p)
                    positive(p)
                    coefficients(p)
                    residual(p)


def gated_mlp(nc, glob, w, y):
    with ExitStack() as stack:
        c = Ctx(nc, stack)
        wab, wh, w3 = mlp_weights(glob["mlp_w"])
        raw = glob["mlp_raw"][:].rearrange("p (q n) -> p q n", q=2)
        bits = glob["mlp_raw"][:, 0:WCH].bitcast(U32)
        xs = c.sb("i_xs", [P, GT, D])
        sc = c.sb("i_sc", [P, 4, KH])
        s3 = c.sb("i_s3", [P, D])
        full = c.sb("i_full", [P, 2, 512])
        h = c.sb("i_h", [P, 2, KH, 2, GW], F32R)
        r = c.sb("i_r", [P, GT, D])
        st6 = c.sb("i_st6", [P, GT, 6])
        mv = c.sb("i_mv", [P, GT, 2])
        rstd = c.sb("i_rstd", [P, GT])
        low = c.sb("i_low", [P, 1], U32)
        lowf = c.sb("i_lowf", [P, 1])
        flagf = c.sb("i_flagf", [1, 1])
        flag = c.sb("i_flag", [1, 1], mybir.dt.int32)
        tb = c.ps("i_tb", [P, 2, 512])
        hb = c.ps("i_hb", [P, 4, 512])
        acc = c.ps("i_acc", [P, 2, 512])
        names = ["loaded", "xs_ready", "tb_ready", "tb_done", "ab_ready", "sg_ready", "ab_done", "ab_split",
                 "h_ready", "full_ready", "h_split", "acc_ready", "acc_done", "mv_ready", "rstd_ready",
                 "y_ready", "stored", "low_ready", "low_turned", "flag_ready"]
        s = dict(zip(names, c.sems(*["i_" + n for n in names])))
        X, ident = glob["X"], glob["ident"]
        raw_ready = c.sems("i_raw_ready0", "i_raw_ready1")
        UNITS = 3 * KH + 2
        xT = h[:, 1, 0:KD]
        with nc.Block() as block:
            @block.sync
            def _(sp):
                sp.dma_start(sc[:], w["scales"]).then_inc(s["loaded"], 16)
                sp.dma_start(s3[:], w["w3_s"].to_broadcast([P, D])).then_inc(s["loaded"], 16)

                def unit(g, u):
                    if u < 2:
                        sp.wait_ge(s["acc_ready"], GT * g)
                    elif u < KH + 2:
                        sp.wait_ge(s["ab_ready"], KH * g + u - 1)
                    else:
                        sp.wait_ge(s["h_ready"], 2 * KH * g + u - KH - 1)
                    if u < KH:
                        for i, name in enumerate(("w1T", "w2T")):
                            sp.dma_start(raw[:, u % 2, i * KD * P:(i + 1) * KD * P].rearrange("p (k n) -> p k n", k=KD),
                                         w[name].rearrange("(k p) n -> p k n", p=P)[:, :, u * P:u * P + P])\
                              .then_inc(raw_ready[u % 2], 16)
                    elif u < 3 * KH:
                        m = u % KH
                        sp.dma_start(raw[:, u % 2].rearrange("p (k n) -> p k n", k=KH),
                                     w["h1T" if u < 2 * KH else "h2T"].rearrange("(k p) n -> p k n", p=P)
                                     [:, :, m * P:m * P + P]).then_inc(raw_ready[u % 2], 16)
                    else:
                        k = (u - 3 * KH) * KH // 2
                        sp.dma_start(raw[:, u % 2].rearrange("p (k n) -> p k n", k=KH // 2),
                                     w["w3T"].rearrange("(k p) n -> p k n", p=P)[:, k:k + KH // 2])\
                          .then_inc(raw_ready[u % 2], 16)

                sp.wait_ge(s["flag_ready"], 1)
                extra = sp.value_load(flag[0:1, 0:1], min_val=0, max_val=FULL_BITS)
                with sp.If(extra > 0):
                    with sp.Fori(0, G) as g:
                        for u in range(UNITS):
                            unit(g, u)

            @block.gpsimd
            def _(pool):
                def finish(g):
                    rstd_group(pool, s, g + 1, mv, rstd, glob, GT)
                    pool.wait_ge(s["y_ready"], g + 1)
                    pool.dma_start(y.rearrange("(t p) d -> p t d", p=P)[:, ds(g * GT, GT), :],
                                   X[:, ds(g * GT, GT), :]).then_inc(s["stored"], 16)

                stage_group(pool, s, 0, xs, X)
                stage_group(pool, s, 1, xs, X)
                with pool.Fori(0, G - 2) as g:
                    finish(g)
                    stage_group(pool, s, g + 2, xs, X)
                finish(G - 2)
                finish(G - 1)
                pool.wait_ge(s["stored"], 16 * G)

            @block.tensor
            def _(pe):
                pe.wait_ge(glob["mlp_loaded"], 16 * 5)
                pe.wait_ge(s["low_ready"], 1)
                pe.transpose(tb[0:1, 0, 0:P], lowf[:], ident[:]).then_inc(s["low_turned"], 1)

                def groups(exact):
                    def read(ap):
                        return ap if exact or ap.dtype == F32 else ap.bitcast(F32)

                    def need(g, u):
                        if not exact:
                            loads = 3 * KH // 2 + KH // 2 + 1
                            before = u // 2 + min(u // 2, KH // 2)
                            pe.wait_ge(raw_ready[u % 2], 16 * (loads * g + before + (2 if u < KH else 1)))

                    def gate_weights(i, k, m):
                        if exact:
                            return wab[:, i, k, m * P:m * P + P]
                        return raw[:, m % 2, (i * KD + k) * P:(i * KD + k + 1) * P]

                    def hidden_weights(layer, k, m):
                        return wh[:, layer, k, m * P:m * P + P] if exact else raw[:, m % 2, k * P:k * P + P]

                    def down_weights(k):
                        half = KH // 2
                        return w3[:, k] if exact else raw[:, k // half, k % half * D:(k % half + 1) * D]

                    def add(out, lhsT, rhs, k, last):
                        for part in range(2):
                            mm = pe.matmul(out, read(lhsT(part)), read(rhs(part)), start=k == 0 and part == 0,
                                           stop=k == last and part == 1)
                        return mm

                    def gated(g):
                        for m in range(KH):
                            if m == 0:
                                pe.wait_ge(s["full_ready"], 2 * KH * g)
                                pe.wait_ge(s["tb_done"], KD * (g + 1))
                            pe.wait_ge(s["ab_done"], ring(KH, g, m, 2))
                            need(g, m)
                            for i in range(2):
                                for k in range(KD):
                                    mm = add(hb[:, 2 * (m % 2) + i], lambda part: gate_weights(i, k, m),
                                             lambda part: xT[:, k, part], k, KD - 1)
                            mm.then_inc(s["ab_ready"], 1)

                    def hidden(g, layer):
                        for m in range(KH):
                            if layer or m >= 4:
                                pe.wait_ge(s["full_ready"], 2 * KH * g + KH * layer + m - 3)
                            elif m == 0:
                                pe.wait_ge(s["ab_done"], KH * (g + 1) - 1)
                            need(g, KH * (layer + 1) + m)
                            for k in range(KH):
                                if m == 0 and layer == 0:
                                    pe.wait_ge(s["ab_split"], KH * g + k + 1)
                                elif m == 0:
                                    pe.wait_ge(s["h_split"], 2 * KH * g + k + 1)
                                mm = add(hb[:, m % 4], lambda part: hidden_weights(layer, k, m),
                                         lambda part: h[:, layer, k, part], k, KH - 1)
                            mm.then_inc(s["h_ready"], 1)

                    def down(g):
                        need(g, 3 * KH)
                        need(g, 3 * KH + 1)
                        for st in range(GT):
                            pe.wait_ge(s["acc_done"], ring(GT, g, st, 2))
                            for k in range(KH):
                                if st == 0:
                                    pe.wait_ge(s["h_split"], 2 * KH * g + KH + k + 1)
                                mm = add(acc[:, st % 2, 0:D], lambda part: h[:, 0, k, part, st * P:st * P + P],
                                         lambda part: down_weights(k), k, KH - 1)
                            mm.then_inc(s["acc_ready"], 1)

                    turn_group(pe, s, 0, xs, tb, ident)
                    with pe.Fori(0, G - 1) as g:
                        gated(g)
                        hidden(g, 0)
                        hidden(g, 1)
                        turn_group(pe, s, g + 1, xs, tb, ident)
                        down(g)
                    gated(G - 1)
                    hidden(G - 1, 0)
                    hidden(G - 1, 1)
                    down(G - 1)

                pe.wait_ge(s["flag_ready"], 1)
                extra = pe.value_load(flag[0:1, 0:1], min_val=0, max_val=FULL_BITS)
                with pe.If(extra == 0):
                    groups(True)
                with pe.If(extra > 0):
                    groups(False)

            @block.scalar
            def _(act):
                act.wait_ge(s["loaded"], 32)
                with act.Fori(0, G) as g:
                    for m in range(KH):
                        act.wait_ge(s["h_split"], 2 * KH * g)
                        act.wait_ge(s["ab_split"], ring(KH, g, m, 2))
                        act.wait_ge(s["ab_ready"], KH * g + m + 1)
                        act.activation(full[:, m % 2], hb[:, 2 * (m % 2)], ACT.Silu, scale=sc[:, 0, m:m + 1])\
                           .then_inc(s["sg_ready"], 1)
                    for layer in range(2):
                        for m in range(KH):
                            j = KH * layer + m
                            if j < 2:
                                act.wait_ge(s["ab_split"], KH * (g + 1) - 1 + j)
                            else:
                                act.wait_ge(s["h_split"], 2 * KH * g + j - 1)
                            act.wait_ge(s["h_ready"], 2 * KH * g + j + 1)
                            act.activation(full[:, m % 2], hb[:, m % 4], ACT.Gelu,
                                           scale=sc[:, 2 + layer, m:m + 1]).then_inc(s["full_ready"], 1)

            @block.vector
            def _(dve):
                dve.wait_ge(s["loaded"], 32)
                n = WCH
                while n % 2 == 0:
                    n //= 2
                    dve.tensor_tensor(bits[:, 0:n], bits[:, 0:n], bits[:, n:2 * n], ALU.bitwise_or)
                    dve.drain()
                dve.tensor_scalar(bits[:, 0:n], bits[:, 0:n], FULL_BITS, None, ALU.bitwise_and)
                dve.drain()
                dve.tensor_reduce(low[:], bits[:, 0:n], AX.X, ALU.max)
                dve.drain()
                dve.tensor_copy(lowf[:], low[:]).then_inc(s["low_ready"], 1)
                dve.wait_ge(s["low_turned"], 1)
                dve.reduce_max(flagf[:], tb[0:1, 0, 0:P], AX.X)
                dve.drain()
                dve.tensor_copy(flag[:], flagf[:]).then_inc(s["flag_ready"], 1)

                def split(to, of):
                    dve.tensor_copy(to[:, 0], of)
                    dve.drain()
                    return dve.tensor_tensor(to[:, 1], of, to[:, 0].bitcast(F32), ALU.subtract)

                def split_x(g):
                    for k in range(KD):
                        dve.drain()
                        dve.wait_ge(s["tb_ready"], KD * g + k + 1)
                        split(xT[:, k], tb[:, k]).then_inc(s["tb_done"], 1)

                def norm_stats():
                    dve.drain()
                    stats(dve, s, lambda i: r[:, i], st6, mv, GT)

                def norm(g):
                    dve.wait_ge(s["rstd_ready"], g + 1)
                    for st in range(GT):
                        a = dve.tensor_scalar(X[:, ds(g * GT + st, 1), :].rearrange("p a d -> p (a d)"), r[:, st],
                                              mv[:, st, 0:1], rstd[:, st:st + 1], ALU.subtract, ALU.mult)
                    a.then_inc(s["y_ready"], 1)

                def one(g):
                    for m in range(KH):
                        dve.wait_ge(s["sg_ready"], KH * g + m + 1)
                        dve.scalar_tensor_tensor(out=full[:, m % 2], in0=hb[:, 2 * (m % 2) + 1],
                                                 scalar=sc[:, 1, m:m + 1], in1=full[:, m % 2], op0=ALU.mult,
                                                 op1=ALU.mult).then_inc(s["ab_done"], 1)
                        dve.drain()
                        split(h[:, 0, m], full[:, m % 2]).then_inc(s["ab_split"], 1)
                    for layer in range(2):
                        for m in range(KH):
                            dve.drain()
                            dve.wait_ge(s["full_ready"], 2 * KH * g + KH * layer + m + 1)
                            split(h[:, 1 - layer, m], full[:, m % 2]).then_inc(s["h_split"], 1)
                            if not (isinstance(g, int) and g == 0) and layer == 0:
                                if m == 1:
                                    norm_stats()
                                if m == 3:
                                    norm(g - 1)
                    if not (isinstance(g, int) and g == G - 1):
                        split_x(g + 1)
                    for st in range(GT):
                        dve.wait_ge(s["acc_ready"], GT * g + st + 1)
                        dve.tensor_tensor(r[:, st], acc[:, st % 2, 0:D], s3[:], ALU.mult)\
                           .then_inc(s["acc_done"], 1)
                    dve.drain()
                    dve.tensor_tensor(r[:], r[:], X[:, ds(g * GT, GT), :], ALU.add)

                split_x(0)
                one(0)
                with dve.Fori(1, G - 1) as g:
                    one(g)
                one(G - 1)
                norm_stats()
                norm(G - 1)


def decoder(nc, a, y, scr):
    with ExitStack() as stack:
        c = Ctx(nc, stack)
        glob = {"X": c.sb("X", [P, NT, D]), "ident": c.sb("ident", [P, P]), "mhalf": c.sb("mhalf", [P, 1]),
                "eps": c.sb("eps", [P, 1])}
        glob["x_loaded"], = c.sems("x_loaded")
        with ExitStack() as att:
            ca = Ctx(nc, att)
            glob["ATT"] = ca.sb("ATT", [P, B * NH, N // P, HD])
            glob["V"] = ca.sb("V", [P, B * NH, N // P, HD + 1])
            self_attention_qkv(nc, glob, a, scr)
            self_attention_heads(nc, glob, scr)
            attention_out(nc, glob, a)
        cross_attention(nc, glob, a, scr, True)
        mixture_of_experts(nc, glob, a)
        delta_rule(nc, glob, a)
        glob["mlp_w"] = c.sb("mlp_w", [P, NW], F32R)
        glob["mlp_raw"] = c.sb("mlp_raw", [P, 2 * KH * P])
        glob["mlp_loaded"], = c.sems("mlp_loaded")
        cross_attention(nc, glob, a, scr, False)
        gated_mlp(nc, glob, a, y)


def layouts(i, np):
    def t(a):
        return np.ascontiguousarray(a.T)

    def cols(v, k):
        return np.ascontiguousarray(v.reshape(k, P).T)

    o = {}
    x = i["x"].reshape(T, D)
    o["x"] = x
    o["xT"] = t(x)
    o["ctxT"] = np.ascontiguousarray(i["ctx_1024"].reshape(B * S, D).T)
    o["w1"] = np.stack([i[f"L0_attn_{q}_w1"] for q in "qkv"])
    o["w2"] = np.stack([i[f"L0_attn_{q}_w2"] for q in "qkv"])
    o["b1"] = np.stack([cols(i[f"L0_attn_{q}_b1"], KH) for q in "qkv"])
    o["b2qk"] = np.stack([cols(i[f"L0_attn_{q}_b2"], KD) for q in "qk"], axis=1)
    o["b2v"] = i["L0_attn_v_b2"].reshape(1, D)
    o["proj_w"] = i["L0_attn_proj_w"]
    o["proj_b"] = i["L0_attn_proj_b"].reshape(1, D)
    o["WkT"], o["WvT"] = t(i["L0_xattn_Wk"]), t(i["L0_xattn_Wv"])
    order = [8 * (rt // 4) + rt % 4 + 4 * half for rt in range(KH) for half in range(2)]
    o["WqR"] = np.ascontiguousarray(i["L0_xattn_Wq"].reshape(NH, 64, D)[order].reshape(HID, D))
    o["WoR"] = np.ascontiguousarray(i["L0_xattn_Wo"].T.reshape(NH, 64, D)[order].reshape(HID, D))
    o["gate_wT"] = t(i["L0_ffn_gate_w"])
    shared = [np.ascontiguousarray(i[f"L0_ffn_sw_{n}"].reshape(D, 2, F).transpose(1, 0, 2)) for n in ("gate", "up")]
    o["w_gu"] = np.ascontiguousarray(np.stack([np.concatenate([i["L0_ffn_w_gate"], shared[0]]),
                                               np.concatenate([i["L0_ffn_w_up"], shared[1]])], axis=1))
    o["w_dn"] = np.concatenate([i["L0_ffn_w_down"], i["L0_ffn_sw_down"].reshape(2, F, D)])
    o["ln_w"], o["ln_b"] = i["L1_attn_ln_w"].reshape(1, D), i["L1_attn_ln_b"].reshape(1, D)
    ws = i["L1_attn_w_slow"].reshape(D, NH, 3 * 64 + 1)
    o["w_slow"] = np.concatenate([np.ascontiguousarray(ws[:, :, 64 * j:64 * j + 64]).reshape(D, HID)
                                  for j in range(3)] + [np.ascontiguousarray(ws[:, :, 192])], axis=1)
    o["w_out"] = i["L1_attn_w_out"]
    o["WcT"] = t(i["L1_xattn_w_concat"])
    for n in ("w1", "w2", "h1", "h2", "w3"):
        o[n + "T"] = t(i[f"L1_ffn_{n}_w"])
    o["mlp_shares"] = np.concatenate([i[f"L1_ffn_{n}_w"].reshape(-1) for n in ("w1", "w2", "h1", "h2", "w3")]
                                     ).reshape(NT, P, WCH)
    o["scales"] = np.stack([cols(i[f"L1_ffn_{n}_s"], KH) for n in ("w1", "w2", "h1", "h2")], axis=1)
    o["w3_s"] = i["L1_ffn_w3_s"].reshape(1, D)
    return o


def kernel(**inputs):
    import numpy as _np
    import concourse.bacc as _bacc
    from concourse import mybir as _mybir
    from concourse.bass_utils import run_bass_kernel_spmd as _run

    nc = _bacc.Bacc("TRN2", target_bir_lowering=False, num_devices=1)
    laid = layouts({k: _np.asarray(v) for k, v in inputs.items()}, _np)
    arrays, args = {}, {}
    for name, a in laid.items():
        a = _np.ascontiguousarray(a)
        arrays[f"in_{name}_dram"] = a
        args[name] = nc.dram_tensor(f"in_{name}_dram", a.shape, _mybir.dt.from_np(a.dtype),
                                    kind="ExternalInput").ap()
    y = nc.dram_tensor("out_0_dram", (T, D), _mybir.dt.float32, kind="ExternalOutput").ap()
    scr = {"qk": nc.dram_tensor("scr_qk", (2, 2, B * D, N), _mybir.dt.float32, kind="Internal").ap(),
           "vals": nc.dram_tensor("scr_vals", (B, FL, D), _mybir.dt.float32, kind="Internal").ap()}
    decoder(nc, args, y, scr)
    r = _run(nc, [arrays], core_ids=[0])
    return r.results[0]["out_0_dram"].reshape(B, N, D)
```

```python
from contextlib import ExitStack

import concourse.bass as bass
from concourse import mybir

F32 = mybir.dt.float32
F32R = mybir.dt.float32r
U32 = mybir.dt.uint32
ALU = mybir.AluOpType
ACT = mybir.ActivationFunctionType
AX = mybir.AxisListType
P = 128
B, N, D = 2, 1024, 256
T = B * N
NT = T // P
KD = D // P
G = 4
GT = NT // G
GW = T // G
NH = 16
HD = D // NH
HID = 1024
KH = HID // P
S = 77
FL = NH * S
FB = -(-FL // P)
E, F = 8, 352
NE = E + 2
EPS = 1e-5
ds = bass.ds
NAB, NWH, NW3 = 2 * KD * HID, 2 * KH * HID, KH * D
NW = NAB + NWH + NW3
WCH = NW // NT
FULL_BITS = (1 << 12) - 1


class Ctx:

    def __init__(self, nc, stack):
        self.nc, self.stack = nc, stack

    def sb(self, name, shape, dt=F32):
        return self.stack.enter_context(self.nc.sbuf_tensor(name, shape, dt))

    def ps(self, name, shape, dt=F32):
        return self.stack.enter_context(self.nc.psum_tensor(name, shape, dt))

    def sems(self, *names):
        return [self.stack.enter_context(self.nc.semaphore(n)) for n in names]


def ring(per_loop, i, j, depth):
    return per_loop * i + max(0, j - depth + 1)


def self_attention_qkv(nc, glob, w, scr):
    with ExitStack() as stack:
        c = Ctx(nc, stack)
        xT = c.sb("qkv_xT", [P, KD, T])
        w1 = c.sb("qkv_w1", [P, 3, KD, HID])
        w2 = c.sb("qkv_w2", [P, 3, KH, D])
        b1 = c.sb("qkv_b1", [P, 3, KH])
        b2 = c.sb("qkv_b2", [P, 2, KD])
        b2v = c.sb("qkv_b2v", [P, D])
        hid = c.sb("qkv_hid", [P, 3, KH, GW])
        full = c.sb("qkv_full", [P, GW])
        parts = c.sb("qkv_parts", [P, 2, 2, GW], F32R)
        hb = c.ps("qkv_hb", [P, 4, 512])
        ob = c.ps("qkv_ob", [P, 2, 512])
        br_loaded = c.sems("a_q_loaded", "a_k_loaded", "a_v_loaded")
        rest_loaded, = c.sems("a_x_rest_loaded")
        loaded, h_ready, h_done, o_ready, o_done, parts_ready, st0, st1 = c.sems(
            "a_x_loaded", "a_h_ready", "a_h_done", "a_o_ready", "a_o_done", "a_parts_ready", "a_st0", "a_st1")
        stored = [st0, st1]
        V = glob["V"]
        with nc.Block() as block:
            @block.sync
            def _(sp):
                xTd = w["xT"].rearrange("(k p) t -> p k t", p=P)
                sp.dma_start(xT[:, :, 0:GW], xTd[:, :, 0:GW]).then_inc(loaded, 16)
                for br in range(3):
                    sp.dma_start(w1[:, br], w["w1"][br].rearrange("(k p) n -> p k n", p=P)).then_inc(br_loaded[br], 16)
                    sp.dma_start(b1[:, br], w["b1"][br]).then_inc(br_loaded[br], 16)
                    sp.dma_start(w2[:, br], w["w2"][br].rearrange("(k p) n -> p k n", p=P)).then_inc(br_loaded[br], 16)
                    if br < 2:
                        sp.dma_start(b2[:, br], w["b2qk"][:, br]).then_inc(br_loaded[br], 16)
                    else:
                        sp.dma_start(b2v[:], w["b2v"].to_broadcast([P, D])).then_inc(br_loaded[br], 16)
                sp.dma_start(xT[:, :, GW:T], xTd[:, :, GW:T]).then_inc(rest_loaded, 16)
                sp.dma_start(glob["X"][:], w["x"].rearrange("(t p) d -> p t d", p=P)).then_inc(glob["x_loaded"], 16)
                with sp.Fori(0, B) as b:
                    for half in range(2):
                        for j in range(4):
                            br, mt = j // 2, j % 2
                            sp.wait_ge(parts_ready, 8 * b + 4 * half + j + 1)
                            sp.dma_start(
                                scr["qk"][br, :, ds(b * D + mt * P, P), half * 512:half * 512 + 512]
                                .rearrange("l r n -> r l n"), parts[:, j % 2].bitcast(F32)).then_inc(stored[j % 2], 16)
                for q in stored:
                    sp.wait_ge(q, 16 * 2 * G)
                sp.wait_ge(glob["x_loaded"], 16)

            @block.tensor
            def _(pe):
                pe.wait_ge(loaded, 16)
                with pe.Fori(0, G) as t:
                    def up(br):
                        pe.wait_ge(br_loaded[br], 64)
                        if br == 2:
                            pe.wait_ge(rest_loaded, 16)
                        for m in range(KH):
                            j = br * KH + m
                            pe.wait_ge(h_done, ring(3 * KH, t, j, 4))
                            for k in range(KD):
                                mm = pe.matmul(hb[:, j % 4], w1[:, br, k, m * P:m * P + P],
                                               xT[:, k, ds(t * GW, GW)], start=k == 0, stop=k == KD - 1)
                            mm.then_inc(h_ready, 1)

                    def down(br):
                        pe.wait_ge(h_done, 3 * KH * t + (br + 1) * KH)
                        for u in range(2 if br < 2 else GT):
                            j = 2 * br + u
                            pe.wait_ge(o_done, ring(8, t, j, 2))
                            for k in range(KH):
                                if br < 2:
                                    mm = pe.matmul(ob[:, j % 2], w2[:, br, k, u * P:u * P + P],
                                                   hid[:, br, k], start=k == 0, stop=k == KH - 1)
                                else:
                                    mm = pe.matmul(ob[:, j % 2, 0:D], hid[:, br, k, u * P:u * P + P],
                                                   w2[:, br, k], start=k == 0, stop=k == KH - 1)
                            mm.then_inc(o_ready, 1)

                    up(0)
                    up(1)
                    down(0)
                    up(2)
                    down(1)
                    down(2)

            @block.scalar
            def _(act):
                with act.Fori(0, G) as t:
                    for j in range(3 * KH):
                        br, m = j // KH, j % KH
                        if m == 0:
                            act.wait_ge(br_loaded[br], 64)
                        act.wait_ge(h_ready, 3 * KH * t + j + 1)
                        act.activation(hid[:, br, m], hb[:, j % 4], ACT.Gelu,
                                       bias=b1[:, br, m:m + 1]).then_inc(h_done, 1)

            @block.vector
            def _(dve):
                dve.memset(V[:, :, :, HD:HD + 1], 1.0)
                with dve.Fori(0, G) as t:
                    for j in range(8):
                        if j in (0, 2, 4):
                            dve.wait_ge(br_loaded[j // 2], 64)
                        if j < 4:
                            br, mt = j // 2, j % 2
                            dve.drain()
                            dve.wait_ge(o_ready, 8 * t + j + 1)
                            dve.tensor_scalar(full[:], ob[:, j % 2], b2[:, br, mt:mt + 1], None,
                                              ALU.add).then_inc(o_done, 1)
                            dve.drain()
                            dve.wait_ge(stored[j % 2], 16 * (2 * t + j // 2))
                            dve.tensor_copy(parts[:, j % 2, 0], full[:])
                            dve.drain()
                            dve.tensor_tensor(parts[:, j % 2, 1], full[:], parts[:, j % 2, 0].bitcast(F32),
                                              ALU.subtract).then_inc(parts_ready, 1)
                        else:
                            dve.wait_ge(o_ready, 8 * t + j + 1)
                            v = V[:, ds(t // 2 * NH, NH), ds(t % 2 * GT + j - 4, 1), 0:HD].rearrange("p h a d -> p (h a) d")
                            dve.tensor_tensor(v, ob[:, j % 2, 0:D].rearrange("p (h d) -> p h d", h=NH),
                                              b2v[:].rearrange("p (h d) -> p h d", h=NH),
                                              ALU.add).then_inc(o_done, 1)

            @block.gpsimd
            def _(pool):
                pool.memset(glob["ident"][:], 0.0)
                pool.drain()
                pool.affine_select(out=glob["ident"][:], in_=glob["ident"][:], compare_op=ALU.not_equal,
                                   fill=1.0, base=0, pattern=[[-1, P]], channel_multiplier=1)
                pool.memset(glob["mhalf"][:], -0.5)
                pool.memset(glob["eps"][:], EPS)


def self_attention_heads(nc, glob, scr):
    NQ = N // P
    VR = 66
    VC = HD + 1
    SB = 3
    LAG = 4
    LEAD = 8
    KR = 4 * HD + 2
    NLD = 16 * 9
    with ExitStack() as stack:
        c = Ctx(nc, stack)
        qs = c.sb("at_qs", [KR, SB, N], F32R)
        ks = c.sb("at_ks", [KR, SB, N], F32R)
        zero = c.sb("at_zero", [2, N], F32R)
        vs = c.sb("at_vs", [P, SB, NQ - 1, VR], F32R)
        vs7 = c.sb("at_vs7", [P, SB, VR])
        pfull = c.sb("at_pfull", [P, NQ - 1, 512])
        pfull7 = c.sb("at_pfull7", [P, 2, 512])
        phi = c.sb("at_phi", [P, 2, NQ - 1, 512], F32R)
        plo = c.sb("at_plo", [P, 2, NQ - 1, 512], F32R)
        olo = c.sb("at_olo", [P, NQ, VC])
        osum = c.sb("at_osum", [P, NQ, VC])
        mx = c.sb("at_mx", [P, SB, NQ, 2])
        nm = c.sb("at_nm", [P, NQ])
        nmp = c.sb("at_nmp", [NQ, 2, P], F32R)
        outT = c.sb("at_outT", [2 * VC, 2, 512])
        rc = c.sb("at_rc", [P, NQ, 1])
        s1 = c.ps("at_s1", [P, SB, 512])
        s2 = c.ps("at_s2", [P, 2, 512])
        pv = c.ps("at_pv", [P, 2, 512])
        turned = c.ps("at_turned", [P, 512])
        ld = c.sems(*[f"b_ld{i}" for i in range(SB)])
        mrow = c.sems(*[f"b_mrow{i}" for i in range(SB)])
        (s1_ready, s1_done, s2_ready, p_ready, v_ready, pv_ready, out_ready, to_ready,
         to_done, nm_ready, tm_ready, nmp_ready, const_ready, lo_pool, lo_dve) = c.sems(
            "b_s1_ready", "b_s1_done", "b_s2_ready", "b_p_ready",
            "b_v_ready", "b_pv_ready", "b_out_ready", "b_to_ready", "b_to_done", "b_nm_ready", "b_tm_ready",
            "b_nmp_ready", "b_const_ready", "b_lo_pool", "b_lo_dve")
        V, ATT, ident = glob["V"], glob["ATT"], glob["ident"]
        NB = B * NH

        to = turned[:, 0:NQ * 2 * VC].rearrange("p (k c) -> p k c", c=2 * VC)
        tm = turned[0:NQ, NQ * 2 * VC:NQ * 2 * VC + P]

        def heads(eng, one):
            one((0, 0, 0))
            with eng.Fori(0, (NB - 3) // SB) as i:
                for k in range(1, SB + 1):
                    one((SB * i + k, k % SB, i + k // SB))
            for n in range(1 + (NB - 3) // SB * SB, NB):
                one((n, n % SB, n // SB))

        def after(h, d):
            n, q, r = h
            if isinstance(n, int) and n + d >= NB:
                return None
            return n + d, (q + d) % SB, r + (q + d) // SB

        def first(h):
            return isinstance(h[0], int) and h[0] == 0

        def row_at(h, s):
            a = after(h, 1 + (s + LEAD) // 16)
            return (a, (s + LEAD) % 16) if a else None

        with nc.Block() as block:
            @block.sync
            def _(sp):
                def load(n, p):
                    for part in range(2):
                        for k in (part, part + 2):
                            sp.dma_start(qs[k * HD:(k + 1) * HD, p].bitcast(F32),
                                         scr["qk"][0, part, ds(n * HD, HD), :]).then_inc(ld[p], 16)
                        for k in (2 * part, 2 * part + 1):
                            sp.dma_start(ks[k * HD:(k + 1) * HD, p].bitcast(F32),
                                         scr["qk"][1, part, ds(n * HD, HD), :]).then_inc(ld[p], 16)
                    if isinstance(n, int) and n == 0:
                        sp.wait_ge(const_ready, 1)
                    sp.dma_start(qs[4 * HD:KR, p].bitcast(F32), zero[:].bitcast(F32)).then_inc(ld[p], 16)

                def maxima(n, p):
                    sp.wait_ge(nmp_ready, n + 1)
                    for part in range(2):
                        sp.dma_start(qs[4 * HD + part:4 * HD + part + 1, p].bitcast(F32)
                                     .rearrange("a (q r) -> a q r", r=P), nmp[:, part, :].bitcast(F32)).then_inc(mrow[p], 16)

                def one(n, q):
                    maxima(n + 1, (q + 1) % SB)
                    sp.wait_ge(s2_ready, 16 * (n + 1))
                    load(n + SB, q)

                for n in range(SB):
                    load(n, n)
                maxima(0, 0)
                with sp.Fori(0, (NB - SB) // SB) as i:
                    for q in range(SB):
                        one(SB * i + q, q)
                for n in range((NB - SB) // SB * SB, NB - SB):
                    one(n, n % SB)
                for n in range(NB - SB, NB - 1):
                    maxima(n + 1, (n + 1) % SB)

            @block.tensor
            def _(pe):
                pe.wait_ge(const_ready, 1)

                def score_rows(h, u):
                    n, q, r = h
                    qt, kh, bank = u // 2, u % 2, (q + u) % SB
                    if u == 0:
                        pe.wait_ge(ld[q], NLD * (r + 1))
                    if not first(h):
                        pe.wait_ge(s1_done, 16 * n + u - SB + 1)
                    elif u >= SB:
                        pe.wait_ge(s1_done, u - SB + 1)
                    pe.matmul(s1[:, bank], qs[:, q, qt * P:qt * P + P], ks[:, q, kh * 512:kh * 512 + 512],
                              start=True, stop=True).then_inc(s1_ready, 1)

                def score_cols(h, s):
                    n, q, r = h
                    qh, kt = s // NQ, s % NQ
                    if s == 0:
                        pe.wait_ge(mrow[q], 32 * (r + 1))
                    if not first(h):
                        pe.wait_ge(p_ready, 16 * n + s - 1)
                    elif s >= 2:
                        pe.wait_ge(p_ready, s - 1)
                    pe.matmul(s2[:, s % 2], ks[:, q, kt * P:kt * P + P], qs[:, q, qh * 512:qh * 512 + 512],
                              start=True, stop=True).then_inc(s2_ready, 1)

                def turn_maxima(h):
                    pe.wait_ge(nm_ready, h[0] + 1)
                    if not isinstance(h[0], int) or h[0] > 1:
                        pe.wait_ge(to_done, h[0] - 1)
                    pe.transpose(tm, nm[:], ident[:]).then_inc(tm_ready, 1)

                def may_turn_out(n):
                    pe.wait_ge(out_ready, 2 * n + 2)
                    pe.wait_ge(nmp_ready, NB if isinstance(n, int) and n == NB - 1 else n + 2)

                def turn_out():
                    for k in range(NQ):
                        t = pe.transpose(to[:, k], outT[:, k // 4, k % 4 * P:k % 4 * P + P],
                                         ident[0:2 * VC, 0:2 * VC])
                    t.then_inc(to_ready, 1)

                def values(h, s):
                    n, q, r = h
                    qh, kt = s // NQ, s % NQ
                    pe.wait_ge(p_ready, 16 * n + s + 1)
                    if s == 0:
                        pe.wait_ge(v_ready, n + 1)
                    if kt == 0 and not (first(h) and qh == 0):
                        pe.wait_ge(out_ready, 2 * n + qh - 1)
                    if kt == NQ - 1:
                        pe.matmul(pv[0:VR, qh], vs7[:, q], pfull7[:, qh], start=False, stop=True)\
                          .then_inc(pv_ready, 1)
                    else:
                        pe.matmul(pv[0:VR, qh], vs[:, q, kt], phi[:, qh, kt], start=kt == 0, stop=False)
                        if kt == 0:
                            pe.wait_ge(lo_dve, 2 * n + qh + 1)
                        else:
                            pe.wait_ge(lo_pool, 6 + 12 * n + 6 * qh + kt)
                        pe.matmul(pv[0:VR, qh], vs[:, q, kt], plo[:, qh, kt], start=False, stop=False)

                def one(h):
                    following = after(h, 1)
                    for s in range(LAG, 16 + LAG):
                        if s < 16:
                            score_cols(h, s)
                        elif following:
                            score_cols(following, s - 16)
                        row = row_at(h, s)
                        if row:
                            score_rows(*row)
                        if s == 18 - LEAD and following:
                            turn_maxima(following)
                        if s == 7 and not first(h):
                            may_turn_out(h[0] - 1)
                        values(h, s - LAG)
                        if s == 7 and not first(h):
                            turn_out()

                for u in range(16):
                    score_rows((0, 0, 0), u)
                turn_maxima((0, 0, 0))
                for u in range(LAG + LEAD):
                    score_rows((1, 1, 0), u)
                for u in range(LAG):
                    score_cols((0, 0, 0), u)
                heads(pe, one)
                may_turn_out(NB - 1)
                turn_out()

            @block.scalar
            def _(act):
                act.preload_act_table(ACT.Exp)
                with act.Fori(0, NB) as n:
                    for s in range(16):
                        qh, kt = s // NQ, s % NQ
                        full = pfull7[:, qh] if kt == NQ - 1 else pfull[:, kt]
                        if kt == 0:
                            act.wait_ge(pv_ready, 2 * n + qh)
                            act.wait_ge(lo_dve, 2 * n + qh)
                        elif kt < NQ - 1:
                            act.wait_ge(lo_pool, 12 * n + 6 * qh + kt)
                        act.wait_ge(s2_ready, 16 * n + s + 1)
                        a = act.activation(full, s2[:, s % 2], ACT.Exp, scale=float(HD) ** -0.5)
                        if kt < NQ - 1:
                            a = act.activation(phi[:, qh, kt], s2[:, s % 2], ACT.Exp, scale=float(HD) ** -0.5)
                        a.then_inc(p_ready, 1)

            @block.vector
            def _(dve):
                dve.memset(zero[:].bitcast(mybir.dt.uint32), 0)
                dve.memset(ks[4 * HD:KR].bitcast(F32), 1.0).then_inc(const_ready, 1)
                dve.memset(vs[:].bitcast(F32), 0.0)
                dve.memset(vs7[:], 0.0)
                dve.drain()

                def row_max(h, u):
                    n, q, r = h
                    dve.wait_ge(s1_ready, 16 * n + u + 1)
                    dve.reduce_max(mx[:, q, u // 2, u % 2:u % 2 + 1], s1[:, (q + u) % SB], AX.X)\
                       .then_inc(s1_done, 1)

                def head_max(h):
                    dve.drain()
                    dve.tensor_reduce(nm[:], mx[:, h[1]], AX.X, ALU.max, negate=True).then_inc(nm_ready, 1)

                def split_max(h):
                    n, q, r = h
                    dve.wait_ge(tm_ready, n + 1)
                    if not first(h):
                        dve.wait_ge(mrow[(q - 1) % SB], 32 * (r + (1 if q else 0)))
                    dve.tensor_copy(nmp[:, 0], tm)
                    dve.drain()
                    dve.tensor_tensor(nmp[:, 1], tm, nmp[:, 0].bitcast(F32), ALU.subtract)\
                       .then_inc(nmp_ready, 1)

                def copy_out(n, qh):
                    if not isinstance(n, int) or n:
                        dve.wait_ge(to_ready, n)
                    dve.wait_ge(pv_ready, 2 * n + qh + 2)
                    dve.tensor_copy(outT[:, qh], pv[0:2 * VC, qh]).then_inc(out_ready, 1)

                def normalise(n):
                    dve.wait_ge(to_ready, n + 1)
                    dve.tensor_copy(olo[:], to[:, :, VC:2 * VC])
                    dve.drain()
                    dve.tensor_tensor(osum[:], to[:, :, 0:VC], olo[:], ALU.add).then_inc(to_done, 1)
                    dve.drain()
                    dve.reciprocal(rc[:], osum[:, :, HD:VC])
                    dve.drain()
                    dve.tensor_tensor(ATT[:, ds(n, 1)].rearrange("p a k d -> p (a k) d"),
                                      osum[:, :, 0:HD], rc[:].to_broadcast([P, NQ, HD]), ALU.mult)

                def low_part(h, qh):
                    dve.wait_ge(p_ready, 16 * h[0] + NQ * qh + 1)
                    dve.tensor_tensor(plo[:, qh, 0], pfull[:, 0], phi[:, qh, 0].bitcast(F32), ALU.subtract)\
                       .then_inc(lo_dve, 1)

                def take_v(h):
                    n, q, r = h
                    if not (isinstance(n, int) and n < SB):
                        dve.wait_ge(pv_ready, 2 * (n - SB) + 3)
                    v = V[:, ds(n, 1)].rearrange("p a k d -> p (a k) d")
                    dve.tensor_copy(vs[:, q, :, 0:VC], v[:, 0:NQ - 1])
                    dve.tensor_copy(vs7[:, q, 0:VC], v[:, NQ - 1])
                    dve.drain()
                    dve.tensor_tensor(vs[:, q, :, VC:2 * VC], v[:, 0:NQ - 1],
                                      vs[:, q, :, 0:VC].bitcast(F32), ALU.subtract).then_inc(v_ready, 1)

                def one(h):
                    following = after(h, 1)
                    for s in range(LAG, 16 + LAG):
                        if s == 5 and not first(h):
                            copy_out(h[0] - 1, 1)
                        if s == 9 and not first(h):
                            normalise(h[0] - 1)
                        if s == 10:
                            low_part(h, 1)
                        if s == 13:
                            copy_out(h[0], 0)
                        if following:
                            if s == 16 - LEAD:
                                head_max(following)
                            if s == 19 - LEAD:
                                split_max(following)
                            if s == 15:
                                take_v(following)
                            if s == 18:
                                low_part(following, 0)
                        row = row_at(h, s)
                        if row:
                            row_max(*row)

                for u in range(16):
                    row_max((0, 0, 0), u)
                head_max((0, 0, 0))
                take_v((0, 0, 0))
                split_max((0, 0, 0))
                for u in range(LAG + LEAD):
                    row_max((1, 1, 0), u)
                low_part((0, 0, 0), 0)
                heads(dve, one)
                copy_out(NB - 1, 1)
                normalise(NB - 1)

            @block.gpsimd
            def _(pool):
                pool.sem_inc(lo_pool, 6)
                pool.sem_inc(pv_ready, 1)
                with pool.Fori(0, NB) as n:
                    for qh in range(2):
                        for kt in range(1, NQ - 1):
                            pool.wait_ge(p_ready, 16 * n + NQ * qh + kt + 1)
                            pool.tensor_tensor(plo[:, qh, kt], pfull[:, kt], phi[:, qh, kt].bitcast(F32),
                                               ALU.subtract).then_inc(lo_pool, 1)


def turn_group(pe, s, g, xs, tb, ident, used=0, per=2):
    pe.wait_ge(s["xs_ready"], g + 1)
    for k in range(KD):
        pe.wait_ge(s["tb_done"], ring(per, g, k, 2))
        for st in range(GT):
            t = pe.transpose(tb[:, k, st * P:st * P + P], xs[:, st, k * P:k * P + P], ident[:])
        t.then_inc(s["tb_ready"], 1)


def stage_group(pool, s, g, xs, src, per=2):
    pool.wait_ge(s["tb_ready"], per * g)
    pool.tensor_copy(xs[:], src[:, ds(g * GT, GT), :]).then_inc(s["xs_ready"], 1)


def rstd_group(pool, s, n, mv, rstd, glob, k):
    eps, mhalf = glob["eps"], glob["mhalf"]
    pool.wait_ge(s["mv_ready"], n)
    pool.tensor_tensor(rstd[:], mv[:, :, 1], eps[:].to_broadcast([P, k]), ALU.add)
    pool.drain()
    pool.tensor_tensor(rstd[:], rstd[:], mhalf[:].to_broadcast([P, k]), ALU.pow).then_inc(s["rstd_ready"], 1)


def stats(dve, s, r, st6, mv, k):
    dve.drain()
    for i in range(k):
        dve.bn_stats(st6[:, i], r(i))
    dve.drain()
    for i in range(k):
        a = dve.bn_aggr(mv[:, i], st6[:, i])
    a.then_inc(s["mv_ready"], 1)


def attention_out(nc, glob, w):
    with ExitStack() as stack:
        c = Ctx(nc, stack)
        xs = c.sb("c_xs", [P, GT, D])
        xT = c.sb("c_xT", [P, KD, GW])
        pw = c.sb("c_pw", [P, KD, D])
        pb = c.sb("c_pb", [P, D])
        r = c.sb("c_r", [P, GT, D])
        st6 = c.sb("c_st6", [P, GT, 6])
        mv = c.sb("c_mv", [P, GT, 2])
        rstd = c.sb("c_rstd", [P, GT])
        tb = c.ps("c_tb", [P, 2, 512])
        acc = c.ps("c_acc", [P, 4, 512])
        names = ["loaded", "xs_ready", "tb_ready", "tb_done", "acc_ready", "acc_done", "mv_ready", "rstd_ready"]
        s = dict(zip(names, c.sems(*["c_" + n for n in names])))
        X, ident = glob["X"], glob["ident"]
        with nc.Block() as block:
            @block.sync
            def _(sp):
                sp.dma_start(pw[:], w["proj_w"].rearrange("(k p) n -> p k n", p=P)).then_inc(s["loaded"], 16)
                sp.dma_start(pb[:], w["proj_b"].to_broadcast([P, D])).then_inc(s["loaded"], 16)

            @block.gpsimd
            def _(pool):
                def stage(g):
                    pool.wait_ge(s["tb_ready"], KD * g)
                    for st in range(GT):
                        a = pool.tensor_copy(xs[:, st].rearrange("p (h d) -> p h d", d=HD),
                                             glob["ATT"][:, ds(g // 2 * NH, NH), ds(g % 2 * GT + st, 1)]
                                             .rearrange("p h a d -> p (h a) d"))
                    a.then_inc(s["xs_ready"], 1)

                stage(0)
                stage(1)
                with pool.Fori(0, G - 2) as g:
                    rstd_group(pool, s, g + 1, mv, rstd, glob, GT)
                    stage(g + 2)
                rstd_group(pool, s, G - 1, mv, rstd, glob, GT)
                rstd_group(pool, s, G, mv, rstd, glob, GT)

            @block.tensor
            def _(pe):
                pe.wait_ge(s["loaded"], 32)
                with pe.Fori(0, G) as g:
                    turn_group(pe, s, g, xs, tb, ident)
                    pe.wait_ge(s["tb_done"], 2 * g + 2)
                    for st in range(GT):
                        pe.wait_ge(s["acc_done"], GT * g)
                        for k in range(KD):
                            mm = pe.matmul(acc[:, st, 0:D], xT[:, k, st * P:st * P + P], pw[:, k],
                                           start=k == 0, stop=k == KD - 1)
                        mm.then_inc(s["acc_ready"], 1)

            @block.scalar
            def _(act):
                with act.Fori(0, G) as g:
                    for k in range(KD):
                        act.wait_ge(s["tb_ready"], KD * g + k + 1)
                        act.copy(xT[:, k], tb[:, k]).then_inc(s["tb_done"], 1)

            @block.vector
            def _(dve):
                dve.wait_ge(s["loaded"], 32)
                with dve.Fori(0, G) as g:
                    dve.drain()
                    for st in range(GT):
                        dve.wait_ge(s["acc_ready"], GT * g + st + 1)
                        dve.tensor_tensor(r[:, st], acc[:, st, 0:D], pb[:], ALU.add).then_inc(s["acc_done"], 1)
                    dve.drain()
                    dve.tensor_tensor(r[:], r[:], X[:, ds(g * GT, GT), :], ALU.add)
                    stats(dve, s, lambda i: r[:, i], st6, mv, GT)
                    dve.wait_ge(s["rstd_ready"], g + 1)
                    for st in range(GT):
                        dve.tensor_scalar(X[:, ds(g * GT + st, 1), :].rearrange("p a d -> p (a d)"), r[:, st],
                                          mv[:, st, 0:1], rstd[:, st:st + 1], ALU.subtract, ALU.mult)


def mlp_weights(tile):
    return (tile[:, 0:NAB].rearrange("p (i k n) -> p i k n", i=2, k=KD),
            tile[:, NAB:NAB + NWH].rearrange("p (i k n) -> p i k n", i=2, k=KH),
            tile[:, NAB + NWH:NW].rearrange("p (k n) -> p k n", k=KH))


def load_mlp_weights(pool, glob, w, g):
    wab, wh, w3 = mlp_weights(glob["mlp_w"])
    loads = [[(wab[:, 0], "w1T"), (wab[:, 1], "w2T")], [(wh[:, 0], "h1T")], [(wh[:, 1], "h2T")], [(w3, "w3T")]]
    for dst, name in loads[g]:
        pool.dma_start(dst, w[name].rearrange("(k p) n -> p k n", p=P)).then_inc(glob["mlp_loaded"], 16)


def cross_attention(nc, glob, w, scr, first):
    tag = "e" if first else "h"
    scale = 64.0 ** -0.5 if first else float(HD) ** -0.5
    with ExitStack() as stack:
        c = Ctx(nc, stack)
        keys = c.sb(tag + "_keys", [P, B, KD, FL])
        vals = c.sb(tag + "_vals", [P, B, FB, D])
        X, ident = glob["X"], glob["ident"]
        BS = B * S
        LAST = FL - (FB - 1) * P

        with ExitStack() as inner:
            d = Ctx(nc, inner)
            cT = d.sb(tag + "_cT", [P, KD, BS])
            loaded, kv_ready, kv_done, m_ready, m_done, o_ready, o_done, stored, back, zeroed = d.sems(
                *[tag + "p_" + n for n in ("loaded", "kv_ready", "kv_done", "m_ready", "m_done", "o_ready",
                                           "o_done", "stored", "back", "zeroed")])
            if first:
                wk = d.sb("e_wk", [P, KD, D])
                wv = d.sb("e_wv", [P, KD, D])
                wq = d.sb("e_wq", [P, KH, D])
                wo = d.sb("e_wo", [P, KH, D])
                kvT = d.sb("e_kvT", [P, 2, KD, BS])
                vstage = d.sb("e_vstage", [S, B, NH, D])
                kvb = d.ps("e_kvb", [P, 2, 512])
                mb = d.ps("e_mb", [P, 2, 512])
                vb = d.ps("e_vb", [P, 4, 512])
                def head(rt, half):
                    return 8 * (rt // 4) + rt % 4 + 4 * half
                with nc.Block() as block:
                    @block.sync
                    def _(sp):
                        sp.dma_start(cT[:], w["ctxT"].rearrange("(k p) n -> p k n", p=P)).then_inc(loaded, 16)
                        for dst, name in ((wk, "WkT"), (wv, "WvT"), (wq, "WqR"), (wo, "WoR")):
                            sp.dma_start(dst[:], w[name].rearrange("(k p) n -> p k n", p=P)).then_inc(loaded, 16)
                        sp.wait_ge(o_done, 2 * KH)
                        sp.dma_start(scr["vals"].rearrange("b (h s) d -> s b h d", s=S), vstage[:])\
                          .then_inc(stored, 16)
                        sp.wait_ge(stored, 16)
                        for b in range(B):
                            sp.dma_start(vals[:, b, 0:FB - 1], scr["vals"][b, 0:(FB - 1) * P]
                                         .rearrange("(k p) d -> p k d", p=P)).then_inc(back, 16)
                            sp.dma_start(vals[0:LAST, b, FB - 1], scr["vals"][b, (FB - 1) * P:FL])\
                              .then_inc(back, 16)
                        sp.wait_ge(back, 64)

                    @block.tensor
                    def _(pe):
                        pe.wait_ge(loaded, 80)
                        for kv, wt in enumerate((wk, wv)):
                            for mt in range(KD):
                                for k in range(KD):
                                    mm = pe.matmul(kvb[:, kv, mt * BS:(mt + 1) * BS], wt[:, k, mt * P:mt * P + P],
                                                   cT[:, k], start=k == 0, stop=k == KD - 1)
                            mm.then_inc(kv_ready, 1)
                        pe.wait_ge(kv_done, 2)
                        for rt in range(KH):
                            for half in range(2):
                                rows = slice(64 * half, 64 * half + 64)
                                tile = head(rt, half) // 8
                                j = 2 * rt + half
                                if j >= 2:
                                    pe.wait_ge(m_done, j - 1)
                                for k in range(KD):
                                    mm = pe.matmul(mb[:, half, k * BS:(k + 1) * BS], wq[rows, rt, k * P:k * P + P],
                                                   kvT[rows, 0, tile], start=True, stop=True)
                                mm.then_inc(m_ready, 1)
                                if j >= 4:
                                    pe.wait_ge(o_done, j - 3)
                                for b in range(B):
                                    mm = pe.matmul(vb[0:S, 2 * (rt % 2) + half, b * D:(b + 1) * D],
                                                   kvT[rows, 1, tile, b * S:(b + 1) * S], wo[rows, rt],
                                                   start=True, stop=True)
                                mm.then_inc(o_ready, 1)

                    @block.vector
                    def _(dve):
                        for kv in range(2):
                            dve.wait_ge(kv_ready, kv + 1)
                            dve.tensor_copy(kvT[:, kv], kvb[:, kv, 0:KD * BS].rearrange("p (k n) -> p k n", k=KD))\
                               .then_inc(kv_done, 1)
                        for j in range(2 * KH):
                            h = head(j // 2, j % 2)
                            dve.wait_ge(m_ready, j + 1)
                            for k in range(KD):
                                cp = dve.tensor_copy(keys[:, :, k, h * S:(h + 1) * S],
                                                     mb[:, j % 2, k * BS:(k + 1) * BS]
                                                     .rearrange("p (b s) -> p b s", b=B))
                            cp.then_inc(m_done, 1)

                    @block.scalar
                    def _(act):
                        for j in range(2 * KH):
                            h = head(j // 2, j % 2)
                            act.wait_ge(o_ready, j + 1)
                            act.copy(vstage[:, :, h], vb[0:S, 2 * (j // 2 % 2) + j % 2]
                                     .rearrange("p (b d) -> p b d", b=B)).then_inc(o_done, 1)
            else:
                wc = d.sb("h_wc", [P, KD, D])
                vb = d.ps("h_vb", [P, 2, 512])
                with nc.Block() as block:
                    @block.sync
                    def _(sp):
                        sp.dma_start(wc[:], w["WcT"].rearrange("(k p) n -> p k n", p=P)).then_inc(loaded, 16)
                        sp.wait_ge(zeroed, 1)
                        for h in range(NH):
                            r0 = (h % 8) * HD
                            sp.dma_start(keys[r0:r0 + HD, :, h // 8, h * S:(h + 1) * S],
                                         w["ctxT"][h * HD:(h + 1) * HD].rearrange("r (b s) -> r b s", b=B))\
                              .then_inc(loaded, 16)

                    @block.vector
                    def _(dve):
                        dve.memset(keys[:], 0.0).then_inc(zeroed, 1)
                        dve.memset(glob["mlp_raw"][:, 0:WCH].bitcast(U32), 0)
                        for j in range(B * FB):
                            b, blk = j // FB, j % FB
                            rows = P if blk < FB - 1 else LAST
                            dve.wait_ge(o_ready, j + 1)
                            dve.tensor_copy(vals[0:rows, b, blk], vb[0:rows, j % 2, 0:D]).then_inc(o_done, 1)

                    @block.tensor
                    def _(pe):
                        pe.wait_ge(loaded, 16 * (NH + 1))
                        for j in range(B * FB):
                            b, blk = j // FB, j % FB
                            rows = P if blk < FB - 1 else LAST
                            if j >= 2:
                                pe.wait_ge(o_done, j - 1)
                            for k in range(KD):
                                mm = pe.matmul(vb[0:rows, j % 2, 0:D], keys[:, b, k, blk * P:blk * P + rows],
                                               wc[:, k], start=k == 0, stop=k == KD - 1)
                            mm.then_inc(o_ready, 1)

        xs = c.sb(tag + "_xs", [P, GT, D])
        xT = c.sb(tag + "_xT", [P, KD, GW])
        pr = c.sb(tag + "_pr", [P, 2, FL])
        pT = c.sb(tag + "_pT", [P, FB, P])
        r = c.sb(tag + "_r", [P, GT, D])
        mx = c.sb(tag + "_mx", [P, 2, NH])
        sm = c.sb(tag + "_sm", [P, 2, NH])
        st6 = c.sb(tag + "_st6", [P, GT, 6])
        mv = c.sb(tag + "_mv", [P, GT, 2])
        rstd = c.sb(tag + "_rstd", [P, GT])
        sc = c.ps(tag + "_sc", [P, 3 * 512])
        tb = c.ps(tag + "_tb", [P, 2, 512])
        acc = c.ps(tag + "_acc", [P, 2, 512])
        names = ["xs_ready", "tb_ready", "tb_done", "s_ready", "d_ready", "e_ready", "p_ready",
                 "acc_ready", "acc_done", "mv_ready", "rstd_ready", "share_done"]
        s = dict(zip(names, c.sems(*[tag + "_" + n for n in names])))
        if not first:
            share = c.sb("h_share", [P, 2, WCH])
            share_ready = c.sems("h_share_ready0", "h_share_ready1")
            bits = glob["mlp_raw"][:, 0:WCH].bitcast(U32)
        NB3 = -(-FB // 4)
        PER = KD + GT * NB3
        if first:
            products = [[(a, min(a + 512, FL), k) for k in range(KD)] for a in range(0, FL, 512)]
        else:
            mid = FL // 2
            products = [[(0, 512, 0)], [(512, mid, 0)], [(mid, 1024, 1)], [(1024, FL, 1)]]
        with nc.Block() as block:
            @block.sync
            def _(sp):
                if not first:
                    with sp.Fori(0, NT // 2) as i:
                        for q in range(2):
                            sp.wait_ge(s["share_done"], 2 * i + q)
                            sp.dma_start(share[:, q], w["mlp_shares"][ds(2 * i + q, 1)]
                                         .rearrange("a p n -> p (a n)")).then_inc(share_ready[q], 16)

            @block.gpsimd
            def _(pool):
                def stage(g, turned):
                    if turned is not None:
                        pool.wait_ge(s["tb_ready"], turned)
                    pool.tensor_copy(xs[:], X[:, ds(g * GT, GT), :]).then_inc(s["xs_ready"], 1)

                stage(0, None)
                stage(1, KD)
                for g in range(G):
                    if not first:
                        load_mlp_weights(pool, glob, w, g)
                    rstd_group(pool, s, g + 1, mv, rstd, glob, GT)
                    if g < G - 2:
                        stage(g + 2, PER * (g + 1) + KD - NB3)

            def use(g, st, q):
                late = st == GT - 1 and not is_last(g)
                return KD + PER * g + NB3 * st + (KD if late else 0) + q

            def use_x(g, k):
                return k if isinstance(g, int) and g == 0 else KD + PER * (g - 1) + NB3 * (GT - 1) + k

            def bank(st, q, last):
                return (NB3 * st + (KD if st == GT - 1 and not last else 0) + q) % 2

            def x_bank(g, k):
                return k % 2 if is_first(g) else (NB3 * (GT - 1) + k) % 2

            def is_first(g):
                return isinstance(g, int) and g == 0

            def is_last(g):
                return isinstance(g, int) and g == G - 1

            @block.tensor
            def _(pe):
                def scores(g, st):
                    if st == 0:
                        pe.wait_ge(s["tb_done"], use_x(g, KD))
                    if not (is_first(g) and st == 0):
                        pe.wait_ge(s["d_ready"], GT * g + st)
                    for group in products:
                        for i, (a, z, k) in enumerate(group):
                            mm = pe.matmul(sc[:, a:z], xT[:, k, st * P:st * P + P],
                                           keys[:, ds(g // 2, 1), k, a:z].rearrange("p a n -> p (a n)"),
                                           start=i == 0, stop=i == len(group) - 1)
                    mm.then_inc(s["s_ready"], 1)

                def turn_x(g):
                    pe.wait_ge(s["xs_ready"], g + 1)
                    for k in range(KD):
                        if not is_first(g):
                            pe.wait_ge(s["tb_done"], use_x(g, k) - 1)
                        for st in range(GT):
                            tr = pe.transpose(tb[:, x_bank(g, k), st * P:st * P + P],
                                              xs[:, st, k * P:k * P + P], ident[:])
                        tr.then_inc(s["tb_ready"], 1)

                def weigh(g, st):
                    pe.wait_ge(s["p_ready"], GT * g + st + 1)

                    def blocks(q):
                        return range(4 * q, min(4 * q + 4, FB))

                    def turn(q):
                        pe.wait_ge(s["tb_done"], use(g, st, q) - 1)
                        for blk in blocks(q):
                            rows = P if blk < FB - 1 else LAST
                            tr = pe.transpose(tb[0:rows, bank(st, q, is_last(g)), (blk % 4) * P:(blk % 4) * P + P],
                                              pr[:, st % 2, blk * P:blk * P + rows], ident[:])
                        tr.then_inc(s["tb_ready"], 1)

                    turn(0)
                    turn(1)
                    pe.wait_ge(s["acc_done"], GT * g + st)
                    for q in range(NB3):
                        pe.wait_ge(s["tb_done"], use(g, st, q) + 1)
                        for blk in blocks(q):
                            rows = P if blk < FB - 1 else LAST
                            mm = pe.matmul(acc[:, st % 2, 0:D], pT[0:rows, blk],
                                           vals[0:rows, ds(g // 2, 1), blk].rearrange("p a n -> p (a n)"),
                                           start=blk == 0, stop=blk == FB - 1)
                        if q + 2 < NB3:
                            turn(q + 2)
                    mm.then_inc(s["acc_ready"], 1)

                def one(g):
                    for st in range(GT):
                        if st < GT - 1:
                            scores(g, st + 1)
                        elif not is_last(g):
                            turn_x(g + 1)
                            scores(g + 1, 0)
                        weigh(g, st)

                turn_x(0)
                scores(0, 0)
                with pe.Fori(0, G - 1) as g:
                    one(g)
                one(G - 1)

            @block.scalar
            def _(act):
                act.preload_act_table(ACT.Exp)

                def copy_x(g):
                    for k in range(KD):
                        act.wait_ge(s["tb_ready"], use_x(g, k) + 1)
                        act.copy(xT[:, k], tb[:, x_bank(g, k)]).then_inc(s["tb_done"], 1)

                def exps(g, st):
                    act.wait_ge(s["d_ready"], GT * g + st + 1)
                    act.activation(pr[:, st % 2], pr[:, st % 2], ACT.Exp, scale=scale)\
                       .then_inc(s["e_ready"], 1)

                def copy_probabilities(g, st):
                    for q in range(NB3):
                        at = bank(st, q, is_last(g))
                        act.wait_ge(s["tb_ready"], use(g, st, q) + 1)
                        if q < NB3 - 1:
                            act.copy(pT[:, 4 * q:4 * q + 4], tb[:, at].rearrange("p (a n) -> p a n", n=P))\
                               .then_inc(s["tb_done"], 1)
                        else:
                            full = (FB - 1) % 4
                            act.copy(pT[:, 4 * q:FB - 1], tb[:, at, 0:full * P].rearrange("p (a n) -> p a n", n=P))
                            act.copy(pT[0:LAST, FB - 1], tb[0:LAST, at, full * P:full * P + P])\
                               .then_inc(s["tb_done"], 1)

                def one(g):
                    for st in range(GT):
                        if st == GT - 1 and not is_last(g):
                            copy_x(g + 1)
                        copy_probabilities(g, st)
                        if st < GT - 1:
                            exps(g, st + 1)
                        elif not is_last(g):
                            exps(g + 1, 0)

                copy_x(0)
                exps(0, 0)
                with act.Fori(0, G - 1) as g:
                    one(g)
                one(G - 1)

            @block.vector
            def _(dve):
                def shift(g, st):
                    q = st % 2
                    dve.drain()
                    dve.wait_ge(s["s_ready"], GT * g + st + 1)
                    dve.tensor_reduce(mx[:, q], sc[:, 0:FL].rearrange("p (h s) -> p h s", s=S), AX.X, ALU.max)
                    dve.drain()
                    dve.tensor_tensor(pr[:, q].rearrange("p (h s) -> p h s", s=S),
                                      sc[:, 0:FL].rearrange("p (h s) -> p h s", s=S),
                                      mx[:, q].rearrange("p (h a) -> p h a", a=1).to_broadcast([P, NH, S]),
                                      ALU.subtract).then_inc(s["d_ready"], 1)

                def norm(g, st):
                    q = st % 2
                    dve.wait_ge(s["e_ready"], GT * g + st + 1)
                    e = pr[:, q].rearrange("p (h s) -> p h s", s=S)
                    dve.tensor_reduce(sm[:, q], e, AX.X, ALU.add)
                    dve.drain()
                    dve.reciprocal(sm[:, q], sm[:, q])
                    dve.drain()
                    dve.tensor_tensor(e, e, sm[:, q].rearrange("p (h a) -> p h a", a=1)
                                      .to_broadcast([P, NH, S]), ALU.mult).then_inc(s["p_ready"], 1)

                def residual(g, st):
                    dve.wait_ge(s["acc_ready"], GT * g + st + 1)
                    dve.tensor_tensor(r[:, st], acc[:, st % 2, 0:D],
                                      X[:, ds(g * GT + st, 1), :].rearrange("p a d -> p (a d)"),
                                      ALU.add).then_inc(s["acc_done"], 1)

                def group_stats():
                    stats(dve, s, lambda i: r[:, i], st6, mv, GT)

                def group_norm(g):
                    dve.wait_ge(s["rstd_ready"], g + 1)
                    for st in range(GT):
                        dve.tensor_scalar(X[:, ds(g * GT + st, 1), :].rearrange("p a d -> p (a d)"), r[:, st],
                                          mv[:, st, 0:1], rstd[:, st:st + 1], ALU.subtract, ALU.mult)

                def one(g):
                    for st in range(GT):
                        norm(g, st)
                        if st < GT - 1:
                            shift(g, st + 1)
                        elif not is_last(g):
                            shift(g + 1, 0)
                        if not first:
                            dve.wait_ge(share_ready[st % 2], 16 * (g * GT // 2 + st // 2 + 1))
                            dve.tensor_tensor(bits, bits, share[:, st % 2].bitcast(U32), ALU.bitwise_or)\
                               .then_inc(s["share_done"], 1)
                        if st:
                            if st == 1 and not is_first(g):
                                group_norm(g - 1)
                                dve.drain()
                            residual(g, st - 1)
                        elif not is_first(g):
                            residual(g - 1, GT - 1)
                            group_stats()

                dve.sem_inc(s["acc_done"], 1)
                shift(0, 0)
                one(0)
                with dve.Fori(1, G - 1) as g:
                    one(g)
                one(G - 1)
                residual(G - 1, GT - 1)
                group_stats()
                group_norm(G - 1)


def mixture_of_experts(nc, glob, w):
    FT = -(-F // P)
    FP = [min(P, F - P * i) for i in range(FT)]
    with ExitStack() as stack:
        c = Ctx(nc, stack)
        xs = c.sb("f_xs", [P, GT, D])
        xf = c.sb("f_xf", [P, KD, GW])
        XT = c.sb("f_XT", [P, 2, KD, T], F32R)
        gw = c.sb("f_gw", [P, KD, E])
        wgu = c.sb("f_wgu", [P, 2, 2, 2, KD, F], F32R)
        wd = c.sb("f_wd", [P, 2, 2, FT, D], F32R)
        rgu = c.sb("f_rgu", [P, 2, 2, KD, F])
        rd = c.sb("f_rd", [P, 2, FT, D])
        rank = c.sb("f_rank", [P, NT, E])
        lg = c.sb("f_lg", [P, NT, E])
        pe_ = c.sb("f_scores", [P, NT, E])
        hot1 = c.sb("f_hot1", [P, NT, E])
        hot2 = c.sb("f_hot2", [P, NT, E])
        tmp = c.sb("f_tmp", [P, NT, E])
        m0 = c.sb("f_m0", [P, NT, 1])
        m1 = c.sb("f_m1", [P, NT, 1])
        m2 = c.sb("f_m2", [P, NT, 1])
        den = c.sb("f_den", [P, NT, 1])
        lgT = c.sb("f_lgT", [P, GW])
        comb = c.sb("f_comb", [P, NE, NT])
        ce = c.sb("f_ce", [P, 2, NT])
        sg = c.sb("f_sg", [P, 2, 512])
        hid = c.sb("f_hid", [P, 2, FT, 2, 512], F32R)
        st6 = c.sb("f_st6", [P, NT, 6])
        mv = c.sb("f_mv", [P, NT, 2])
        rstd = c.sb("f_rstd", [P, NT])
        tb = c.ps("f_tb", [P, 2, 512])
        gu = c.ps("f_gu", [P, 2, 2, 512])
        acc = c.ps("f_acc", [P, 2, 512])
        sums = [acc[:, 0], acc[:, 1], tb[:, 0], tb[:, 1]]
        names = ["loaded", "xs_ready", "tb_ready", "tb_done", "l_ready", "l_done", "comb_ready", "sub_ready",
                 "exp_ready", "gu_ready", "sg_ready", "h_done", "acc_ready", "acc_done", "ce_ready", "mv_ready",
                 "rstd_ready", "raw0", "raw1", "high0", "high1", "w_ready", "rank_ready", "low_ready", "gu_done"]
        s = dict(zip(names, c.sems(*["f_" + n for n in names])))
        raw, high = [s["raw0"], s["raw1"]], [s["high0"], s["high1"]]
        X, ident = glob["X"], glob["ident"]
        HPE = G * FT

        def load(eng, gu_to, d_to, e, p, done):
            eng.dma_start(gu_to[:, p], w["w_gu"][ds(e, 1)].rearrange("a u (k p) f -> p (a u) k f", p=P))\
               .then_inc(done[p], 16)
            eng.dma_start(d_to[:, p, 0:FT - 1], w["w_dn"][ds(e, 1), 0:(FT - 1) * P]
                          .rearrange("a (k p) d -> p (a k) d", p=P)).then_inc(done[p], 16)
            eng.dma_start(d_to[0:FP[-1], p, FT - 1], w["w_dn"][ds(e, 1), (FT - 1) * P:F]
                          .rearrange("a p d -> p (a d)")).then_inc(done[p], 16)

        with nc.Block() as block:
            @block.sync
            def _(sp):
                sp.dma_start(gw[:], w["gate_wT"].rearrange("(k p) e -> p k e", p=P)).then_inc(s["loaded"], 16)
                load(sp, rgu, rd, 0, 0, raw)
                load(sp, rgu, rd, 1, 1, raw)
                with sp.Fori(1, NE // 2) as i:
                    for p in range(2):
                        sp.wait_ge(s["w_ready"], 2 * i + p - 1)
                        load(sp, rgu, rd, 2 * i + p, p, raw)

            @block.gpsimd
            def _(pool):
                for j in range(E):
                    pool.memset(rank[:, :, j:j + 1], float(E - j))
                pool.drain()
                pool.memset(comb[:, E:NE], 1.0).then_inc(s["rank_ready"], 1)

                def load_high(e, p):
                    load(pool, wgu[:, :, 0], wd[:, :, 0], e, p, high)

                def lower(p, r):
                    pool.wait_ge(raw[p], 48 * (r + 1))
                    pool.wait_ge(high[p], 48 * (r + 1))
                    pool.tensor_tensor(wgu[:, p, 1], rgu[:, p], wgu[:, p, 0].bitcast(F32), ALU.subtract)
                    pool.tensor_tensor(wd[:, p, 1, 0:FT - 1], rd[:, p, 0:FT - 1],
                                       wd[:, p, 0, 0:FT - 1].bitcast(F32), ALU.subtract)
                    pool.drain()
                    pool.tensor_tensor(wd[0:FP[-1], p, 1, FT - 1], rd[0:FP[-1], p, FT - 1],
                                       wd[0:FP[-1], p, 0, FT - 1].bitcast(F32), ALU.subtract)\
                        .then_inc(s["w_ready"], 1)

                def weigh(e, p):
                    pool.wait_ge(s["acc_done"], NT * e)
                    pool.tensor_copy(ce[:, p:p + 1], comb[:, ds(e, 1)]).then_inc(s["ce_ready"], 1)

                load_high(0, 0)
                for g in range(G):
                    stage_group(pool, s, g, xs, X)
                    if g == 1:
                        lower(0, 0)
                pool.wait_ge(s["comb_ready"], 1)
                with pool.Fori(0, NE // 2 - 1) as i:
                    weigh(2 * i, 0)
                    load_high(2 * i + 1, 1)
                    lower(1, i)
                    weigh(2 * i + 1, 1)
                    load_high(2 * i + 2, 0)
                    lower(0, i + 1)
                weigh(NE - 2, 0)
                load_high(NE - 1, 1)
                lower(1, NE // 2 - 1)
                weigh(NE - 1, 1)
                rstd_group(pool, s, 1, mv, rstd, glob, NT)

            @block.tensor
            def _(pe):
                pe.wait_ge(s["loaded"], 16)
                with pe.Fori(0, G) as g:
                    turn_group(pe, s, g, xs, tb, ident)
                    pe.wait_ge(s["tb_done"], 2 * g + 2)
                    pe.wait_ge(s["l_done"], g)
                    for k in range(KD):
                        mm = pe.matmul(acc[0:E, 0], gw[:, k], xf[:, k], start=k == 0,
                                       stop=k == KD - 1)
                    mm.then_inc(s["l_ready"], 1)
                    pe.wait_ge(s["sub_ready"], g + 1)
                    for st in range(GT):
                        t = pe.transpose(acc[:, 1, st * P:st * P + P], lgT[:, st * P:st * P + P], ident[:])
                    t.then_inc(s["l_ready"], 1)

                def add(out, a, b, k, tiles):
                    for i, (x, y) in enumerate(((0, 0), (0, 1), (1, 0))):
                        mm = pe.matmul(out, a(x), b(y), start=k == 0 and i == 0, stop=k == tiles - 1 and i == 2)
                    return mm

                pe.wait_ge(s["low_ready"], G)
                with pe.Fori(0, NE // 2) as i:
                    for p in range(2):
                        e = 2 * i + p

                        def up(g):
                            for hm in range(FT):
                                j = FT * g + hm
                                pe.wait_ge(s["gu_done"], ring(HPE, e, j, 2))
                                if j == 0:
                                    pe.wait_ge(s["w_ready"], e + 1)
                                for u in range(2):
                                    for k in range(KD):
                                        mm = add(gu[0:FP[hm], j % 2, u],
                                                 lambda part: wgu[:, p, part, u, k, hm * P:hm * P + FP[hm]],
                                                 lambda part: XT[:, part, k, g * GW:g * GW + GW], k, KD)
                                mm.then_inc(s["gu_ready"], 1)

                        def down(g):
                            pe.wait_ge(s["h_done"], HPE * e + FT * (g + 1))
                            for st in range(GT):
                                pe.wait_ge(s["acc_done"], ring(NT, e, GT * g + st, 4))
                                for hm in range(FT):
                                    n = FP[hm]
                                    mm = add(sums[st][:, 0:D],
                                             lambda part: hid[0:n, g % 2, hm, part, st * P:st * P + P],
                                             lambda part: wd[0:n, p, part, hm], hm, FT)
                                mm.then_inc(s["acc_ready"], 1)

                        up(0)
                        for g in range(1, G):
                            up(g)
                            down(g - 1)
                        down(G - 1)

            @block.scalar
            def _(act):
                with act.Fori(0, G) as g:
                    for k in range(KD):
                        if k == 0:
                            act.wait_ge(s["low_ready"], g)
                            act.wait_ge(s["l_ready"], 2 * g)
                        act.wait_ge(s["tb_ready"], KD * g + k + 1)
                        act.copy(xf[:, k], tb[:, k])
                        act.copy(XT[:, 0, k, ds(g * GW, GW)], tb[:, k]).then_inc(s["tb_done"], 1)
                act.wait_ge(s["sub_ready"], G + 1)
                act.activation(pe_[:], lg[:], ACT.Exp).then_inc(s["exp_ready"], 1)
                with act.Fori(0, NE) as e:
                    for j in range(HPE):
                        act.wait_ge(s["gu_ready"], HPE * e + j + 1)
                        act.wait_ge(s["h_done"], ring(HPE, e, j, 2))
                        n = FP[j % FT]
                        act.activation(sg[0:n, j % 2], gu[0:n, j % 2, 0], ACT.Silu).then_inc(s["sg_ready"], 1)

            @block.vector
            def _(dve):
                dve.memset(lgT[:], 0.0)
                dve.drain()
                dve.wait_ge(s["rank_ready"], 1)

                def wide(a):
                    return a[:].to_broadcast([P, NT, E])

                def first_of(hot, scores, top):
                    dve.tensor_tensor(tmp[:], scores[:], wide(top), ALU.is_equal)
                    dve.drain()
                    dve.tensor_tensor(tmp[:], tmp[:], rank[:], ALU.mult)
                    dve.drain()
                    dve.tensor_reduce(m0[:], tmp[:], AX.X, ALU.max)
                    dve.drain()
                    dve.tensor_tensor(hot[:], tmp[:], wide(m0), ALU.is_equal)
                    dve.drain()

                with dve.Fori(0, G) as g:
                    dve.drain()
                    dve.wait_ge(s["tb_done"], 2 * g + 2)
                    dve.tensor_tensor(XT[:, 1, :, ds(g * GW, GW)], xf[:], XT[:, 0, :, ds(g * GW, GW)].bitcast(F32),
                                      ALU.subtract).then_inc(s["low_ready"], 1)
                    dve.wait_ge(s["l_ready"], 2 * g + 1)
                    dve.tensor_copy(lgT[0:E], acc[0:E, 0]).then_inc(s["sub_ready"], 1)
                    dve.wait_ge(s["l_ready"], 2 * g + 2)
                    dve.tensor_copy(tmp[:, ds(g * GT, GT)], acc[:, 1].rearrange("p (s e) -> p s e", e=P)[:, :, 0:E])\
                       .then_inc(s["l_done"], 1)
                dve.drain()
                dve.tensor_reduce(m0[:], tmp[:], AX.X, ALU.max)
                dve.drain()
                dve.tensor_tensor(lg[:], tmp[:], wide(m0), ALU.subtract).then_inc(s["sub_ready"], 1)
                dve.wait_ge(s["exp_ready"], 1)
                dve.tensor_reduce(den[:], pe_[:], AX.X, ALU.add)
                dve.drain()
                dve.reciprocal(den[:], den[:])
                dve.drain()
                dve.tensor_tensor(pe_[:], pe_[:], wide(den), ALU.mult)
                dve.drain()
                dve.tensor_reduce(m1[:], pe_[:], AX.X, ALU.max)
                dve.drain()
                first_of(hot1, pe_, m1)
                dve.scalar_tensor_tensor(out=pe_[:], in0=hot1[:], scalar=-2.0, in1=pe_[:], op0=ALU.mult,
                                         op1=ALU.add)
                dve.drain()
                dve.tensor_reduce(m2[:], pe_[:], AX.X, ALU.max)
                dve.drain()
                first_of(hot2, pe_, m2)
                dve.tensor_tensor(den[:], m1[:], m2[:], ALU.add)
                dve.drain()
                dve.tensor_scalar(den[:], den[:], 1e-20, None, ALU.add)
                dve.drain()
                dve.reciprocal(den[:], den[:])
                dve.drain()
                dve.scalar_tensor_tensor(out=m1[:], in0=m1[:], scalar=2.5, in1=den[:], op0=ALU.mult,
                                         op1=ALU.mult)
                dve.scalar_tensor_tensor(out=m2[:], in0=m2[:], scalar=2.5, in1=den[:], op0=ALU.mult,
                                         op1=ALU.mult)
                dve.drain()
                dve.tensor_tensor(hot1[:], hot1[:], wide(m1), ALU.mult)
                dve.tensor_tensor(hot2[:], hot2[:], wide(m2), ALU.mult)
                dve.drain()
                dve.tensor_tensor(comb[:, 0:E].rearrange("p e s -> p s e"), hot1[:], hot2[:],
                                  ALU.add).then_inc(s["comb_ready"], 1)

                with dve.Fori(0, NE // 2) as i:
                    for p in range(2):
                        e = 2 * i + p

                        def hidden(g):
                            for hm in range(FT):
                                j = FT * g + hm
                                n = FP[hm]
                                dve.wait_ge(s["sg_ready"], HPE * e + j + 1)
                                full = sg[0:n, j % 2]
                                dve.tensor_tensor(full, full, gu[0:n, j % 2, 1], ALU.mult).then_inc(s["gu_done"], 1)
                                dve.drain()
                                dve.tensor_copy(hid[0:n, g % 2, hm, 0], full)
                                dve.drain()
                                dve.tensor_tensor(hid[0:n, g % 2, hm, 1], full, hid[0:n, g % 2, hm, 0].bitcast(F32),
                                                  ALU.subtract).then_inc(s["h_done"], 1)

                        def add_up(g):
                            if g == 0:
                                dve.wait_ge(s["ce_ready"], e + 1)
                            for st in range(GT):
                                t = g * GT + st
                                dve.wait_ge(s["acc_ready"], NT * e + t + 1)
                                dve.scalar_tensor_tensor(out=X[:, t], in0=sums[st][:, 0:D],
                                                         scalar=ce[:, p, t:t + 1], in1=X[:, t], op0=ALU.mult,
                                                         op1=ALU.add).then_inc(s["acc_done"], 1)

                        hidden(0)
                        for g in range(1, G):
                            hidden(g)
                            add_up(g - 1)
                        add_up(G - 1)

                stats(dve, s, lambda i: X[:, i], st6, mv, NT)
                dve.wait_ge(s["rstd_ready"], 1)
                for i in range(NT):
                    dve.tensor_scalar(X[:, i], X[:, i], mv[:, i, 0:1], rstd[:, i:i + 1], ALU.subtract, ALU.mult)


def delta_rule(nc, glob, w):
    NP = NT // 2
    KW = HID // NH
    CH = 7
    with ExitStack() as stack:
        c = Ctx(nc, stack)
        ws = c.sb("g_ws", [P, KD, 3 * HID + NH])
        wo = c.sb("g_wo", [P, KH, D])
        lnw = c.sb("g_lnw", [P, D])
        lnb = c.sb("g_lnb", [P, D])
        hs = c.sb("g_hs", [P, 2, D])
        hT = c.sb("g_hT", [P, 2, KD, P])
        st6 = c.sb("g_st6", [P, 2, 6])
        mv = c.sb("g_mv", [P, 2, 2])
        rstd = c.sb("g_rstd", [P, 2])
        mv_r = c.sb("g_mv_r", [P, 2, 2])
        rstd_r = c.sb("g_rstd_r", [P, 2])
        ut = c.sb("g_ut", [P, 2, 512])
        qk = c.sb("g_qk", [P, 2, 2, 2, HID])
        vb = c.sb("g_vb", [P, 2, 2, HID])
        bt = c.sb("g_bt", [P, 2, 2, NH])
        prod = c.sb("g_prod", [P, 4, HID])
        sums = c.sb("g_sums", [P, 4, NH])
        dots = c.sb("g_dots", [P, 4, NH])
        fac = c.sb("g_fac", [P, 4, NH])
        co = c.sb("g_co", [P, 3, NH])
        out = c.sb("g_out", [P, 2, HID])
        oT = c.sb("g_oT", [P, 2, KH, P])
        r = c.sb("g_r", [P, 2, D])
        hb = c.ps("g_hb", [P, 512])
        ch = c.ps("g_ch", [P, 3, 512])
        tb = c.ps("g_tb", [P, 2, 512])
        acc = c.ps("g_acc", [P, 2, 512])
        names = ["loaded", "mv_ready", "rstd_ready", "hs_ready", "hb_ready", "hT_ready", "ch_ready", "act_done",
                 "t_ready", "stt_done", "qk_ready", "prod_ready", "co_ready", "part_ready", "o_ready", "tb_ready",
                 "tb_done", "acc_ready", "acc_done", "mv_r_ready", "rstd_r_ready"]
        s = dict(zip(names, c.sems(*["g_" + n for n in names])))
        s_r = {"mv_ready": s["mv_r_ready"], "rstd_ready": s["rstd_r_ready"]}
        X, ident = glob["X"], glob["ident"]

        def heads(a):
            return a.rearrange("p (h d) -> p h d", h=NH)

        def rounds(eng, one):
            one(0, 0)
            one(1, 1)
            with eng.Fori(1, NP // 2 - 1) as h:
                one(2 * h, 0)
                one(2 * h + 1, 1)
            for i in range(NP - 2, NP + 2):
                one(i, i % 2)

        def there(i, back):
            return not isinstance(i, int) or 0 <= i - back < NP

        with nc.Block() as block:
            @block.sync
            def _(sp):
                for k in range(KD):
                    sp.dma_start(ws[:, k], w["w_slow"][k * P:(k + 1) * P]).then_inc(s["loaded"], 16)
                sp.dma_start(wo[:], w["w_out"].rearrange("(k p) n -> p k n", p=P)).then_inc(s["loaded"], 16)
                sp.dma_start(lnw[:], w["ln_w"].to_broadcast([P, D])).then_inc(s["loaded"], 16)
                sp.dma_start(lnb[:], w["ln_b"].to_broadcast([P, D])).then_inc(s["loaded"], 16)

            @block.gpsimd
            def _(pool):
                def dot_products(p, par):
                    if not isinstance(p, int) or p:
                        pool.wait_ge(s["o_ready"], p)
                    pool.wait_ge(s["qk_ready"], p + 1)
                    q0, k0, q1, k1 = (qk[:, par, j // 2, j % 2] for j in range(4))
                    for i, (a, b) in enumerate(((k0, q0), (k0, k1), (k0, q1), (k1, q1))):
                        pool.tensor_tensor(prod[:, i], a, b, ALU.mult).then_inc(s["prod_ready"], 1)

                def outputs(p, par):
                    pool.wait_ge(s["co_ready"], p + 1)
                    pool.wait_ge(s["act_done"], 2 * CH * p + 2 * CH)
                    if not isinstance(p, int) or p:
                        pool.wait_ge(s["tb_ready"], 4 * p)
                    pool.tensor_tensor(heads(out[:, 0]), heads(vb[:, par, 0]), co[:, 0].rearrange(
                        "p (h a) -> p h a", a=1).to_broadcast([P, NH, KW]), ALU.mult).then_inc(s["part_ready"], 1)
                    pool.tensor_tensor(heads(prod[:, 0]), heads(vb[:, par, 1]), co[:, 2].rearrange(
                        "p (h a) -> p h a", a=1).to_broadcast([P, NH, KW]), ALU.mult).then_inc(s["part_ready"], 1)

                def one(i, par):
                    if there(i, 1):
                        dot_products(i - 1, 1 - par)
                        outputs(i - 1, 1 - par)
                    if there(i, 2):
                        rstd_group(pool, s_r, i - 1, mv_r, rstd_r, glob, 2)
                    if there(i, -1):
                        rstd_group(pool, s, i + 2, mv, rstd, glob, 2)

                rstd_group(pool, s, 1, mv, rstd, glob, 2)
                rounds(pool, one)

            @block.tensor
            def _(pe):
                def project(p):
                    pe.wait_ge(s["hs_ready"], p + 1)
                    if not isinstance(p, int) or p:
                        pe.wait_ge(s["hT_ready"], p)
                    for tm in range(2):
                        for k in range(KD):
                            a = (tm * KD + k) * P
                            t = pe.transpose(hb[:, a:a + P], hs[:, tm, k * P:k * P + P], ident[:])
                    t.then_inc(s["hb_ready"], 1)
                    pe.wait_ge(s["hT_ready"], p + 1)
                    for j in range(2 * CH):
                        tm, q = j // CH, j % CH
                        width = 512 if q < 6 else NH
                        if j < 3:
                            if not isinstance(p, int) or p:
                                pe.wait_ge(s["act_done"], 2 * CH * p)
                                pe.wait_ge(s["stt_done"], 8 * p)
                        elif (j - 3) % CH < 4:
                            pe.wait_ge(s["stt_done"], 8 * p + 4 * ((j - 3) // CH) + (j - 3) % CH + 1)
                        else:
                            pe.wait_ge(s["act_done"], 2 * CH * p + j - 3 + 1)
                        for k in range(KD):
                            mm = pe.matmul(ch[:, j % 3, 0:width], hT[:, tm, k], ws[:, k, q * 512:q * 512 + width],
                                           start=k == 0, stop=k == KD - 1)
                        mm.then_inc(s["ch_ready"], 1)

                def project_out(p):
                    pe.wait_ge(s["o_ready"], p + 1)

                    def turn(q):
                        if not (isinstance(p, int) and p == 0 and q < 2):
                            pe.wait_ge(s["tb_done"], ring(4, p, q, 2))
                        for blk in range(4):
                            b8 = (q % 2) * 4 + blk
                            t = pe.transpose(tb[:, q % 2, blk * P:blk * P + P],
                                             out[:, q // 2, b8 * P:b8 * P + P], ident[:])
                        t.then_inc(s["tb_ready"], 1)

                    turn(0)
                    turn(1)
                    if not isinstance(p, int) or p:
                        pe.wait_ge(s["acc_done"], 2 * p)
                    for q in range(4):
                        pe.wait_ge(s["tb_done"], 4 * p + q + 1)
                        tm = q // 2
                        for k in range(4 * (q % 2), 4 * (q % 2) + 4):
                            mm = pe.matmul(acc[:, tm, 0:D], oT[:, tm, k], wo[:, k], start=k == 0, stop=k == KH - 1)
                        if q % 2:
                            mm.then_inc(s["acc_ready"], 1)
                        if q < 2:
                            turn(q + 2)

                pe.wait_ge(s["loaded"], 16 * (KD + 3))
                def one(i, par):
                    if there(i, 0):
                        project(i)
                    if there(i, 1):
                        project_out(i - 1)

                rounds(pe, one)

            @block.scalar
            def _(act):
                def chunks(p, par):
                    act.wait_ge(s["hb_ready"], p + 1)
                    act.copy(hT[:], hb[:].rearrange("p (t k n) -> p t k n", t=2, k=KD)).then_inc(s["hT_ready"], 1)
                    used = not isinstance(p, int) or p >= 2
                    n = 0
                    for j in range(2 * CH):
                        tm, q = j // CH, j % CH
                        act.wait_ge(s["ch_ready"], 2 * CH * p + j + 1)
                        if q < 4:
                            if not (isinstance(p, int) and p == 0 and n < 2):
                                act.wait_ge(s["stt_done"], ring(8, p, n, 2))
                            act.activation(ut[:, n % 2], ch[:, j % 3], ACT.Relu, scale=-1.0)\
                               .then_inc(s["act_done"], 1)
                            act.drain()
                            act.activation(ut[:, n % 2], ut[:, n % 2], ACT.Exp, scale=-1.0)\
                               .then_inc(s["t_ready"], 1)
                            n += 1
                        elif q < 6:
                            if j == 4 and used:
                                act.wait_ge(s["o_ready"], p - 1)
                            act.copy(vb[:, par, tm, (q - 4) * 512:(q - 3) * 512], ch[:, j % 3])\
                               .then_inc(s["act_done"], 1)
                        else:
                            if tm == 0 and used:
                                act.wait_ge(s["co_ready"], p - 1)
                            act.activation(bt[:, par, tm], ch[:, j % 3, 0:NH], ACT.Tanh, scale=0.5)\
                               .then_inc(s["act_done"], 1)

                def one(i, par):
                    if there(i, 0):
                        chunks(i, par)
                    if there(i, 1):
                        for q in range(4):
                            act.wait_ge(s["tb_ready"], 4 * (i - 1) + q + 1)
                            act.copy(oT[:, q // 2, (q % 2) * 4:(q % 2) * 4 + 4],
                                     tb[:, q % 2].rearrange("p (b n) -> p b n", n=P)).then_inc(s["tb_done"], 1)

                rounds(act, one)

            @block.vector
            def _(dve):
                dve.wait_ge(s["loaded"], 16 * (KD + 3))

                def tile(p, tm):
                    return X[:, ds(p + NP * tm, 1), :].rearrange("p a d -> p (a d)")

                def normed_stats(p):
                    stats(dve, s, lambda i: tile(p, i), st6, mv, 2)

                def normed(p):
                    dve.wait_ge(s["rstd_ready"], p + 1)
                    if not isinstance(p, int) or p:
                        dve.wait_ge(s["hb_ready"], p)
                    for tm in range(2):
                        dve.tensor_scalar(hs[:, tm], tile(p, tm), mv[:, tm, 0:1], rstd[:, tm:tm + 1],
                                          ALU.subtract, ALU.mult)
                    dve.drain()
                    for tm in range(2):
                        dve.tensor_tensor(hs[:, tm], hs[:, tm], lnw[:], ALU.mult)
                    dve.drain()
                    for tm in range(2):
                        a = dve.tensor_tensor(hs[:, tm], hs[:, tm], lnb[:], ALU.add)
                    a.then_inc(s["hs_ready"], 1)

                def positive(p, par, n):
                    tm, q = n // 4, n % 4
                    dve.wait_ge(s["t_ready"], 8 * p + n + 1)
                    dve.scalar_tensor_tensor(out=qk[:, par, tm, q // 2, (q % 2) * 512:(q % 2) * 512 + 512],
                                             in0=ch[:, (CH * tm + q) % 3], scalar=0.0, in1=ut[:, n % 2],
                                             op0=ALU.max, op1=ALU.add).then_inc(s["stt_done"], 1)

                def sum_up(p, par):
                    dve.drain()
                    dve.tensor_reduce(sums[:].rearrange("p a h -> p (a h)"),
                                      qk[:, par].rearrange("p t a (h d) -> p (t a h) d", h=NH), AX.X, ALU.add)\
                       .then_inc(s["qk_ready"], 1)

                def dot(p, i):
                    dve.wait_ge(s["prod_ready"], 4 * p + i + 1)
                    dve.tensor_reduce(dots[:, i], heads(prod[:, i]), AX.X, ALU.add)

                def coefficients(p, par):
                    dve.drain()
                    dve.reciprocal(sums[:], sums[:])
                    dve.drain()
                    q0, k0, q1, k1 = (sums[:, i] for i in range(4))
                    for i, (a, b) in enumerate(((k0, q0), (k0, k1), (k0, q1), (k1, q1))):
                        dve.tensor_tensor(fac[:, i], a, b, ALU.mult)
                    dve.drain()
                    dve.wait_ge(s["act_done"], 2 * CH * p + 2 * CH)
                    dve.tensor_tensor(dots[:], dots[:], fac[:], ALU.mult)
                    dve.tensor_scalar(bt[:, par], bt[:, par], 0.5, 0.5, ALU.mult, ALU.add)
                    dve.drain()
                    b0, b1 = bt[:, par, 0], bt[:, par, 1]
                    dve.tensor_tensor(co[:, 0], b0, dots[:, 0], ALU.mult)
                    dve.tensor_tensor(fac[:, 0], b0, dots[:, 1], ALU.mult)
                    dve.tensor_tensor(fac[:, 1], b0, dots[:, 2], ALU.mult)
                    dve.tensor_tensor(co[:, 2], b1, dots[:, 3], ALU.mult)
                    dve.drain()
                    dve.tensor_tensor(fac[:, 0], fac[:, 0], co[:, 2], ALU.mult)
                    dve.drain()
                    dve.tensor_tensor(co[:, 1], fac[:, 1], fac[:, 0], ALU.subtract).then_inc(s["co_ready"], 1)

                def second_output(p, par):
                    dve.drain()
                    if not isinstance(p, int) or p:
                        dve.wait_ge(s["tb_ready"], 4 * p)
                    dve.tensor_tensor(heads(out[:, 1]), heads(vb[:, par, 0]), co[:, 1].rearrange(
                        "p (h a) -> p h a", a=1).to_broadcast([P, NH, KW]), ALU.mult)

                def second_output_sum(p):
                    dve.drain()
                    dve.wait_ge(s["part_ready"], 2 * p + 2)
                    dve.tensor_tensor(out[:, 1], out[:, 1], prod[:, 0], ALU.add).then_inc(s["o_ready"], 1)

                def residual(p):
                    dve.drain()
                    for tm in range(2):
                        dve.wait_ge(s["acc_ready"], 2 * p + tm + 1)
                        dve.scalar_tensor_tensor(out=r[:, tm], in0=tile(p, tm), scalar=2.0, in1=acc[:, tm, 0:D],
                                                 op0=ALU.mult, op1=ALU.add).then_inc(s["acc_done"], 1)
                    stats(dve, s_r, lambda i: r[:, i], st6, mv_r, 2)

                def residual_norm(p):
                    dve.wait_ge(s["rstd_r_ready"], p + 1)
                    for tm in range(2):
                        dve.tensor_scalar(tile(p, tm), r[:, tm], mv_r[:, tm, 0:1], rstd_r[:, tm:tm + 1],
                                          ALU.subtract, ALU.mult)

                def one(i, par):
                    for n in range(8):
                        if there(i, 0):
                            positive(i, par, n)
                        if there(i, 1):
                            if n < 4:
                                dot(i - 1, n)
                            if n == 3:
                                coefficients(i - 1, 1 - par)
                            if n == 4:
                                second_output(i - 1, 1 - par)
                            if n == 5:
                                second_output_sum(i - 1)
                        if there(i, 2):
                            if n == 3:
                                residual(i - 2)
                            if n == 6:
                                residual_norm(i - 2)
                    if there(i, -1):
                        normed_stats(i + 1)
                    if there(i, 0):
                        sum_up(i, par)
                    if there(i, -1):
                        normed(i + 1)

                normed_stats(0)
                normed(0)
                rounds(dve, one)


def gated_mlp(nc, glob, w, y):
    with ExitStack() as stack:
        c = Ctx(nc, stack)
        wab, wh, w3 = mlp_weights(glob["mlp_w"])
        raw = glob["mlp_raw"][:].rearrange("p (q n) -> p q n", q=2)
        bits = glob["mlp_raw"][:, 0:WCH].bitcast(U32)
        xs = c.sb("i_xs", [P, GT, D])
        sc = c.sb("i_sc", [P, 4, KH])
        s3 = c.sb("i_s3", [P, D])
        full = c.sb("i_full", [P, 2, 512])
        h = c.sb("i_h", [P, 2, KH, 2, GW], F32R)
        r = c.sb("i_r", [P, GT, D])
        st6 = c.sb("i_st6", [P, GT, 6])
        mv = c.sb("i_mv", [P, GT, 2])
        rstd = c.sb("i_rstd", [P, GT])
        low = c.sb("i_low", [P, 1], U32)
        lowf = c.sb("i_lowf", [P, 1])
        flagf = c.sb("i_flagf", [1, 1])
        flag = c.sb("i_flag", [1, 1], mybir.dt.int32)
        tb = c.ps("i_tb", [P, 2, 512])
        hb = c.ps("i_hb", [P, 4, 512])
        acc = c.ps("i_acc", [P, 2, 512])
        names = ["loaded", "xs_ready", "tb_ready", "tb_done", "ab_ready", "sg_ready", "ab_done", "ab_split",
                 "h_ready", "full_ready", "h_split", "acc_ready", "acc_done", "mv_ready", "rstd_ready",
                 "y_ready", "stored", "low_ready", "low_turned", "flag_ready"]
        s = dict(zip(names, c.sems(*["i_" + n for n in names])))
        X, ident = glob["X"], glob["ident"]
        raw_ready = c.sems("i_raw_ready0", "i_raw_ready1")
        UNITS = 3 * KH + 2
        xT = h[:, 1, 0:KD]
        with nc.Block() as block:
            @block.sync
            def _(sp):
                sp.dma_start(sc[:], w["scales"]).then_inc(s["loaded"], 16)
                sp.dma_start(s3[:], w["w3_s"].to_broadcast([P, D])).then_inc(s["loaded"], 16)

                def unit(g, u):
                    if u < 2:
                        sp.wait_ge(s["acc_ready"], GT * g)
                    elif u < KH + 2:
                        sp.wait_ge(s["ab_ready"], KH * g + u - 1)
                    else:
                        sp.wait_ge(s["h_ready"], 2 * KH * g + u - KH - 1)
                    if u < KH:
                        for i, name in enumerate(("w1T", "w2T")):
                            sp.dma_start(raw[:, u % 2, i * KD * P:(i + 1) * KD * P].rearrange("p (k n) -> p k n", k=KD),
                                         w[name].rearrange("(k p) n -> p k n", p=P)[:, :, u * P:u * P + P])\
                              .then_inc(raw_ready[u % 2], 16)
                    elif u < 3 * KH:
                        m = u % KH
                        sp.dma_start(raw[:, u % 2].rearrange("p (k n) -> p k n", k=KH),
                                     w["h1T" if u < 2 * KH else "h2T"].rearrange("(k p) n -> p k n", p=P)
                                     [:, :, m * P:m * P + P]).then_inc(raw_ready[u % 2], 16)
                    else:
                        k = (u - 3 * KH) * KH // 2
                        sp.dma_start(raw[:, u % 2].rearrange("p (k n) -> p k n", k=KH // 2),
                                     w["w3T"].rearrange("(k p) n -> p k n", p=P)[:, k:k + KH // 2])\
                          .then_inc(raw_ready[u % 2], 16)

                sp.wait_ge(s["flag_ready"], 1)
                extra = sp.value_load(flag[0:1, 0:1], min_val=0, max_val=FULL_BITS)
                with sp.If(extra > 0):
                    with sp.Fori(0, G) as g:
                        for u in range(UNITS):
                            unit(g, u)

            @block.gpsimd
            def _(pool):
                def finish(g):
                    rstd_group(pool, s, g + 1, mv, rstd, glob, GT)
                    pool.wait_ge(s["y_ready"], g + 1)
                    pool.dma_start(y.rearrange("(t p) d -> p t d", p=P)[:, ds(g * GT, GT), :],
                                   X[:, ds(g * GT, GT), :]).then_inc(s["stored"], 16)

                stage_group(pool, s, 0, xs, X)
                stage_group(pool, s, 1, xs, X)
                with pool.Fori(0, G - 2) as g:
                    finish(g)
                    stage_group(pool, s, g + 2, xs, X)
                finish(G - 2)
                finish(G - 1)
                pool.wait_ge(s["stored"], 16 * G)

            @block.tensor
            def _(pe):
                pe.wait_ge(glob["mlp_loaded"], 16 * 5)
                pe.wait_ge(s["low_ready"], 1)
                pe.transpose(tb[0:1, 0, 0:P], lowf[:], ident[:]).then_inc(s["low_turned"], 1)

                def groups(exact):
                    def read(ap):
                        return ap if exact or ap.dtype == F32 else ap.bitcast(F32)

                    def need(g, u):
                        if not exact:
                            loads = 3 * KH // 2 + KH // 2 + 1
                            before = u // 2 + min(u // 2, KH // 2)
                            pe.wait_ge(raw_ready[u % 2], 16 * (loads * g + before + (2 if u < KH else 1)))

                    def gate_weights(i, k, m):
                        if exact:
                            return wab[:, i, k, m * P:m * P + P]
                        return raw[:, m % 2, (i * KD + k) * P:(i * KD + k + 1) * P]

                    def hidden_weights(layer, k, m):
                        return wh[:, layer, k, m * P:m * P + P] if exact else raw[:, m % 2, k * P:k * P + P]

                    def down_weights(k):
                        half = KH // 2
                        return w3[:, k] if exact else raw[:, k // half, k % half * D:(k % half + 1) * D]

                    def add(out, lhsT, rhs, k, last):
                        for part in range(2):
                            mm = pe.matmul(out, read(lhsT(part)), read(rhs(part)), start=k == 0 and part == 0,
                                           stop=k == last and part == 1)
                        return mm

                    def gated(g):
                        for m in range(KH):
                            if m == 0:
                                pe.wait_ge(s["full_ready"], 2 * KH * g)
                                pe.wait_ge(s["tb_done"], KD * (g + 1))
                            pe.wait_ge(s["ab_done"], ring(KH, g, m, 2))
                            need(g, m)
                            for i in range(2):
                                for k in range(KD):
                                    mm = add(hb[:, 2 * (m % 2) + i], lambda part: gate_weights(i, k, m),
                                             lambda part: xT[:, k, part], k, KD - 1)
                            mm.then_inc(s["ab_ready"], 1)

                    def hidden(g, layer):
                        for m in range(KH):
                            if layer or m >= 4:
                                pe.wait_ge(s["full_ready"], 2 * KH * g + KH * layer + m - 3)
                            elif m == 0:
                                pe.wait_ge(s["ab_done"], KH * (g + 1) - 1)
                            need(g, KH * (layer + 1) + m)
                            for k in range(KH):
                                if m == 0 and layer == 0:
                                    pe.wait_ge(s["ab_split"], KH * g + k + 1)
                                elif m == 0:
                                    pe.wait_ge(s["h_split"], 2 * KH * g + k + 1)
                                mm = add(hb[:, m % 4], lambda part: hidden_weights(layer, k, m),
                                         lambda part: h[:, layer, k, part], k, KH - 1)
                            mm.then_inc(s["h_ready"], 1)

                    def down(g):
                        need(g, 3 * KH)
                        need(g, 3 * KH + 1)
                        for st in range(GT):
                            pe.wait_ge(s["acc_done"], ring(GT, g, st, 2))
                            for k in range(KH):
                                if st == 0:
                                    pe.wait_ge(s["h_split"], 2 * KH * g + KH + k + 1)
                                mm = add(acc[:, st % 2, 0:D], lambda part: h[:, 0, k, part, st * P:st * P + P],
                                         lambda part: down_weights(k), k, KH - 1)
                            mm.then_inc(s["acc_ready"], 1)

                    turn_group(pe, s, 0, xs, tb, ident)
                    with pe.Fori(0, G - 1) as g:
                        gated(g)
                        hidden(g, 0)
                        hidden(g, 1)
                        turn_group(pe, s, g + 1, xs, tb, ident)
                        down(g)
                    gated(G - 1)
                    hidden(G - 1, 0)
                    hidden(G - 1, 1)
                    down(G - 1)

                pe.wait_ge(s["flag_ready"], 1)
                extra = pe.value_load(flag[0:1, 0:1], min_val=0, max_val=FULL_BITS)
                with pe.If(extra == 0):
                    groups(True)
                with pe.If(extra > 0):
                    groups(False)

            @block.scalar
            def _(act):
                act.wait_ge(s["loaded"], 32)
                with act.Fori(0, G) as g:
                    for m in range(KH):
                        act.wait_ge(s["h_split"], 2 * KH * g)
                        act.wait_ge(s["ab_split"], ring(KH, g, m, 2))
                        act.wait_ge(s["ab_ready"], KH * g + m + 1)
                        act.activation(full[:, m % 2], hb[:, 2 * (m % 2)], ACT.Silu, scale=sc[:, 0, m:m + 1])\
                           .then_inc(s["sg_ready"], 1)
                    for layer in range(2):
                        for m in range(KH):
                            j = KH * layer + m
                            if j < 2:
                                act.wait_ge(s["ab_split"], KH * (g + 1) - 1 + j)
                            else:
                                act.wait_ge(s["h_split"], 2 * KH * g + j - 1)
                            act.wait_ge(s["h_ready"], 2 * KH * g + j + 1)
                            act.activation(full[:, m % 2], hb[:, m % 4], ACT.Gelu,
                                           scale=sc[:, 2 + layer, m:m + 1]).then_inc(s["full_ready"], 1)

            @block.vector
            def _(dve):
                dve.wait_ge(s["loaded"], 32)
                n = WCH
                while n % 2 == 0:
                    n //= 2
                    dve.tensor_tensor(bits[:, 0:n], bits[:, 0:n], bits[:, n:2 * n], ALU.bitwise_or)
                    dve.drain()
                dve.tensor_scalar(bits[:, 0:n], bits[:, 0:n], FULL_BITS, None, ALU.bitwise_and)
                dve.drain()
                dve.tensor_reduce(low[:], bits[:, 0:n], AX.X, ALU.max)
                dve.drain()
                dve.tensor_copy(lowf[:], low[:]).then_inc(s["low_ready"], 1)
                dve.wait_ge(s["low_turned"], 1)
                dve.reduce_max(flagf[:], tb[0:1, 0, 0:P], AX.X)
                dve.drain()
                dve.tensor_copy(flag[:], flagf[:]).then_inc(s["flag_ready"], 1)

                def split(to, of):
                    dve.tensor_copy(to[:, 0], of)
                    dve.drain()
                    return dve.tensor_tensor(to[:, 1], of, to[:, 0].bitcast(F32), ALU.subtract)

                def split_x(g):
                    for k in range(KD):
                        dve.drain()
                        dve.wait_ge(s["tb_ready"], KD * g + k + 1)
                        split(xT[:, k], tb[:, k]).then_inc(s["tb_done"], 1)

                def norm_stats():
                    dve.drain()
                    stats(dve, s, lambda i: r[:, i], st6, mv, GT)

                def norm(g):
                    dve.wait_ge(s["rstd_ready"], g + 1)
                    for st in range(GT):
                        a = dve.tensor_scalar(X[:, ds(g * GT + st, 1), :].rearrange("p a d -> p (a d)"), r[:, st],
                                              mv[:, st, 0:1], rstd[:, st:st + 1], ALU.subtract, ALU.mult)
                    a.then_inc(s["y_ready"], 1)

                def one(g):
                    for m in range(KH):
                        dve.wait_ge(s["sg_ready"], KH * g + m + 1)
                        dve.scalar_tensor_tensor(out=full[:, m % 2], in0=hb[:, 2 * (m % 2) + 1],
                                                 scalar=sc[:, 1, m:m + 1], in1=full[:, m % 2], op0=ALU.mult,
                                                 op1=ALU.mult).then_inc(s["ab_done"], 1)
                        dve.drain()
                        split(h[:, 0, m], full[:, m % 2]).then_inc(s["ab_split"], 1)
                    for layer in range(2):
                        for m in range(KH):
                            dve.drain()
                            dve.wait_ge(s["full_ready"], 2 * KH * g + KH * layer + m + 1)
                            split(h[:, 1 - layer, m], full[:, m % 2]).then_inc(s["h_split"], 1)
                            if not (isinstance(g, int) and g == 0) and layer == 0:
                                if m == 1:
                                    norm_stats()
                                if m == 3:
                                    norm(g - 1)
                    if not (isinstance(g, int) and g == G - 1):
                        split_x(g + 1)
                    for st in range(GT):
                        dve.wait_ge(s["acc_ready"], GT * g + st + 1)
                        dve.tensor_tensor(r[:, st], acc[:, st % 2, 0:D], s3[:], ALU.mult)\
                           .then_inc(s["acc_done"], 1)
                    dve.drain()
                    dve.tensor_tensor(r[:], r[:], X[:, ds(g * GT, GT), :], ALU.add)

                split_x(0)
                one(0)
                with dve.Fori(1, G - 1) as g:
                    one(g)
                one(G - 1)
                norm_stats()
                norm(G - 1)


def decoder(nc, a, y, scr):
    with ExitStack() as stack:
        c = Ctx(nc, stack)
        glob = {"X": c.sb("X", [P, NT, D]), "ident": c.sb("ident", [P, P]), "mhalf": c.sb("mhalf", [P, 1]),
                "eps": c.sb("eps", [P, 1])}
        glob["x_loaded"], = c.sems("x_loaded")
        with ExitStack() as att:
            ca = Ctx(nc, att)
            glob["ATT"] = ca.sb("ATT", [P, B * NH, N // P, HD])
            glob["V"] = ca.sb("V", [P, B * NH, N // P, HD + 1])
            self_attention_qkv(nc, glob, a, scr)
            self_attention_heads(nc, glob, scr)
            attention_out(nc, glob, a)
        cross_attention(nc, glob, a, scr, True)
        mixture_of_experts(nc, glob, a)
        delta_rule(nc, glob, a)
        glob["mlp_w"] = c.sb("mlp_w", [P, NW], F32R)
        glob["mlp_raw"] = c.sb("mlp_raw", [P, 2 * KH * P])
        glob["mlp_loaded"], = c.sems("mlp_loaded")
        cross_attention(nc, glob, a, scr, False)
        gated_mlp(nc, glob, a, y)


def layouts(i, np):
    def t(a):
        return np.ascontiguousarray(a.T)

    def cols(v, k):
        return np.ascontiguousarray(v.reshape(k, P).T)

    o = {}
    x = i["x"].reshape(T, D)
    o["x"] = x
    o["xT"] = t(x)
    o["ctxT"] = np.ascontiguousarray(i["ctx_1024"].reshape(B * S, D).T)
    o["w1"] = np.stack([i[f"L0_attn_{q}_w1"] for q in "qkv"])
    o["w2"] = np.stack([i[f"L0_attn_{q}_w2"] for q in "qkv"])
    o["b1"] = np.stack([cols(i[f"L0_attn_{q}_b1"], KH) for q in "qkv"])
    o["b2qk"] = np.stack([cols(i[f"L0_attn_{q}_b2"], KD) for q in "qk"], axis=1)
    o["b2v"] = i["L0_attn_v_b2"].reshape(1, D)
    o["proj_w"] = i["L0_attn_proj_w"]
    o["proj_b"] = i["L0_attn_proj_b"].reshape(1, D)
    o["WkT"], o["WvT"] = t(i["L0_xattn_Wk"]), t(i["L0_xattn_Wv"])
    order = [8 * (rt // 4) + rt % 4 + 4 * half for rt in range(KH) for half in range(2)]
    o["WqR"] = np.ascontiguousarray(i["L0_xattn_Wq"].reshape(NH, 64, D)[order].reshape(HID, D))
    o["WoR"] = np.ascontiguousarray(i["L0_xattn_Wo"].T.reshape(NH, 64, D)[order].reshape(HID, D))
    o["gate_wT"] = t(i["L0_ffn_gate_w"])
    shared = [np.ascontiguousarray(i[f"L0_ffn_sw_{n}"].reshape(D, 2, F).transpose(1, 0, 2)) for n in ("gate", "up")]
    o["w_gu"] = np.ascontiguousarray(np.stack([np.concatenate([i["L0_ffn_w_gate"], shared[0]]),
                                               np.concatenate([i["L0_ffn_w_up"], shared[1]])], axis=1))
    o["w_dn"] = np.concatenate([i["L0_ffn_w_down"], i["L0_ffn_sw_down"].reshape(2, F, D)])
    o["ln_w"], o["ln_b"] = i["L1_attn_ln_w"].reshape(1, D), i["L1_attn_ln_b"].reshape(1, D)
    ws = i["L1_attn_w_slow"].reshape(D, NH, 3 * 64 + 1)
    o["w_slow"] = np.concatenate([np.ascontiguousarray(ws[:, :, 64 * j:64 * j + 64]).reshape(D, HID)
                                  for j in range(3)] + [np.ascontiguousarray(ws[:, :, 192])], axis=1)
    o["w_out"] = i["L1_attn_w_out"]
    o["WcT"] = t(i["L1_xattn_w_concat"])
    for n in ("w1", "w2", "h1", "h2", "w3"):
        o[n + "T"] = t(i[f"L1_ffn_{n}_w"])
    o["mlp_shares"] = np.concatenate([i[f"L1_ffn_{n}_w"].reshape(-1) for n in ("w1", "w2", "h1", "h2", "w3")]
                                     ).reshape(NT, P, WCH)
    o["scales"] = np.stack([cols(i[f"L1_ffn_{n}_s"], KH) for n in ("w1", "w2", "h1", "h2")], axis=1)
    o["w3_s"] = i["L1_ffn_w3_s"].reshape(1, D)
    return o


def kernel(**inputs):
    import numpy as _np
    import concourse.bacc as _bacc
    from concourse import mybir as _mybir
    from concourse.bass_utils import run_bass_kernel_spmd as _run

    nc = _bacc.Bacc("TRN2", target_bir_lowering=False, num_devices=1)
    laid = layouts({k: _np.asarray(v) for k, v in inputs.items()}, _np)
    arrays, args = {}, {}
    for name, a in laid.items():
        a = _np.ascontiguousarray(a)
        arrays[f"in_{name}_dram"] = a
        args[name] = nc.dram_tensor(f"in_{name}_dram", a.shape, _mybir.dt.from_np(a.dtype),
                                    kind="ExternalInput").ap()
    y = nc.dram_tensor("out_0_dram", (T, D), _mybir.dt.float32, kind="ExternalOutput").ap()
    scr = {"qk": nc.dram_tensor("scr_qk", (2, 2, B * D, N), _mybir.dt.float32, kind="Internal").ap(),
           "vals": nc.dram_tensor("scr_vals", (B, FL, D), _mybir.dt.float32, kind="Internal").ap()}
    decoder(nc, args, y, scr)
    r = _run(nc, [arrays], core_ids=[0])
    return r.results[0]["out_0_dram"].reshape(B, N, D)
```
